# Optimizing a Trainium2 kernel written in Bass

```python
import numpy as np
import jax
import jax.numpy as jnp

def _softmax(x, axis=-1):
    return jax.nn.softmax(x, axis=axis)

def _gelu(x):
    return jax.nn.gelu(x, approximate=True)

def _silu(x):
    return jax.nn.silu(x)

def _sigmoid(x):
    return jax.nn.sigmoid(x)

def _layernorm(x, axis=-1, eps=1e-05):
    m = jnp.mean(x, axis=axis, keepdims=True)
    v = jnp.var(x, axis=axis, keepdims=True)
    return (x - m) / jnp.sqrt(v + eps)

def _scatter_add(tgt, idx, src, axis=0):
    return tgt.at[idx].add(src)

def _segment_sum(src, seg, n):
    return jax.ops.segment_sum(src, seg, n)
kernel_name = 'mk_cond_resid_d2_seqx_r8_6ad12a'

def setup_inputs(seed: int=0):
    np.random.seed(seed)
    _w = jnp.asarray

    def _rec_inputs():
        import jax
        import jax.numpy as jnp
        _rk = jax.random.key(seed)
        x = -0.0005207 + 1.001 * jax.random.normal(jax.random.fold_in(_rk, 1), (32, 32, 512), jnp.float32)
        _lenS = 32 - jax.random.randint(jax.random.fold_in(_rk, 7), (32,), 0, max(1, 32 // 4) + 1, jnp.int32)
        _lenS2 = 32 - jax.random.randint(jax.random.fold_in(_rk, 8), (32,), 0, max(1, 32 // 4) + 1, jnp.int32)
        itok_Bx16_0_63 = jax.random.randint(jax.random.fold_in(_rk, 11), (32, 16), 0, 64, jnp.int32)
        itok_B_207_1644 = jax.random.randint(jax.random.fold_in(_rk, 12), (32,), 207, 1645, jnp.int32)
        itok_B_78_3631 = jax.random.randint(jax.random.fold_in(_rk, 13), (32,), 78, 454, jnp.int32)
        return (x, itok_Bx16_0_63, itok_B_207_1644, itok_B_78_3631)
    x, itok_Bx16_0_63, itok_B_207_1644, itok_B_78_3631 = _rec_inputs()

    def _L0_cond_setup():
        import jax, jax.numpy as jnp
        import numpy as np
        B, S, HID = (4, 128, 512)
        D, HQ, HK = (128, 32, 8)
        PAGES, PSIZE, NPP = (64, 32, 16)
        THETA = 10000.0
        EPS = 1e-06
        SCALE = 1.0 / float(np.sqrt(D))

        def _rmsnorm(t, w):
            var = jnp.mean(t * t, axis=-1, keepdims=True)
            return t * jax.lax.rsqrt(var + EPS) * w

        def _rope(t, pos):
            inv_freq = 1.0 / THETA ** (jnp.arange(0, D, 2, dtype=jnp.float32) / D)
            freqs = pos[..., None].astype(jnp.float32) * inv_freq
            cos = jnp.cos(freqs)[:, :, None, :]
            sin = jnp.sin(freqs)[:, :, None, :]
            t1, t2 = (t[..., :D // 2], t[..., D // 2:])
            return jnp.concatenate([t1 * cos - t2 * sin, t2 * cos + t1 * sin], axis=-1)
        key = jax.random.key(seed)
        ks = jax.random.split(key, 10)
        x = jax.random.normal(ks[0], (B, S, HID), jnp.float32)
        Wq = jax.random.normal(ks[1], (HQ * D, HID), jnp.float32) * 0.02
        Wk = jax.random.normal(ks[2], (HK * D, HID), jnp.float32) * 0.02
        Wv = jax.random.normal(ks[3], (HK * D, HID), jnp.float32) * 0.02
        Wo = jax.random.normal(ks[4], (HID, HQ * D), jnp.float32) * 0.02
        q_norm_w = jax.random.uniform(ks[5], (D,), jnp.float32)
        k_norm_w = jax.random.uniform(ks[6], (D,), jnp.float32)
        k_cache = jax.random.normal(ks[7], (PAGES, PSIZE, HK, D), jnp.float32)
        v_cache = jax.random.normal(ks[8], (PAGES, PSIZE, HK, D), jnp.float32)
        block_table = jnp.arange(B * NPP, dtype=jnp.int32).reshape(B, NPP)
        cache_seqlens = jax.random.randint(ks[9], (B,), 0, 475).astype(jnp.int32)
        return dict(x=x, Wq=Wq, Wk=Wk, Wv=Wv, Wo=Wo, q_norm_w=q_norm_w, k_norm_w=k_norm_w, k_cache=k_cache, v_cache=v_cache, block_table=block_table, cache_seqlens=cache_seqlens)
    _L0_cond_all = _L0_cond_setup()
    _L0_cond_in = {k: v for k, v in _L0_cond_all.items() if k in ('Wq', 'Wk', 'Wv', 'Wo', 'q_norm_w', 'k_norm_w', 'k_cache', 'v_cache')}
    del _L0_cond_all

    def _L1_cond_setup():
        import math
        import jax, jax.numpy as jnp
        import numpy as np
        B, H, N, L = (16, 32, 64, 512)
        DT_MIN, DT_MAX = (0.001, 0.1)

        def _get_kernel(log_dt, C, log_A_real, A_imag, length):
            dt = jnp.exp(log_dt)
            Cc = C[..., 0] + 1j * C[..., 1]
            A = -jnp.exp(log_A_real) + 1j * A_imag
            dtA = A * dt[:, None]
            Ct = Cc * (jnp.exp(dtA) - 1.0) / A
            P = dtA[:, :, None] * jnp.arange(length, dtype=jnp.float32)
            K = 2.0 * jnp.einsum('hn,hnl->hl', Ct, jnp.exp(P)).real
            return K
        key = jax.random.key(seed)
        ks = jax.random.split(key, 5)
        u = jax.random.normal(ks[0], (B, H, L), dtype=jnp.float32)
        log_dt = jax.random.uniform(ks[1], (H,), dtype=jnp.float32) * (math.log(DT_MAX) - math.log(DT_MIN)) + math.log(DT_MIN)
        C = jax.random.normal(ks[2], (H, N, 2), dtype=jnp.float32)
        log_A_real = jnp.log(0.5 * jnp.ones((H, N), dtype=jnp.float32))
        A_imag = math.pi * jnp.broadcast_to(jnp.arange(N, dtype=jnp.float32), (H, N))
        D = jax.random.normal(ks[3], (H,), dtype=jnp.float32)
        length = jax.random.randint(ks[4], (B,), 1, L + 1, dtype=jnp.int32)
        return {'u': u, 'log_dt': log_dt, 'C': C, 'log_A_real': log_A_real, 'A_imag': A_imag, 'D': D, 'length': length}
    _L1_cond_all = _L1_cond_setup()
    _L1_cond_in = {k: v for k, v in _L1_cond_all.items() if k in ('log_dt', 'C', 'log_A_real', 'A_imag', 'D')}
    del _L1_cond_all
    return {'x': x, 'itok_Bx16_0_63': itok_Bx16_0_63, 'itok_B_207_1644': itok_B_207_1644, 'itok_B_78_3631': itok_B_78_3631, 'L0_cond_Wq': _L0_cond_in['Wq'], 'L0_cond_Wk': _L0_cond_in['Wk'], 'L0_cond_Wv': _L0_cond_in['Wv'], 'L0_cond_Wo': _L0_cond_in['Wo'], 'L0_cond_q_norm_w': _L0_cond_in['q_norm_w'], 'L0_cond_k_norm_w': _L0_cond_in['k_norm_w'], 'L0_cond_k_cache': _L0_cond_in['k_cache'], 'L0_cond_v_cache': _L0_cond_in['v_cache'], 'L1_cond_log_dt': _L1_cond_in['log_dt'], 'L1_cond_C': _L1_cond_in['C'], 'L1_cond_log_A_real': _L1_cond_in['log_A_real'], 'L1_cond_A_imag': _L1_cond_in['A_imag'], 'L1_cond_D': _L1_cond_in['D']}

def reference(x, itok_Bx16_0_63, itok_B_207_1644, itok_B_78_3631, L0_cond_Wq, L0_cond_Wk, L0_cond_Wv, L0_cond_Wo, L0_cond_q_norm_w, L0_cond_k_norm_w, L0_cond_k_cache, L0_cond_v_cache, L1_cond_log_dt, L1_cond_C, L1_cond_log_A_real, L1_cond_A_imag, L1_cond_D):
    import jax
    import jax.numpy as jnp

    def _L0_cond_ref(x, Wq, Wk, Wv, Wo, q_norm_w, k_norm_w, k_cache, v_cache, block_table, cache_seqlens):
        import jax, jax.numpy as jnp
        import numpy as np
        B, S, HID = (4, 128, 512)
        D, HQ, HK = (128, 32, 8)
        PAGES, PSIZE, NPP = (64, 32, 16)
        THETA = 10000.0
        EPS = 1e-06
        SCALE = 1.0 / float(np.sqrt(D))

        def _rmsnorm(t, w):
            var = jnp.mean(t * t, axis=-1, keepdims=True)
            return t * jax.lax.rsqrt(var + EPS) * w

        def _rope(t, pos):
            inv_freq = 1.0 / THETA ** (jnp.arange(0, D, 2, dtype=jnp.float32) / D)
            freqs = pos[..., None].astype(jnp.float32) * inv_freq
            cos = jnp.cos(freqs)[:, :, None, :]
            sin = jnp.sin(freqs)[:, :, None, :]
            t1, t2 = (t[..., :D // 2], t[..., D // 2:])
            return jnp.concatenate([t1 * cos - t2 * sin, t2 * cos + t1 * sin], axis=-1)
        bsz, seqlen, _ = x.shape
        q = jnp.einsum('bsd,ed->bse', x, Wq).reshape(bsz, seqlen, HQ, D)
        k = jnp.einsum('bsd,ed->bse', x, Wk).reshape(bsz, seqlen, HK, D)
        v = jnp.einsum('bsd,ed->bse', x, Wv).reshape(bsz, seqlen, HK, D)
        q = _rmsnorm(q, q_norm_w)
        k = _rmsnorm(k, k_norm_w)
        pos = cache_seqlens[:, None] + jnp.arange(seqlen)[None, :]
        q = _rope(q, pos)
        k = _rope(k, pos)
        L = NPP * PSIZE
        kc = k_cache[block_table].reshape(bsz, L, HK, D)
        vc = v_cache[block_table].reshape(bsz, L, HK, D)
        k_all = jnp.concatenate([kc, k], axis=1)
        v_all = jnp.concatenate([vc, v], axis=1)
        valid_c = jnp.arange(L)[None, :] < cache_seqlens[:, None]
        valid = jnp.concatenate([valid_c, jnp.ones((bsz, seqlen), dtype=bool)], axis=1)
        rep = HQ // HK
        k_all = jnp.repeat(k_all, rep, axis=2)
        v_all = jnp.repeat(v_all, rep, axis=2)
        scores = jnp.einsum('bqhd,bkhd->bhqk', q, k_all) * SCALE
        scores = jnp.where(valid[:, None, None, :], scores, -1e+30)
        probs = jax.nn.softmax(scores, axis=-1)
        o = jnp.einsum('bhqk,bkhd->bqhd', probs, v_all)
        o = o.reshape(bsz, seqlen, HQ * D)
        return jnp.einsum('bse,de->bsd', o, Wo)

    def _L1_cond_ref(u, log_dt, C, log_A_real, A_imag, D, length):
        import math
        import jax, jax.numpy as jnp
        import numpy as np
        B, H, N, L = (16, 32, 64, 512)
        DT_MIN, DT_MAX = (0.001, 0.1)

        def _get_kernel(log_dt, C, log_A_real, A_imag, length):
            dt = jnp.exp(log_dt)
            Cc = C[..., 0] + 1j * C[..., 1]
            A = -jnp.exp(log_A_real) + 1j * A_imag
            dtA = A * dt[:, None]
            Ct = Cc * (jnp.exp(dtA) - 1.0) / A
            P = dtA[:, :, None] * jnp.arange(length, dtype=jnp.float32)
            K = 2.0 * jnp.einsum('hn,hnl->hl', Ct, jnp.exp(P)).real
            return K
        Bq, Hq, Lq = u.shape
        K = _get_kernel(log_dt, C, log_A_real, A_imag, Lq)
        n = 2 * Lq
        kf = jnp.fft.rfft(K, n=n)
        uf = jnp.fft.rfft(u, n=n)
        y = jnp.fft.irfft(uf * kf[None], n=n)[..., :Lq]
        y = y + u * D[:, None]
        mask = (jnp.arange(Lq)[None, :] < length[:, None]).astype(u.dtype)
        return y * mask[:, None, :]
    x = x + _L0_cond_ref(x, L0_cond_Wq, L0_cond_Wk, L0_cond_Wv, L0_cond_Wo, L0_cond_q_norm_w, L0_cond_k_norm_w, L0_cond_k_cache, L0_cond_v_cache, itok_Bx16_0_63, itok_B_207_1644)
    x = x + _L1_cond_ref(x, L1_cond_log_dt, L1_cond_C, L1_cond_log_A_real, L1_cond_A_imag, L1_cond_D, itok_B_78_3631)
    return x

_drawn_inputs = setup_inputs


def setup_inputs(seed=0):
    import zlib

    import numpy as np

    out = dict(_drawn_inputs(seed))
    spreads = {'L1_cond_log_A_real': (-0.6931471824645996, 0.2)}
    factors = {'L0_cond_Wk': 8.0,
     'L0_cond_Wv': 8.0,
     'L0_cond_k_norm_w': 8.0,
     'L0_cond_k_cache': 4.308,
     'L0_cond_v_cache': 3.113}
    for name, (base, spread) in spreads.items():
        noise = np.random.default_rng([zlib.crc32(name.encode()), seed]).standard_normal(out[name].shape)
        drawn = base * np.exp(spread * noise) if base else spread * noise
        out[name] = jnp.asarray(drawn.astype(out[name].dtype))
    for name, factor in factors.items():
        out[name] = (out[name] * factor).astype(out[name].dtype)
    return out
```

```python
from contextlib import ExitStack

import numpy as np

import concourse.bass as bass
from concourse import mybir

F32 = mybir.dt.float32
F16 = mybir.dt.float16
I32 = mybir.dt.int32
ALU = mybir.AluOpType
ACT = mybir.ActivationFunctionType
AX_X = mybir.AxisListType.X

P = 128
B, S, HID = 32, 32, 512
D, HQ, HK = 128, 32, 8
REP = HQ // HK
PAGES, PSIZE, NPP = 64, 32, 16
L = NPP * PSIZE
KEYS = L + S
HALF = KEYS // 2
TOK = B * S
TILES = TOK // P
BPT = P // S
KT = HID // P
E_ALL = (HQ + 2 * HK) * D
CHUNKS = E_ALL // 512
NORMED = (HQ + HK) * D // 512
QCH = HQ * D // 512
NPIECE = 4
UNITS = 2 * HK
NSTATE, LCONV = 64, HID
KA, KB = 16, 32
EPS = 1e-6
SCALE = 1.0 / float(np.sqrt(D))
WSCALE = 64.0
NEG = -1e30
MAGIC = 1.5 * 2.0 ** 23
TWO_PI = 6.283185307179586
PI2_HI = 6.28125
PI2_MID = float(np.float32(np.float16(TWO_PI - PI2_HI)))
PI2_LO = TWO_PI - PI2_HI - PI2_MID
PI_SAFE = 3.1415925
ROT_LAG, TURN_LAG = 2, 3

_cols, _at = {}, 0
for _name, _n in (("ident", P), ("token_in_batch", 1), ("inv_freq", D // 2),
                  ("hid_index", KT), ("a_step", KA), ("b_step", KB), ("v_turn", 1), ("v_angle", 1),
                  ("mix", 4)):
    _cols[_name] = slice(_at, _at + _n)
    _at += _n
NCONST = _at


def phase0(nc, dram, keep):
    const, w_hi, w_lo, cos_t, sin_t, w_tab = (
        keep[k] for k in ("const", "w_hi", "w_lo", "cos_t", "sin_t", "w_tab"))
    with ExitStack() as ctx:
        def sb(name, shape, dt):
            return ctx.enter_context(nc.sbuf_tensor("p0_" + name, shape, dt))

        def sem(name):
            return ctx.enter_context(nc.semaphore("p0_" + name))

        w_in = sb("w_in", [P, 3, KT, 512], F32)
        seq_i = sb("seq_i", [P, TILES], I32)
        pos = sb("pos", [P, TILES], F32)
        ang = sb("ang", [P, TILES, D // 2], F32)
        turns = sb("turns", [P, TILES, D // 2], F32)
        red_c = sb("red_c", [P, TILES, D // 2], F32)
        red_s = sb("red_s", [P, TILES, D // 2], F32)
        const_in, w_loaded = sem("const_in"), [sem(f"w_loaded{i}") for i in range(3)]
        w_hi_done, w_free = sem("w_hi_done"), sem("w_free")
        rope_step, angles_done, sincos_done = sem("rope_step"), sem("angles_done"), sem("sincos_done")
        block = ctx.enter_context(nc.Block())

        @block.sync
        def _(sp):
            sp.dma_start(const[:, :], dram["consts"]).then_inc(const_in, 16)
            sp.dma_start(seq_i[:, :], dram["seqlens_by_token"]).then_inc(const_in, 16)
            sp.dma_start(w_tab[:, :, :], dram["norm_w"]).then_inc(const_in, 16)
            w_src = dram["w_all"].rearrange("(i p) e -> p i e", p=P)
            with sp.Fori(0, CHUNKS // 3) as c3:
                for k in range(3):
                    sp.wait_ge(w_free, c3 * 3 + k + 1)
                    sp.dma_start(w_in[:, k, :, :],
                                 w_src[:, :, bass.ds((c3 * 3 + k) * 512, 512)]).then_inc(w_loaded[k], 16)

        @block.scalar
        def _(act):
            with act.Fori(0, CHUNKS // 3) as c3:
                for k in range(3):
                    act.wait_ge(w_loaded[k], c3 * 16 + 16)
                    nc.scalar.activation(w_hi[:, :, bass.ds((c3 * 3 + k) * 512, 512)], w_in[:, k, :, :],
                                         ACT.Copy, scale=WSCALE).then_inc(w_hi_done, 1)
            act.wait_ge(angles_done, 2)
            nc.scalar.activation(cos_t[:, :, :], red_c[:, :, :], ACT.Sin).then_inc(sincos_done, 1)
            nc.scalar.activation(sin_t[:, :, :], red_s[:, :, :], ACT.Sin).then_inc(sincos_done, 1)

        @block.vector
        def _(dve):
            nc.vector.memset(pos[:, :], 0.0).then_inc(w_free, 3)
            dve.wait_ge(w_free, 3)
            dve.wait_ge(const_in, 16 * 3)
            steps = [0]

            def stepped(instruction):
                steps[0] += 1
                instruction.then_inc(rope_step, 1)
                dve.wait_ge(rope_step, steps[0])

            stepped(nc.vector.tensor_copy(pos[:, :], seq_i[:, :]))
            stepped(nc.vector.tensor_scalar(pos[:, :], pos[:, :], const[:, _cols["token_in_batch"]], None, ALU.add))
            freq = const[:, _cols["inv_freq"]]
            stepped(nc.vector.tensor_tensor(
                ang[:, :, :], pos[:, :].rearrange("p (t o) -> p t o", o=1).broadcast_to([P, TILES, D // 2]),
                freq.rearrange("p (o f) -> p o f", o=1).broadcast_to([P, TILES, D // 2]), ALU.mult))
            for quarter, red in ((0.25, red_c), (0.0, red_s)):
                stepped(nc.vector.tensor_scalar(turns[:, :, :], ang[:, :, :], 1.0 / TWO_PI, quarter, ALU.mult, ALU.add))
                stepped(nc.vector.tensor_scalar(turns[:, :, :], turns[:, :, :], MAGIC, MAGIC, ALU.add, ALU.subtract))
                src = ang
                for part in (PI2_HI, PI2_MID, PI2_LO):
                    stepped(nc.vector.scalar_tensor_tensor(out=red[:, :, :], in0=turns[:, :, :], scalar=-part,
                                                           in1=src[:, :, :], op0=ALU.mult, op1=ALU.add))
                    src = red
                stepped(nc.vector.tensor_scalar(red[:, :, :], red[:, :, :], quarter * TWO_PI, PI_SAFE, ALU.add, ALU.min))
                nc.vector.tensor_scalar(red[:, :, :], red[:, :, :], -PI_SAFE, None, ALU.max).then_inc(angles_done, 1)
            for j in range(2):
                stepped(nc.vector.tensor_scalar(w_tab[:, 2 * j + 1, 0:D // 2], w_tab[:, 2 * j + 1, 0:D // 2],
                                                -1.0, None, ALU.mult))
            with dve.Fori(0, CHUNKS // 3) as c3:
                for k in range(3):
                    dve.wait_ge(w_hi_done, c3 * 3 + k + 1)
                    nc.vector.scalar_tensor_tensor(
                        out=w_lo[:, :, bass.ds((c3 * 3 + k) * 512, 512)], in0=w_in[:, k, :, :], scalar=WSCALE,
                        in1=w_hi[:, :, bass.ds((c3 * 3 + k) * 512, 512)], op0=ALU.mult,
                        op1=ALU.subtract).then_inc(w_free, 1)
            dve.wait_ge(w_free, CHUNKS + 3)
            dve.wait_ge(sincos_done, 2)


def phase1(nc, dram, keep):
    const, w_hi, w_lo, cos_t, sin_t, w_tab, kt_all = (
        keep[k] for k in ("const", "w_hi", "w_lo", "cos_t", "sin_t", "w_tab", "kt_all"))
    ident = const[:, _cols["ident"]]
    with ExitStack() as ctx:
        def sb(name, shape, dt):
            return ctx.enter_context(nc.sbuf_tensor("p1_" + name, shape, dt))

        def ps(name, shape):
            return ctx.enter_context(nc.psum_tensor("p1_" + name, shape, F32))

        def sem(name):
            return ctx.enter_context(nc.semaphore("p1_" + name))

        x_in = sb("x_in", [P, KT, P], F32)
        x_hi = sb("x_hi", [P, 2, KT, P], F16)
        x_lo = sb("x_lo", [P, 2, KT, P], F16)
        piece_in = sb("piece_in", [P, 3, 512], F32)
        piece_out = sb("piece_out", [P, 2, 2, 512], F16)
        eps_t = sb("eps_t", [P, 2], F32)
        sumsq = sb("sumsq", [P, 2, REP], F32)
        rms = sb("rms", [P, 2, REP], F32)
        rrms = sb("rrms", [P, 2, REP], F32)
        normed = sb("normed", [P, 2, REP, D], F32)
        rot_a = sb("rot_a", [P, 3, REP, D], F32)
        rot_b = sb("rot_b", [P, 2, REP, D], F32)
        tables = sb("tables", [P, 4, D], F32)
        v_stage = sb("v_stage", [P, 2, 2, 512], F16)
        stage = sb("stage", [P, 2, 1024], F16)
        proj = [ps(f"proj{i}", [P, 512]) for i in range(3)]
        squares = ps("squares", [P, REP, D])
        turned = [ps(f"turned{i}", [P, 512]) for i in range(2)]

        x_loaded, x_hi_done, x_lo_done = sem("x_loaded"), sem("x_hi_done"), sem("x_lo_done")
        piece_loaded = [sem(f"piece_loaded{i}") for i in range(3)]
        piece_hi_done, piece_free = sem("piece_hi_done"), sem("piece_free")
        piece_stored = [sem("piece_stored0"), sem("piece_stored1")]
        proj_done, proj_free = sem("proj_done"), sem("proj_free")
        squares_done, rms_done, rrms_done = sem("squares_done"), sem("rms_done"), sem("rrms_done")
        normed_done, rotated_parts, rotated, turned_done = (
            sem("normed_done"), sem("rotated_parts"), sem("rotated"), sem("turned_done"))
        table_done = sem("table_done")
        stage_hi_done, stage_lo_done, v_hi_done = sem("stage_hi_done"), sem("stage_lo_done"), sem("v_hi_done")
        stored = [sem(f"stored{i}") for i in range(2)]
        v_stored = [sem(f"v_stored{i}") for i in range(2)]
        block = ctx.enter_context(nc.Block())

        def k_piece(tile, c, part):
            pages = kt_all[:, bass.ds((tile * NPIECE + c // 3) * 2, 2), :, part, :]
            return pages

        def split_q(slot, part):
            return stage[:, slot, :].rearrange("p (b l h s) -> p l h b s", b=BPT, l=2, h=REP)[:, part]

        def split_k(slot, part):
            return stage[:, slot, :].rearrange("p (b h l s) -> p l h b s", b=BPT, h=REP, l=2)[:, part]

        @block.sync
        def _(sp):
            x_src = dram["xt"].rearrange("(i p) t -> p i t", p=P)
            v_src = dram["v_cache"].rearrange("(t p) (h e) -> p t h e", p=P, e=512)
            o_src = dram["wo_t"].rearrange("(h p) n -> p h n", p=P)

            def load_piece(tile, c):
                sp.wait_ge(piece_free, tile * CHUNKS + c + 1)
                nth = tile * NPIECE + c // 3
                if c % 3 == 0:
                    src = dram["kt"][:, bass.ds(nth * 512, 512)]
                elif c % 3 == 1:
                    src = v_src[:, bass.ds(tile * 2 + c // 6, 1), (c // 3) % 2, :]
                else:
                    src = o_src[:, bass.ds(nth, 1), :]
                sp.dma_start(piece_in[:, c % 3, :], src).then_inc(piece_loaded[c % 3], 16)

            def store_chunk(tile, j):
                needed = sp.compute_val(tile * NORMED + j + 1)
                if j >= QCH:
                    sp.wait_ge(piece_free, 3)
                sp.wait_ge(stage_lo_done, needed)
                dst = dram["q_t"][bass.ds(tile * BPT, BPT), :, j, :] if j < QCH else \
                    dram["k_new"][bass.ds(tile * BPT, BPT), :, j - QCH, :]
                sp.dma_start(dst.rearrange("b p n -> p b n"),
                             stage[:, j % 2, :].rearrange("p (b n) -> p b n", b=BPT)).then_inc(stored[j % 2], 16)

            def store_v(tile, half):
                sp.wait_ge(proj_free, tile * CHUNKS + NORMED + half + 4)
                sp.dma_start(dram["v_new"][bass.ds(tile * P, P), :, half * 512:(half + 1) * 512],
                             v_stage[:, half, :, :]).then_inc(v_stored[half], 16)

            def store_piece(tile, c):
                sp.wait_ge(piece_free, tile * CHUNKS + c + 4)
                if c % 3 == 1:
                    half = (c // 3) % 2
                    dst = dram["v_split"][bass.ds((tile * 2 + c // 6) * P, P), :, half * 512:(half + 1) * 512]
                else:
                    dst = dram["wo_split"][:, bass.ds(tile * NPIECE + c // 3, 1), :, :].rearrange("p o l n -> p (o l) n")
                sp.dma_start(dst, piece_out[:, c % 3 - 1, :, :]).then_inc(piece_stored[c % 3 - 1], 16)

            sp.dma_start(x_in[:, :, :], x_src[:, :, 0:P]).then_inc(x_loaded, 16)
            for c in range(3):
                load_piece(0, c)
            with sp.Fori(0, TILES // 2) as i2:
                for tt in range(2):
                    tile = i2 * 2 + tt
                    for c in range(CHUNKS + 1):
                        if c >= TURN_LAG:
                            store_chunk(tile, c - TURN_LAG)
                        if c > NORMED:
                            store_v(tile, c - NORMED - 1)
                        if c == CHUNKS:
                            break
                        load_piece(tile + (c + 3) // CHUNKS, (c + 3) % CHUNKS)
                        if c % 3:
                            store_piece(tile, c)
                        if c == 1:
                            sp.wait_ge(x_lo_done, tile + 1)
                            sp.dma_start(x_in[:, :, :], x_src[:, :, bass.ds((tile + 1) * P, P)]).then_inc(x_loaded, 16)
            for slot in range(2):
                sp.wait_ge(stored[slot], TILES * (NORMED // 2) * 16)
                sp.wait_ge(piece_stored[slot], TILES * NPIECE * 16)
                sp.wait_ge(v_stored[slot], TILES * 16)
            for slot in range(3):
                sp.wait_ge(piece_loaded[slot], (TILES * NPIECE + 1) * 16)
            sp.wait_ge(x_loaded, (TILES + 1) * 16)

        @block.tensor
        def _(pe):
            with pe.Fori(0, TILES // 2) as i2:
                for tt in range(2):
                    tile = i2 * 2 + tt
                    pe.wait_ge(x_lo_done, tile + 1)
                    for c in range(CHUNKS + 1):
                        if c >= TURN_LAG:
                            j = c - TURN_LAG
                            pe.wait_ge(rotated, tile * NORMED + j + 1)
                            pe.wait_ge(stage_lo_done, tile * NORMED + max(j - 1, 0))
                            for h in range(REP):
                                last = nc.tensor.transpose(turned[j % 2][:, h * P:(h + 1) * P],
                                                           rot_a[:, j % 3, h, :], ident)
                            last.then_inc(turned_done, 1)
                        if c == CHUNKS:
                            break
                        pe.wait_ge(proj_free, tile * CHUNKS + c + 1)
                        n = 0
                        for k in range(KT):
                            for x_part, w_part in ((x_hi, w_hi), (x_hi, w_lo), (x_lo, w_hi)):
                                last = nc.tensor.matmul(proj[c % 3][:, :], x_part[:, tt, k, :],
                                                        w_part[:, k, c * 512:(c + 1) * 512],
                                                        start=(n == 0), stop=(n == 3 * KT - 1))
                                n += 1
                        last.then_inc(proj_done, 1)

        @block.scalar
        def _(act):
            act.wait_ge(proj_free, 3)
            act.wait_ge(x_loaded, 16)
            nc.scalar.activation(x_hi[:, 0, :, :], x_in[:, :, :], ACT.Copy).then_inc(x_hi_done, 1)
            with act.Fori(0, TILES // 2) as i2:
                for tt in range(2):
                    tile = i2 * 2 + tt

                    for c in range(CHUNKS + 1):
                        if c >= TURN_LAG:
                            j = c - TURN_LAG
                            act.wait_ge(turned_done, tile * NORMED + j + 1)
                            act.wait_ge(stored[j % 2], (tile * (NORMED // 2) + j // 2) * 16)
                            split = split_q if j < QCH else split_k
                            nc.scalar.activation(split(j % 2, 0),
                                                 turned[j % 2][:, :].rearrange("p (h b s) -> p h b s", h=REP, b=BPT),
                                                 ACT.Copy).then_inc(stage_hi_done, 1)
                        if c == CHUNKS:
                            break
                        slot, nth = c % 3, tile * NPIECE + c // 3
                        act.wait_ge(piece_loaded[slot], (nth + 1) * 16)
                        if slot == 0:
                            nc.scalar.activation(k_piece(tile, c, 0),
                                                 piece_in[:, slot, :].rearrange("p (g h s) -> p g h s", g=2, h=HK),
                                                 ACT.Copy).then_inc(piece_hi_done, 1)
                        else:
                            act.wait_ge(piece_stored[slot - 1], nth * 16)
                            nc.scalar.activation(piece_out[:, slot - 1, 0, :], piece_in[:, slot, :], ACT.Copy,
                                                 scale=WSCALE if slot == 2 else 1.0).then_inc(piece_hi_done, 1)
                        act.wait_ge(proj_done, tile * CHUNKS + c + 1)
                        if c < NORMED:
                            n = tile * NORMED + c
                            act.wait_ge(squares_done, n * REP)
                            for h in range(REP):
                                nc.scalar.activation(squares[:, h, :], proj[c % 3][:, h * D:(h + 1) * D], ACT.Square,
                                                     accum_out=sumsq[:, c % 2, h:h + 1]).then_inc(squares_done, 1)
                            act.wait_ge(squares_done, (n + 1) * REP)
                            act.wait_ge(rrms_done, tile * NORMED + max(c - 1, 0))
                            nc.scalar.activation(rms[:, c % 2, :], sumsq[:, c % 2, :], ACT.Sqrt,
                                                 bias=eps_t[:, 0:1], scale=1.0 / D).then_inc(rms_done, 1)
                        else:
                            act.wait_ge(v_stored[c - NORMED], tile * 16)
                            nc.scalar.activation(v_stage[:, c - NORMED, 0, :], proj[c % 3][:, :], ACT.Copy,
                                                 scale=1.0 / WSCALE).then_inc(v_hi_done, 1)
                        if c == 5:
                            act.wait_ge(x_loaded, (tile + 2) * 16)
                            act.wait_ge(proj_done, tile * CHUNKS)
                            nc.scalar.activation(x_hi[:, 1 - tt, :, :], x_in[:, :, :], ACT.Copy).then_inc(x_hi_done, 1)

        @block.vector
        def _(dve):
            nc.vector.memset(eps_t[:, 0:1], EPS * WSCALE * WSCALE).then_inc(proj_free, 3)
            nc.vector.memset(eps_t[:, 1:2], 0.0).then_inc(piece_free, 3)
            dve.wait_ge(x_hi_done, 1)
            nc.vector.tensor_tensor(x_lo[:, 0, :, :], x_in[:, :, :], x_hi[:, 0, :, :], ALU.subtract).then_inc(x_lo_done, 1)
            with dve.Fori(0, TILES // 2) as i2:
                for tt in range(2):
                    tile = i2 * 2 + tt
                    for c in range(CHUNKS + 1):
                        if c >= TURN_LAG:
                            j = c - TURN_LAG
                            split = split_q if j < QCH else split_k
                            dve.wait_ge(stage_hi_done, tile * NORMED + j + 1)
                            nc.vector.tensor_tensor(split(j % 2, 1),
                                                    turned[j % 2][:, :].rearrange("p (h b s) -> p h b s", h=REP, b=BPT),
                                                    split(j % 2, 0), ALU.subtract).then_inc(stage_lo_done, 1)
                        if c == CHUNKS:
                            break
                        if ROT_LAG <= c < NORMED + ROT_LAG:
                            j = c - ROT_LAG
                            dve.wait_ge(rotated_parts, (tile * NORMED + j + 1) * 2)
                            nc.vector.tensor_tensor(rot_a[:, j % 3, :, :], rot_a[:, j % 3, :, :],
                                                    rot_b[:, j % 2, :, :], ALU.add).then_inc(rotated, 1)
                        if c < NORMED:
                            n = tile * NORMED + c
                            dve.wait_ge(rms_done, n + 1)
                            nc.vector.reciprocal(rrms[:, c % 2, :], rms[:, c % 2, :]).then_inc(rrms_done, 1)
                            dve.wait_ge(rrms_done, n + 1)
                            nc.vector.tensor_tensor(
                                normed[:, c % 2, :, :], proj[c % 3][:, :].rearrange("p (h d) -> p h d", h=REP),
                                rrms[:, c % 2, :].rearrange("p (h o) -> p h o", o=1).broadcast_to([P, REP, D]),
                                ALU.mult).then_inc(proj_free, 1)
                        else:
                            dve.wait_ge(v_hi_done, tile * (CHUNKS - NORMED) + c - NORMED + 1)
                            nc.vector.scalar_tensor_tensor(out=v_stage[:, c - NORMED, 1, :], in0=proj[c % 3][:, :],
                                                           scalar=1.0 / WSCALE, in1=v_stage[:, c - NORMED, 0, :],
                                                           op0=ALU.mult, op1=ALU.subtract).then_inc(proj_free, 1)
                        if c % 3 != 1:
                            dve.wait_ge(piece_hi_done, tile * CHUNKS + c + 1)
                            dve.wait_ge(piece_free, tile * CHUNKS + c + 3)
                            if c % 3 == 0:
                                nc.vector.tensor_tensor(k_piece(tile, c, 1),
                                                        piece_in[:, 0, :].rearrange("p (g h s) -> p g h s", g=2, h=HK),
                                                        k_piece(tile, c, 0), ALU.subtract).then_inc(piece_free, 1)
                            else:
                                nc.vector.scalar_tensor_tensor(out=piece_out[:, 1, 1, :], in0=piece_in[:, 2, :],
                                                               scalar=WSCALE, in1=piece_out[:, 1, 0, :],
                                                               op0=ALU.mult, op1=ALU.subtract).then_inc(piece_free, 1)
                        if c == 5:
                            dve.wait_ge(x_hi_done, tile + 2)
                            nc.vector.tensor_tensor(x_lo[:, 1 - tt, :, :], x_in[:, :, :], x_hi[:, 1 - tt, :, :],
                                                    ALU.subtract).then_inc(x_lo_done, 1)

        @block.gpsimd
        def _(pool):
            with pool.Fori(0, TILES // 2) as i2:
                for tt in range(2):
                    tile = i2 * 2 + tt
                    pool.wait_ge(rotated_parts, tile * NORMED * 2)
                    for j, trig in enumerate((cos_t, sin_t, cos_t, sin_t)):
                        nc.gpsimd.tensor_tensor(
                            tables[:, j, :].rearrange("p (a f) -> p a f", a=2),
                            trig[:, bass.ds(tile, 1), :].broadcast_to([P, 2, D // 2]),
                            w_tab[:, j, :].rearrange("p (a f) -> p a f", a=2), ALU.mult).then_inc(table_done, 1)
                    pool.wait_ge(table_done, (tile + 1) * 4)
                    for c in range(CHUNKS):
                        if c % 3 == 1:
                            pool.wait_ge(piece_hi_done, tile * CHUNKS + c + 1)
                            pool.wait_ge(piece_free, tile * CHUNKS + c + 3)
                            nc.gpsimd.tensor_tensor(piece_out[:, 0, 1, :], piece_in[:, 1, :],
                                                    piece_out[:, 0, 0, :], ALU.subtract).then_inc(piece_free, 1)
                        if c < NORMED:
                            pool.wait_ge(proj_free, tile * CHUNKS + c + 4)
                            pool.wait_ge(turned_done, tile * NORMED + max(c - 2, 0))
                            kind, half = 0 if c < QCH else 2, D // 2
                            cos_b, sin_b = (tables[:, kind + k, :].rearrange("p (o d) -> p o d", o=1)
                                            .broadcast_to([P, REP, D]) for k in range(2))
                            nc.gpsimd.tensor_tensor(rot_a[:, c % 3, :, :], normed[:, c % 2, :, :], cos_b,
                                                    ALU.mult).then_inc(rotated_parts, 1)
                            for k in range(2):
                                ins = nc.gpsimd.tensor_tensor(rot_b[:, c % 2, :, k * half:(k + 1) * half],
                                                              normed[:, c % 2, :, (1 - k) * half:(2 - k) * half],
                                                              sin_b[:, :, k * half:(k + 1) * half], ALU.mult)
                            ins.then_inc(rotated_parts, 1)


def phase2(nc, dram, keep):
    const, kt_all = keep["const"], keep["kt_all"]
    ident = const[:, _cols["ident"]]
    pool_pages = 12
    last_iter = B // 2 - 1
    with ExitStack() as ctx:
        def sb(name, shape, dt):
            return ctx.enter_context(nc.sbuf_tensor("p2_" + name, shape, dt))

        def ps(name, shape):
            return ctx.enter_context(nc.psum_tensor("p2_" + name, shape, F32))

        def sem(name):
            return ctx.enter_context(nc.semaphore("p2_" + name))

        key_index = sb("key_index", [P, KEYS], F32)
        lens_i = sb("lens_i", [P, B], I32)
        lens = sb("lens", [P, B], F32)
        pages_i = sb("pages_i", [1, B * NPP // 4, 4], I32)
        pages_f = sb("pages_f", [1, B * NPP // 4, 4], F32)
        packed_f = sb("packed_f", [1, B * NPP // 4], F32)
        packed = sb("packed", [1, B * NPP // 4], I32)
        q_in = sb("q_in", [P, 2, HK, 2, P], F16)
        kn_in = sb("kn_in", [P, 2, HK, 2, S], F16)
        keys = sb("keys", [P, 2, HK, 2, KEYS], F16)
        v_in = sb("v_in", [P, 2, KT, 2, HK, D], F16)
        vn_in = sb("vn_in", [S, 2, 2, HK, D], F16)
        mask = sb("mask", [P, 2, KEYS], F32)
        masked = sb("masked", [P, 2, KEYS], F32)
        rowmax = sb("rowmax", [P, 4], F32)
        bias = sb("bias", [P, 4], F32)
        denom = sb("denom", [P, 4], F32)
        rdenom = sb("rdenom", [P, 4], F32)
        probs = sb("probs", [P, 2, KEYS], F32)
        pt_hi = sb("pt_hi", [P, 2, 5, P], F16)
        pt_lo = sb("pt_lo", [P, 2, 5, P], F16)
        o_stage = sb("o_stage", [P, 2, 4, D], F32)
        scores = [ps(f"scores{i}", [P, 2, 512]) for i in range(2)]
        pt_old = [ps(f"pt_old{i}", [P, 4, P]) for i in range(2)]
        pt_new = ps("pt_new", [P, 512])
        o_acc = ps("o_acc", [P, 512])
        kt32 = kt_all[:, :, :, :, :].bitcast(F32)
        keys32 = keys[:, :, :, :, :].bitcast(F32)
        kn32 = kn_in[:, :, :, :, :].bitcast(F32)
        W = PSIZE // 2

        tables_in, packed_done = sem("tables_in"), sem("packed_done")
        q_loaded = [sem("q_loaded0"), sem("q_loaded1")]
        kn_loaded = [sem("kn_loaded0"), sem("kn_loaded1")]
        vn_loaded = [sem("vn_loaded0"), sem("vn_loaded1")]
        v_loaded = [sem("v_loaded0"), sem("v_loaded1")]
        keys_pool, keys_dve = sem("keys_pool"), sem("keys_dve")
        scores_done, masked_done, bias_done = sem("scores_done"), sem("masked_done"), sem("bias_done")
        mask_done, rdenom_done, exp_done = sem("mask_done"), sem("rdenom_done"), sem("exp_done")
        turned_new, turned_old = sem("turned_new"), sem("turned_old")
        hi_new, hi_old, lo_new, lo_old = sem("hi_new"), sem("hi_old"), sem("lo_new"), sem("lo_old")
        pv_done, o_done = sem("pv_done"), sem("o_done")
        o_stored = [sem("o_stored0"), sem("o_stored1")]
        block = ctx.enter_context(nc.Block())

        def page_of(eng, batch, j, words):
            if j % 4 == 0:
                words[0] = eng.value_load(packed[0:1, bass.ds(batch * (NPP // 4) + j // 4, 1)],
                                          min_val=0, max_val=PAGES ** 4 - 1)
            return (words[0] >> (6 * (j % 4))) & (PAGES - 1)

        def gather(eng, ops, batch, buf, j, words):
            page = page_of(eng, batch, j, words)
            src = kt32[:, bass.ds(page, 1), :, :, :].rearrange("p o h l w -> p (o h) l w")
            return ops.tensor_copy(keys32[:, buf, :, :, j * W:(j + 1) * W], src)

        @block.sync
        def _(sp):
            sp.dma_start(pages_i[:, :, :], dram["pages"].rearrange("a (b c) -> a b c", c=4)).then_inc(tables_in, 16)
            sp.dma_start(lens_i[:, :], dram["seqlens_wide"]).then_inc(tables_in, 16)
            sp.dma_start(key_index[:, :], dram["key_index"]).then_inc(tables_in, 16)
            sp.wait_ge(packed_done, 5)

            def load_values(batch, buf):
                words = [None]
                for j in range(NPP):
                    page = page_of(sp, batch, j, words)
                    r = (j % 4) * PSIZE
                    sp.dma_start(v_in[r:r + PSIZE, buf, j // 4, :, :, :].rearrange("p l h d -> p (l h d)"),
                                 dram["v_split"][bass.ds(page * PSIZE, PSIZE), :, :].rearrange("p l n -> p (l n)")
                                 ).then_inc(v_loaded[buf], 16)

            def batch_io(batch, buf, more):
                if more:
                    sp.wait_ge(pv_done, batch * HK)
                    load_values(batch + 1, 1 - buf)
                for half in range(2):
                    sp.wait_ge(o_done, batch * HK + half * 4 + 4)
                    rows = dram["attn"][bass.ds(batch * S, S), :].rearrange("s (u h d) -> h s u d", h=REP, d=D)
                    for h in range(REP):
                        sp.dma_start(rows[h, :, half * 4:half * 4 + 4, :],
                                     o_stage[h * S:(h + 1) * S, half, :, :]).then_inc(o_stored[half], 16)

            load_values(0, 0)
            with sp.Fori(0, last_iter) as i:
                for k in range(2):
                    batch_io(i * 2 + k, k, True)
            for k in range(2):
                batch_io(last_iter * 2 + k, k, k == 0)
            for half in range(2):
                sp.wait_ge(o_stored[half], B * REP * 16)

        @block.gpsimd
        def _(pool):
            pool.wait_ge(packed_done, 5)

            def gather_pool(batch, buf):
                words = [None]
                for j in range(pool_pages):
                    ins = gather(pool, nc.gpsimd, batch, buf, j, words)
                ins.then_inc(keys_pool, 1)

            gather_pool(0, 0)
            gather_pool(1, 1)
            with pool.Fori(1, B // 2) as i:
                for k in range(2):
                    pool.wait_ge(scores_done, (i * 2 + k - 1) * HK)
                    pool.wait_ge(keys_pool, i * 2 + k)
                    gather_pool(i * 2 + k, k)

        @block.tensor
        def _(pe):
            def scores_of(i, s, u):
                buf, h = s // HK, s % HK
                if h == 0:
                    pe.wait_ge(q_loaded[buf], (i + 1) * 16)
                    pe.wait_ge(keys_pool, i * 2 + buf + 1)
                    pe.wait_ge(keys_dve, i * 2 + buf + 1)
                if not (isinstance(u, int) and u < 2):
                    pe.wait_ge(masked_done, u - 1)
                q_hi, q_lo = q_in[:, buf, h, 0, :], q_in[:, buf, h, 1, :]
                k_hi, k_lo = keys[:, buf, h, 0, :], keys[:, buf, h, 1, :]
                for n, (q, k) in enumerate(((q_hi, k_hi), (q_hi, k_lo), (q_lo, k_hi))):
                    for half in range(2):
                        last = nc.tensor.matmul(scores[s % 2][:, half, 0:HALF], q, k[:, half * HALF:(half + 1) * HALF],
                                                start=(n == 0), stop=(n == 2))
                last.then_inc(scores_done, 1)

            def turn(i, s, first):
                g = i * UNITS + s
                pe.wait_ge(exp_done, g + 1)
                if not (first and s < 1):
                    pe.wait_ge(lo_new, g)
                nc.tensor.transpose(pt_new[0:S, 0:P], probs[:, s % 2, L:KEYS], ident).then_inc(turned_new, 1)
                if not (first and s < 2):
                    pe.wait_ge(lo_old, g - 1)
                for t in range(4):
                    last = nc.tensor.transpose(pt_old[s % 2][:, t, :], probs[:, s % 2, t * P:(t + 1) * P], ident)
                last.then_inc(turned_old, 1)

            def pv(i, s, first):
                g, buf, h = i * UNITS + s, s // HK, s % HK
                if h == 0:
                    pe.wait_ge(v_loaded[buf], (i + 1) * NPP * 16)
                    pe.wait_ge(vn_loaded[buf], (i + 1) * 16)
                pe.wait_ge(lo_new, g + 1)
                pe.wait_ge(lo_old, g + 1)
                if not (first and s < 1):
                    pe.wait_ge(o_done, g)
                n = 0
                for t in range(5):
                    rows = S if t == 4 else P
                    v = vn_in[:, buf] if t == 4 else v_in[:, buf, t]
                    for p_part, l in ((pt_hi, 0), (pt_hi, 1), (pt_lo, 0)):
                        last = nc.tensor.matmul(o_acc[:, 0:D], p_part[0:rows, s % 2, t, :], v[0:rows, l, h, :],
                                                start=(n == 0), stop=(n == 14))
                        n += 1
                last.then_inc(pv_done, 1)

            def iteration(i, first=False, last=False):
                for s in range(UNITS):
                    if s + 2 < UNITS:
                        scores_of(i, s + 2, i * UNITS + s + 2)
                    elif not last:
                        scores_of(i + 1, s + 2 - UNITS, i * UNITS + s + 2)
                    turn(i, s, first)
                    if s >= 1:
                        pv(i, s - 1, first)
                    elif not first:
                        pv(i - 1, UNITS - 1, False)

            scores_of(0, 0, 0)
            scores_of(0, 1, 1)
            iteration(0, first=True)
            with pe.Fori(1, last_iter) as i:
                iteration(i)
            iteration(last_iter, last=True)
            pv(last_iter, UNITS - 1, False)

        @block.scalar
        def _(act):
            def load_batch(batch, buf):
                act.dma_start(q_in[:, buf, :, :, :].rearrange("p h l n -> p (h l n)"),
                              dram["q_t"][bass.ds(batch, 1), :, :, :].rearrange("o p h n -> (o p) (h n)")
                              ).then_inc(q_loaded[buf], 16)
                act.dma_start(kn_in[:, buf, :, :, :].rearrange("p h l s -> p (h l s)"),
                              dram["k_new"][bass.ds(batch, 1), :, :, :].rearrange("o p c n -> (o p) (c n)")
                              ).then_inc(kn_loaded[buf], 16)
                act.dma_start(vn_in[:, buf, :, :, :].rearrange("p l h d -> p (l h d)"),
                              dram["v_new"][bass.ds(batch * S, S), :, :].rearrange("p l n -> p (l n)")
                              ).then_inc(vn_loaded[buf], 16)

            def exp(i, s, u):
                act.wait_ge(bias_done, u + 1)
                nc.scalar.activation(probs[:, s % 2, :], masked[:, s % 2, :], ACT.Exp, bias=bias[:, s % 4:s % 4 + 1],
                                     scale=SCALE, accum_out=denom[:, s % 4:s % 4 + 1]).then_inc(exp_done, 1)

            def output(i, s, first):
                g, half = i * UNITS + s, s // 4 % 2
                act.wait_ge(pv_done, g + 1)
                act.wait_ge(rdenom_done, g + 1)
                if s % 4 == 0 and not (first and s < HK):
                    act.wait_ge(o_stored[half], (i * 2 + s // HK) * REP * 16)
                nc.scalar.activation(o_stage[:, half, s % 4, :], o_acc[:, 0:D], ACT.Copy,
                                     scale=rdenom[:, s % 4:s % 4 + 1]).then_inc(o_done, 1)

            def iteration(i, first=False, last=False):
                for s in range(UNITS):
                    g = i * UNITS + s
                    act.wait_ge(turned_new, g + 1)
                    if not (first and s < 2):
                        act.wait_ge(pv_done, g - 1)
                    nc.scalar.activation(pt_hi[0:S, s % 2, 4, :], pt_new[0:S, 0:P], ACT.Copy).then_inc(hi_new, 1)
                    act.wait_ge(turned_old, g + 1)
                    nc.scalar.activation(pt_hi[:, s % 2, 0:4, :], pt_old[s % 2][:, :, :], ACT.Copy).then_inc(hi_old, 1)
                    if s + 2 < UNITS or not last:
                        exp(i, s + 2, g + 2)
                    if s >= 1:
                        output(i, s - 1, first)
                    elif not first:
                        output(i - 1, UNITS - 1, False)
                    if s % HK == 2 and not (last and s > HK):
                        batch = i * 2 + s // HK
                        act.wait_ge(scores_done, batch * HK)
                        act.wait_ge(keys_dve, batch)
                        act.wait_ge(pv_done, batch * HK)
                        load_batch(batch + 1, 1 - s // HK)

            load_batch(0, 0)
            exp(0, 0, 0)
            exp(0, 1, 1)
            iteration(0, first=True)
            with act.Fori(1, last_iter) as i:
                iteration(i)
            iteration(last_iter, last=True)
            output(last_iter, UNITS - 1, False)

        @block.vector
        def _(dve):
            def mask_of(batch, buf):
                nc.vector.tensor_scalar(mask[:, buf, :], key_index[:, :], lens[:, bass.ds(batch, 1)], NEG,
                                        ALU.is_ge, ALU.mult).then_inc(mask_done, 1)

            def masked_max(i, s, u):
                buf = s // HK
                if s % HK == 0:
                    mask_of(i * 2 + buf, buf)
                    dve.wait_ge(mask_done, i * 2 + buf + 1)
                early = isinstance(u, int) and u < 2
                scores_needed, exps_needed = (u + 1, u - 1) if isinstance(u, int) else (dve.compute_val(u + 1), dve.compute_val(u - 1))
                dve.wait_ge(packed_done, 5)
                dve.wait_ge(scores_done, scores_needed)
                if not early:
                    dve.wait_ge(exp_done, exps_needed)
                nc.vector.tensor_tensor_reduce(
                    masked[:, s % 2, :].rearrange("p (a k) -> p a k", a=2), scores[s % 2][:, :, 0:HALF],
                    mask[:, buf, :].rearrange("p (a k) -> p a k", a=2), 1.0, 3.0 * NEG, ALU.add, ALU.max,
                    rowmax[:, s % 4:s % 4 + 1]).then_inc(masked_done, 1)
                dve.wait_ge(masked_done, u + 1)
                nc.vector.tensor_scalar(bias[:, s % 4:s % 4 + 1], rowmax[:, s % 4:s % 4 + 1], -SCALE, None,
                                        ALU.mult).then_inc(bias_done, 1)

            def copy_new_keys(batch, buf):
                nc.vector.tensor_copy(keys32[:, buf, :, :, NPP * W:], kn32[:, buf, :, :, :]).then_inc(keys_dve, 1)

            def iteration(i, first=False, last=False):
                words = [None]
                for s in range(UNITS):
                    g = i * UNITS + s
                    if s + 2 < UNITS:
                        masked_max(i, s + 2, g + 2)
                    elif not last:
                        masked_max(i + 1, s + 2 - UNITS, g + 2)
                    dve.wait_ge(exp_done, g + 1)
                    nc.vector.reciprocal(rdenom[:, s % 4:s % 4 + 1], denom[:, s % 4:s % 4 + 1]).then_inc(rdenom_done, 1)
                    dve.wait_ge(hi_new, g + 1)
                    nc.vector.tensor_tensor(pt_lo[0:S, s % 2, 4, :], pt_new[0:S, 0:P], pt_hi[0:S, s % 2, 4, :],
                                            ALU.subtract).then_inc(lo_new, 1)
                    dve.wait_ge(hi_old, g + 1)
                    nc.vector.tensor_tensor(pt_lo[:, s % 2, 0:4, :], pt_old[s % 2][:, :, :], pt_hi[:, s % 2, 0:4, :],
                                            ALU.subtract).then_inc(lo_old, 1)
                    buf, h = s // HK, s % HK
                    if 1 <= h <= 5 and not (last and buf == 1):
                        batch = i * 2 + buf
                        if h <= NPP - pool_pages:
                            if h == 1:
                                dve.wait_ge(scores_done, batch * HK)
                            gather(dve, nc.vector, batch + 1, 1 - buf, pool_pages + h - 1, words)
                        else:
                            dve.wait_ge(kn_loaded[1 - buf], (i + buf + 1) * 16)
                            copy_new_keys(batch + 1, 1 - buf)

            dve.wait_ge(tables_in, 48)
            nc.vector.tensor_copy(lens[:, :], lens_i[:, :]).then_inc(packed_done, 1)
            nc.vector.tensor_copy(pages_f[:, :, :], pages_i[:, :, :]).then_inc(packed_done, 1)
            dve.wait_ge(packed_done, 2)
            previous = pages_f[:, :, 3]
            for n in (2, 1, 0):
                out = packed if n == 0 else packed_f
                nc.vector.scalar_tensor_tensor(out=out[:, :], in0=previous, scalar=float(PAGES), in1=pages_f[:, :, n],
                                               op0=ALU.mult, op1=ALU.add).then_inc(packed_done, 1)
                previous = packed_f[:, :]
                dve.wait_ge(packed_done, 5 - n)
            words = [None]
            for j in range(pool_pages, NPP):
                gather(dve, nc.vector, 0, 0, j, words)
            dve.wait_ge(kn_loaded[0], 16)
            copy_new_keys(0, 0)
            masked_max(0, 0, 0)
            masked_max(0, 1, 1)
            iteration(0, first=True)
            with dve.Fori(1, last_iter) as i:
                iteration(i)
            iteration(last_iter, last=True)


def phase3(nc, dram, keep):
    const = keep["const"]
    ident = const[:, _cols["ident"]]
    groups = HQ // REP
    n_angle = 3 * S + 2 * S * KA + S * KB
    with ExitStack() as ctx:
        def sb(name, shape, dt):
            return ctx.enter_context(nc.sbuf_tensor("p3_" + name, shape, dt))

        def ps(name, shape):
            return ctx.enter_context(nc.psum_tensor("p3_" + name, shape, F32))

        def sem(name):
            return ctx.enter_context(nc.semaphore("p3_" + name))

        wo = sb("wo", [P, HQ, 2, HID], F16)
        x1_t = sb("x1_t", [P, KT, S, B], F32)
        keep_mask = sb("keep_mask", [P, KT, B], F32)
        a_in = sb("a_in", [P, 2, HQ, D], F32)
        x_in = sb("x_rows", [P, 2, HID], F32)
        at = sb("at", [P, 2, 2, REP, P], F16)
        x1_t_back = sb("x1_t_back", [P, KT, S, B], F32)
        x1 = sb("x1", [P, HID], F32)
        x1_back = sb("x1_back", [P, KT, P], F32)
        toep = sb("toep", [P, 8, LCONV], F32)
        z = sb("z", [P, 2, KT, 4, B], F32)
        len_i = sb("len_i", [P, B], I32)
        len_f = sb("len_f", [P, B], F32)
        s4 = sb("s4", [P, 5, S], F32)
        d_row = sb("d_row", [1, S], F32)
        conv_k = sb("conv_k_sb", [KA, S, KB], F32)
        zeros = sb("zeros", [S, P], F32)
        ang = sb("ang3", [P, n_angle], F32)
        turns = sb("turns3", [P, n_angle], F32)
        growth = sb("growth", [P, S * (KA + KB)], F32)
        par = sb("par", [P, 15, S], F32)
        turned = [ps(f"turned_a{i}", [P, REP, P]) for i in range(2)]
        y_acc = [ps(f"y_acc{i}", [P, HID]) for i in range(2)]
        x1_turned = [ps(f"x1_turned{i}", [P, KT, P]) for i in range(2)]
        k_acc = ps("k_acc", [P, 2, 512])

        params_in, wo_loaded = sem("params_in"), [sem(f"wo_loaded{i}") for i in range(4)]
        a_loaded = [sem("a_loaded0"), sem("a_loaded1")]
        step = sem("step")
        rates_done, angles_ready, growth_done, trig_done = (
            sem("rates_done"), sem("angles_ready"), sem("growth_done"), sem("trig_done"))
        factors_done, k_done, k_ready, k_stored = sem("factors_done"), sem("k_done"), sem("k_ready"), sem("k_stored")
        zeros_ready = sem("zeros_ready")
        turned_done, at_hi_done, at_lo_done, group_done = (
            sem("turned_done"), sem("at_hi_done"), sem("at_lo_done"), sem("group_done"))
        x1_done, x1_turned_done, x1_t_done = sem("x1_done"), sem("x1_turned_done"), sem("x1_t_done")
        x1_back_done = sem("x1_back_done")
        toep_loaded = [sem(f"toep_loaded{j}") for j in range(8)]
        conv_done, z_part, z_done = sem("conv_done"), sem("z_part"), sem("z_done")
        z_stored = [sem("z_stored0"), sem("z_stored1")]
        block = ctx.enter_context(nc.Block())

        n_cos, n_sin, n_b = S + S * KA, 2 * S + S * KA, S * KB
        cos_part, sin_part, b_part = slice(0, n_cos), slice(n_cos, n_cos + n_sin), slice(n_cos + n_sin, n_angle)

        def grid(tile, at, steps):
            return tile[:, at:at + S * steps].rearrange("p (h k) -> p h k", h=S)

        @block.sync
        def _(sp):
            sp.dma_start(s4[:, :, :], dram["s4d"]).then_inc(params_in, 16)
            sp.dma_start(d_row[:, :], dram["s4d_d"]).then_inc(params_in, 16)
            sp.dma_start(len_i[:, :], dram["lengths_wide"]).then_inc(params_in, 16)

            def load_tile(tile, buf):
                sp.dma_start(a_in[:, buf, :, :], dram["attn"][bass.ds(tile * P, P), :]
                             .rearrange("p (h d) -> p h d", h=HQ)).then_inc(a_loaded[buf], 16)
                sp.dma_start(x_in[:, buf, :], dram["x"][bass.ds(tile * P, P), :]).then_inc(a_loaded[buf], 16)

            load_tile(0, 0)
            for n in range(4):
                sp.dma_start(wo[:, n * 8:(n + 1) * 8, :, :], dram["wo_split"][:, n * 8:(n + 1) * 8, :, :]
                             ).then_inc(wo_loaded[n], 16)
            load_tile(1, 1)
            with sp.Fori(1, TILES // 2) as i:
                for buf in range(2):
                    sp.wait_ge(group_done, (i * 2 + buf - 1) * groups)
                    sp.wait_ge(x1_done, i * 2 + buf - 1)
                    load_tile(i * 2 + buf, buf)
            with sp.Fori(0, S // 8) as i:
                for par in range(2):
                    sp.wait_ge(z_done, i * 2 + par + 1)
                    sp.dma_start(dram["out"][:, :, bass.ds((i * 2 + par) * 4, 4), :].rearrange("i p s b -> p i s b"),
                                 z[:, par, :, :, :]).then_inc(z_stored[par], 16)
            for par in range(2):
                sp.wait_ge(z_stored[par], S // 8 * 16)

        @block.gpsimd
        def _(pool):
            nc.gpsimd.memset(zeros[:, :], 0.0).then_inc(zeros_ready, 1)
            pool.wait_ge(zeros_ready, 1)
            pool.wait_ge(k_ready, 2)
            pool.dma_start(dram["conv_k"][:, LCONV - P:LCONV], zeros[:, :]).then_inc(k_stored, 16)
            pool.dma_start(dram["conv_k"][:, LCONV:].rearrange("h (a b) -> a h b", b=KB), conv_k[:, :, :]).then_inc(k_stored, 16)
            pool.wait_ge(k_stored, 32)
            shifted = bass.AP(tensor=dram["conv_k"].tensor, offset=LCONV - (P - 1), ap=[[2 * LCONV, S], [1, P], [1, LCONV]])

            def load_toeplitz(s, j):
                pool.dma_start(toep[:, j, :], shifted[bass.ds(s, 1)].rearrange("o p n -> (o p) n")).then_inc(toep_loaded[j], 16)

            for j in range(8):
                load_toeplitz(j, j)
            backwards = bass.AP(tensor=x1[:, :].tensor, offset=P - 1, ap=[[HID, P], [P, KT], [-1, P]])
            with pool.Fori(1, TILES + 1) as done:
                pool.wait_ge(k_stored, 32)
                pool.wait_ge(x1_done, done)
                nc.gpsimd.tensor_copy(x1_back[:, :, :], backwards).then_inc(x1_back_done, 1)
            with pool.Fori(1, S // 8) as i:
                for j in range(8):
                    pool.wait_ge(conv_done, i * 2 - 1 + j // 4)
                    load_toeplitz(i * 8 + j, j)

        @block.scalar
        def _(act):
            act.wait_ge(params_in, 48)
            nc.scalar.activation(par[:, 0:2, :], s4[:, 0:2, :], ACT.Exp).then_inc(rates_done, 1)
            act.wait_ge(angles_ready, 1)
            nc.scalar.activation(par[:, 4, :], par[:, 2, :], ACT.Tanh, scale=0.5).then_inc(growth_done, 1)
            nc.scalar.activation(growth[:, :], growth[:, :], ACT.Exp).then_inc(growth_done, 1)
            act.wait_ge(angles_ready, 4)
            nc.scalar.activation(turns[:, :], ang[:, :], ACT.Sin).then_inc(trig_done, 1)

            def high(n, hg, early):
                act.wait_ge(turned_done, n + 1)
                if not early:
                    act.wait_ge(group_done, n - 1)
                nc.scalar.activation(at[:, hg % 2, 0, :, :], turned[hg % 2][:, :, :], ACT.Copy).then_inc(at_hi_done, 1)

            def spread(tile):
                act.wait_ge(x1_turned_done, tile + 1)
                for src, dst in zip(x1_turned, (x1_t, x1_t_back)):
                    nc.scalar.activation(dst[:, :, :, bass.ds(tile * BPT, BPT)].rearrange("p i s b -> p i b s"),
                                         src[:, :, :].rearrange("p i (b s) -> p i b s", b=BPT),
                                         ACT.Copy).then_inc(x1_t_done, 1)

            def iteration(i, first=False):
                for tt in range(2):
                    for hg in range(groups):
                        high((i * 2 + tt) * groups + hg, hg, first and tt == 0 and hg < 2)
                        if hg == 4 and not (first and tt == 0):
                            spread(i * 2 + tt - 1)

            iteration(0, first=True)
            with act.Fori(1, TILES // 2) as i:
                iteration(i)
            spread(TILES - 1)

        @block.vector
        def _(dve):
            count = [0]

            def chain(instruction):
                count[0] += 1
                instruction.then_inc(step, 1)
                dve.wait_ge(step, count[0])

            v, wide3 = nc.vector, lambda t, k: t.rearrange("p (h o) -> p h o", o=1).broadcast_to([P, S, k])
            dt, ar, wr, wi, th, g_re, g_im, n_re, n_im, ct_re, ct_im, tmp, inv, fx, fy = (par[:, k, :] for k in range(15))
            ai, cr, ci = s4[:, 2, :], s4[:, 3, :], s4[:, 4, :]
            dve.wait_ge(params_in, 48)
            chain(v.tensor_copy(len_f[:, :], len_i[:, :]))
            chain(v.tensor_tensor(keep_mask[:, :, :],
                                  const[:, _cols["hid_index"]].rearrange("p (i o) -> p i o", o=1).broadcast_to([P, KT, B]),
                                  len_f[:, :].rearrange("p (o b) -> p o b", o=1).broadcast_to([P, KT, B]), ALU.is_lt))
            dve.wait_ge(rates_done, 1)
            chain(v.tensor_scalar(ar, ar, -1.0, None, ALU.mult))
            chain(v.tensor_tensor(wr, ar, dt, ALU.mult))
            chain(v.tensor_tensor(wi, ai, dt, ALU.mult))
            steps_of = {k: const[:, _cols[k]].rearrange("p (o k) -> p o k", o=1).broadcast_to([P, S, n])
                        for k, n in (("a_step", KA), ("b_step", KB))}
            chain(v.tensor_tensor(grid(growth, 0, KA), wide3(wr, KA), steps_of["a_step"], ALU.mult))
            v.tensor_tensor(grid(growth, S * KA, KB), wide3(wr, KB), steps_of["b_step"], ALU.mult).then_inc(angles_ready, 1)
            chain(v.tensor_copy(ang[:, 0:S], wi))
            chain(v.tensor_copy(ang[:, n_cos:n_cos + S], wi))
            chain(v.tensor_scalar(ang[:, n_cos + S:n_cos + 2 * S], wi, 0.5, None, ALU.mult))
            chain(v.tensor_tensor(grid(ang, S, KA), wide3(wi, KA), steps_of["a_step"], ALU.mult))
            chain(v.tensor_copy(ang[:, n_cos + 2 * S:n_cos + n_sin], ang[:, S:n_cos]))
            chain(v.tensor_tensor(grid(ang, n_cos + n_sin, KB), wide3(wi, KB), steps_of["b_step"], ALU.mult))
            regions = ((cos_part, 0.25, 0.25 * TWO_PI), (sin_part, 0.0, 0.0),
                       (b_part, const[:, _cols["v_turn"]], const[:, _cols["v_angle"]]))
            for cols, quarter, _ in regions:
                chain(v.tensor_scalar(turns[:, cols], ang[:, cols], 1.0 / TWO_PI, quarter, ALU.mult, ALU.add))
            chain(v.tensor_scalar(turns[:, :], turns[:, :], MAGIC, MAGIC, ALU.add, ALU.subtract))
            for part in (PI2_HI, PI2_MID, PI2_LO):
                chain(v.scalar_tensor_tensor(out=ang[:, :], in0=turns[:, :], scalar=-part, in1=ang[:, :],
                                             op0=ALU.mult, op1=ALU.add))
            for cols, _, angle in regions:
                chain(v.tensor_scalar(ang[:, cols], ang[:, cols], angle, PI_SAFE, ALU.add, ALU.min))
                v.tensor_scalar(ang[:, cols], ang[:, cols], -PI_SAFE, None, ALU.max).then_inc(angles_ready, 1)
            dve.wait_ge(growth_done, 1)
            chain(v.tensor_scalar(tmp, th, -1.0, 1.0, ALU.mult, ALU.add))
            chain(v.reciprocal(inv, tmp))
            chain(v.scalar_tensor_tensor(out=th, in0=th, scalar=2.0, in1=inv, op0=ALU.mult, op1=ALU.mult))
            dve.wait_ge(trig_done, 1)
            cos_w, sin_w, sin_h = turns[:, 0:S], turns[:, n_cos:n_cos + S], turns[:, n_cos + S:n_cos + 2 * S]
            chain(v.tensor_tensor(tmp, sin_h, sin_h, ALU.mult))
            chain(v.tensor_tensor(g_re, th, cos_w, ALU.mult))
            chain(v.scalar_tensor_tensor(out=g_re, in0=tmp, scalar=-2.0, in1=g_re, op0=ALU.mult, op1=ALU.add))
            chain(v.scalar_tensor_tensor(out=g_im, in0=th, scalar=1.0, in1=sin_w, op0=ALU.add, op1=ALU.mult))
            chain(v.tensor_tensor(n_re, cr, g_re, ALU.mult))
            chain(v.tensor_tensor(tmp, ci, g_im, ALU.mult))
            chain(v.tensor_tensor(n_re, n_re, tmp, ALU.subtract))
            chain(v.tensor_tensor(n_im, cr, g_im, ALU.mult))
            chain(v.tensor_tensor(tmp, ci, g_re, ALU.mult))
            chain(v.tensor_tensor(n_im, n_im, tmp, ALU.add))
            chain(v.tensor_tensor(tmp, ar, ar, ALU.mult))
            chain(v.tensor_tensor(inv, ai, ai, ALU.mult))
            chain(v.tensor_tensor(tmp, tmp, inv, ALU.add))
            chain(v.reciprocal(inv, tmp))
            chain(v.tensor_tensor(ct_re, n_re, ar, ALU.mult))
            chain(v.tensor_tensor(tmp, n_im, ai, ALU.mult))
            chain(v.tensor_tensor(ct_re, ct_re, tmp, ALU.add))
            chain(v.tensor_tensor(ct_re, ct_re, inv, ALU.mult))
            chain(v.tensor_tensor(ct_im, n_im, ar, ALU.mult))
            chain(v.tensor_tensor(tmp, n_re, ai, ALU.mult))
            chain(v.tensor_tensor(ct_im, ct_im, tmp, ALU.subtract))
            chain(v.tensor_tensor(ct_im, ct_im, inv, ALU.mult))
            mix = _cols["mix"].start
            for out, one, two, m in ((fx, ct_re, ct_im, 0), (fy, ct_im, ct_re, 2)):
                chain(v.tensor_scalar(tmp, one, const[:, mix + m:mix + m + 1], None, ALU.mult))
                chain(v.scalar_tensor_tensor(out=out, in0=two, scalar=const[:, mix + m + 1:mix + m + 2], in1=tmp,
                                             op0=ALU.mult, op1=ALU.add))
            cos_a, sin_a = grid(turns, S, KA), grid(turns, n_cos + 2 * S, KA)
            chain(v.tensor_tensor(cos_a, cos_a, wide3(fx, KA), ALU.mult))
            chain(v.tensor_tensor(sin_a, sin_a, wide3(fy, KA), ALU.mult))
            chain(v.tensor_tensor(cos_a, cos_a, sin_a, ALU.add))
            dve.wait_ge(growth_done, 2)
            chain(v.tensor_tensor(grid(ang, 0, KA), cos_a, grid(growth, 0, KA), ALU.mult))
            v.tensor_tensor(grid(ang, S * KA, KB), grid(turns, n_cos + n_sin, KB), grid(growth, S * KA, KB),
                            ALU.mult).then_inc(factors_done, 1)
            dve.wait_ge(k_done, 1)
            v.tensor_copy(conv_k[:, :, :].rearrange("p h b -> p (h b)"),
                          k_acc[0:KA, :, :].rearrange("p a n -> p (a n)")).then_inc(k_ready, 1)
            dve.wait_ge(k_ready, 1)
            v.tensor_tensor(conv_k[0:1, :, 0], conv_k[0:1, :, 0], d_row[:, :], ALU.add).then_inc(k_ready, 1)

            def low(n, hg):
                dve.wait_ge(at_hi_done, n + 1)
                v.tensor_tensor(at[:, hg % 2, 1, :, :], turned[hg % 2][:, :, :], at[:, hg % 2, 0, :, :],
                                ALU.subtract).then_inc(at_lo_done, 1)

            def iteration(i, first=False):
                for tt in range(2):
                    for hg in range(groups):
                        low((i * 2 + tt) * groups + hg, hg)
                        if hg == 0 and not (first and tt == 0):
                            add_input(i - 1 + tt, i * 2 + tt - 1, 1 - tt)

            def add_input(pair, tile, buf):
                dve.wait_ge(group_done, (tile + 1) * groups)
                dve.wait_ge(a_loaded[buf], (pair + 1) * 32)
                dve.wait_ge(x1_turned_done, tile)
                v.scalar_tensor_tensor(out=x1[:, :], in0=y_acc[buf][:, :], scalar=1.0 / WSCALE, in1=x_in[:, buf, :],
                                       op0=ALU.mult, op1=ALU.add).then_inc(x1_done, 1)

            iteration(0, first=True)
            with dve.Fori(1, TILES // 2) as i:
                iteration(i)
            add_input(TILES // 2 - 1, TILES - 1, 1)
            dve.wait_ge(x1_t_done, TILES * 2)
            with dve.Fori(0, S // 8) as i:
                for par_z in range(2):
                    q = i * 2 + par_z
                    dve.wait_ge(conv_done, q + 1)
                    dve.wait_ge(z_stored[par_z], i * 16)
                    zq = z[:, par_z, :, :, :].rearrange("p i s b -> p s i b")
                    v.tensor_tensor(zq, k_acc[:, par_z, :].rearrange("p (s i b) -> p s i b", s=4, i=KT),
                                    keep_mask[:, :, :].rearrange("p (o i) b -> p o i b", o=1).broadcast_to([P, 4, KT, B]),
                                    ALU.mult).then_inc(z_part, 1)
                    dve.wait_ge(z_part, q + 1)
                    v.tensor_tensor(z[:, par_z, :, :, :], z[:, par_z, :, :, :], x1_t[:, :, bass.ds(q * 4, 4), :],
                                    ALU.add).then_inc(z_done, 1)

        @block.tensor
        def _(pe):
            pe.wait_ge(factors_done, 1)
            for h in range(S):
                last = nc.tensor.matmul(k_acc[0:KA, h // 16, h % 16 * KB:(h % 16 + 1) * KB],
                                        ang[:, h * KA:(h + 1) * KA], ang[:, S * KA + h * KB:S * KA + (h + 1) * KB],
                                        start=True, stop=True)
            last.then_inc(k_done, 1)

            def turn(i, n, tt, hg):
                if hg == 0:
                    pe.wait_ge(a_loaded[tt], (i + 1) * 32)
                if not (isinstance(n, int) and n == 0):
                    pe.wait_ge(at_lo_done, n - 1)
                for h in range(REP):
                    last = nc.tensor.transpose(turned[hg % 2][:, h, :], a_in[:, tt, hg * REP + h, :], ident)
                last.then_inc(turned_done, 1)

            def project(n, tt, hg):
                pe.wait_ge(at_lo_done, n + 1)
                for h in range(REP):
                    head = hg * REP + h
                    for k, (a, w) in enumerate(((0, 0), (0, 1), (1, 0))):
                        last = nc.tensor.matmul(y_acc[tt][:, :], at[:, hg % 2, a, h, :], wo[:, head, w, :],
                                                start=(head == 0 and k == 0), stop=(head == HQ - 1 and k == 2))
                last.then_inc(group_done, 1)

            def turn_x1(tile):
                pe.wait_ge(x1_done, tile + 1)
                pe.wait_ge(x1_t_done, tile * 2)
                for k in range(KT):
                    nc.tensor.transpose(x1_turned[0][:, k, :], x1[:, k * P:(k + 1) * P], ident)
                pe.wait_ge(x1_back_done, tile + 1)
                for k in range(KT):
                    last = nc.tensor.transpose(x1_turned[1][:, k, :], x1_back[:, k, :], ident)
                last.then_inc(x1_turned_done, 1)

            def iteration(i, first=False, final=False):
                for tt in range(2):
                    for hg in range(groups):
                        n = (i * 2 + tt) * groups + hg
                        if hg + 1 < groups:
                            turn(i, n + 1, tt, hg + 1)
                        elif not (final and tt == 1):
                            turn(i + tt, n + 1, 1 - tt, 0)
                        if hg == 2 and not (first and tt == 0):
                            turn_x1(i * 2 + tt - 1)
                        if first and tt == 0 and hg % 2 == 0:
                            pe.wait_ge(wo_loaded[hg // 2], 16)
                        if hg == 0 and not first:
                            pe.wait_ge(x1_done, i * 2 + tt - 1)
                        project(n, tt, hg)

            turn(0, 0, 0, 0)
            iteration(0, first=True)
            with pe.Fori(1, TILES // 2 - 1) as i:
                iteration(i)
            iteration(TILES // 2 - 1, final=True)
            turn_x1(TILES - 1)
            pe.wait_ge(x1_t_done, TILES * 2)
            with pe.Fori(0, S // 8) as i:
                for j in range(8):
                    pe.wait_ge(toep_loaded[j], (i + 1) * 16)
                    if j % 4 == 0:
                        pe.wait_ge(z_part, i * 2)
                    s = i * 8 + j
                    for d in range(KT):
                        base = j % 4 * KT * B
                        last = nc.tensor.matmul(
                            k_acc[:, j // 4, base + d * B:base + KT * B], toep[:, j, d * P:(d + 1) * P],
                            x1_t_back[:, 0:KT - d, bass.ds(s, 1), :].rearrange("p i o b -> p i (o b)"),
                            start=(d == 0), stop=(d == KT - 1))
                    if j % 4 == 3:
                        last.then_inc(conv_done, 1)


def build_program(nc, dram):
    keep = {}
    with ExitStack() as outer:
        def sb(stack, name, shape, dt):
            keep[name] = stack.enter_context(nc.sbuf_tensor(name, shape, dt))

        sb(outer, "const", [P, NCONST], F32)
        with ExitStack() as keys:
            sb(keys, "kt_all", [P, PAGES, HK, 2, PSIZE], F16)
            with ExitStack() as weights:
                sb(weights, "w_hi", [P, KT, E_ALL], F16)
                sb(weights, "w_lo", [P, KT, E_ALL], F16)
                sb(weights, "cos_t", [P, TILES, D // 2], F32)
                sb(weights, "sin_t", [P, TILES, D // 2], F32)
                sb(weights, "w_tab", [P, 4, D], F32)
                phase0(nc, dram, keep)
                phase1(nc, dram, keep)
            phase2(nc, dram, keep)
        phase3(nc, dram, keep)


def constants():
    c = np.zeros((P, NCONST), np.float32)
    p = np.arange(P)
    c[:, _cols["ident"]] = np.eye(P)
    c[:, _cols["token_in_batch"]] = (p % S)[:, None]
    c[:, _cols["inv_freq"]] = np.float32(1.0) / np.float32(10000.0) ** (np.arange(0, D, 2, dtype=np.float32) / np.float32(D))
    c[:, _cols["hid_index"]] = p[:, None] + P * np.arange(KT)
    c[:, _cols["a_step"]] = KB * np.arange(KA)
    c[:, _cols["b_step"]] = np.arange(KB)
    c[:, _cols["v_turn"]] = np.where(p < NSTATE, 0.25, 0.0)[:, None]
    c[:, _cols["v_angle"]] = c[:, _cols["v_turn"]] * np.float32(TWO_PI)
    top, low = (p < NSTATE)[:, None], (p >= NSTATE)[:, None]
    c[:, _cols["mix"]] = np.concatenate([2.0 * top, -2.0 * low, -2.0 * top, -2.0 * low], 1)
    return c


SCRATCH = {
    "q_t": ([B, P, HK, 2 * REP * S], F16),
    "k_new": ([B, P, HK * D // 512, 2 * REP * S], F16),
    "v_new": ([TOK, 2, HK * D], F16),
    "v_split": ([PAGES * PSIZE, 2, HK * D], F16),
    "wo_split": ([P, HQ, 2, HID], F16),
    "attn": ([TOK, HQ * D], F32),
    "conv_k": ([S, 2 * LCONV], F32),
}


def layout(x, itok_Bx16_0_63, itok_B_207_1644, itok_B_78_3631, L0_cond_Wq, L0_cond_Wk, L0_cond_Wv, L0_cond_Wo,
           L0_cond_q_norm_w, L0_cond_k_norm_w, L0_cond_k_cache, L0_cond_v_cache, L1_cond_log_dt, L1_cond_C,
           L1_cond_log_A_real, L1_cond_A_imag, L1_cond_D):
    a = np.asarray
    h = D // 2
    rows = a(x).reshape(TOK, HID)
    qw, kw = a(L0_cond_q_norm_w), a(L0_cond_k_norm_w)
    tab = np.stack([qw, np.concatenate([qw[h:], qw[:h]]), kw, np.concatenate([kw[h:], kw[:h]])])
    twice = lambda m: np.concatenate([a(m).T, a(m).T])
    wide = lambda v: np.broadcast_to(a(v), (P,) + a(v).shape)
    c = a(L1_cond_C)

    def padded(m, n, axis):
        return np.pad(m, [(0, n if k == axis else 0) for k in range(2)])

    arrays = {
        "x": rows,
        "xt": padded(rows.T, P, 1),
        "w_all": np.concatenate([a(L0_cond_Wq), a(L0_cond_Wk), a(L0_cond_Wv)]).T,
        "wo_t": padded(a(L0_cond_Wo).T, P, 0),
        "kt": padded(a(L0_cond_k_cache).transpose(3, 0, 2, 1).reshape(D, PAGES * HK * PSIZE), 512, 1),
        "v_cache": padded(a(L0_cond_v_cache).reshape(PAGES * PSIZE, HK * D), P, 0),
        "norm_w": wide(tab),
        "pages": a(itok_Bx16_0_63).reshape(1, B * NPP),
        "seqlens_by_token": np.repeat(a(itok_B_207_1644), S).reshape(TILES, P).T,
        "seqlens_wide": wide(itok_B_207_1644),
        "lengths_wide": wide(itok_B_78_3631),
        "s4d": np.stack([wide(L1_cond_log_dt), twice(L1_cond_log_A_real), twice(L1_cond_A_imag),
                         twice(c[:, :, 0]), twice(c[:, :, 1])], 1),
        "s4d_d": a(L1_cond_D).reshape(1, S),
        "consts": constants(),
        "key_index": wide(np.concatenate([np.arange(L), np.full(S, -1)]).astype(np.float32)),
    }
    return {k: np.ascontiguousarray(v) for k, v in arrays.items()}


def kernel(**inputs):
    from concourse import bacc
    from concourse.bass_utils import run_bass_kernel_spmd

    nc = bacc.Bacc("TRN2", target_bir_lowering=False, num_devices=1)
    arrays = layout(**inputs)
    dram = {n: nc.dram_tensor(n, list(v.shape), mybir.dt.from_np(v.dtype), kind="ExternalInput").ap()
            for n, v in arrays.items()}
    for n, (shape, dt) in SCRATCH.items():
        dram[n] = nc.dram_tensor(n, shape, dt, kind="Internal").ap()
    dram["out"] = nc.dram_tensor("out", [KT, P, S, B], F32, kind="ExternalOutput").ap()
    build_program(nc, dram)
    r = run_bass_kernel_spmd(nc, [arrays], core_ids=[0])
    out = r.results[0]["out"]
    return np.ascontiguousarray(out.transpose(3, 2, 0, 1).reshape(B, S, HID))
```

```python
from contextlib import ExitStack

import numpy as np

import concourse.bass as bass
from concourse import mybir

F32 = mybir.dt.float32
F16 = mybir.dt.float16
I32 = mybir.dt.int32
ALU = mybir.AluOpType
ACT = mybir.ActivationFunctionType
AX_X = mybir.AxisListType.X

P = 128
B, S, HID = 32, 32, 512
D, HQ, HK = 128, 32, 8
REP = HQ // HK
PAGES, PSIZE, NPP = 64, 32, 16
L = NPP * PSIZE
KEYS = L + S
HALF = KEYS // 2
TOK = B * S
TILES = TOK // P
BPT = P // S
KT = HID // P
E_ALL = (HQ + 2 * HK) * D
CHUNKS = E_ALL // 512
NORMED = (HQ + HK) * D // 512
QCH = HQ * D // 512
NPIECE = 4
UNITS = 2 * HK
NSTATE, LCONV = 64, HID
KA, KB = 16, 32
EPS = 1e-6
SCALE = 1.0 / float(np.sqrt(D))
WSCALE = 64.0
NEG = -1e30
MAGIC = 1.5 * 2.0 ** 23
TWO_PI = 6.283185307179586
PI2_HI = 6.28125
PI2_MID = float(np.float32(np.float16(TWO_PI - PI2_HI)))
PI2_LO = TWO_PI - PI2_HI - PI2_MID
PI_SAFE = 3.1415925
ROT_LAG, TURN_LAG = 2, 3

_cols, _at = {}, 0
for _name, _n in (("ident", P), ("token_in_batch", 1), ("inv_freq", D // 2),
                  ("hid_index", KT), ("a_step", KA), ("b_step", KB), ("v_turn", 1), ("v_angle", 1),
                  ("mix", 4)):
    _cols[_name] = slice(_at, _at + _n)
    _at += _n
NCONST = _at


def phase0(nc, dram, keep):
    const, w_hi, w_lo, cos_t, sin_t, w_tab = (
        keep[k] for k in ("const", "w_hi", "w_lo", "cos_t", "sin_t", "w_tab"))
    with ExitStack() as ctx:
        def sb(name, shape, dt):
            return ctx.enter_context(nc.sbuf_tensor("p0_" + name, shape, dt))

        def sem(name):
            return ctx.enter_context(nc.semaphore("p0_" + name))

        w_in = sb("w_in", [P, 3, KT, 512], F32)
        seq_i = sb("seq_i", [P, TILES], I32)
        pos = sb("pos", [P, TILES], F32)
        ang = sb("ang", [P, TILES, D // 2], F32)
        turns = sb("turns", [P, TILES, D // 2], F32)
        red_c = sb("red_c", [P, TILES, D // 2], F32)
        red_s = sb("red_s", [P, TILES, D // 2], F32)
        const_in, w_loaded = sem("const_in"), [sem(f"w_loaded{i}") for i in range(3)]
        w_hi_done, w_free = sem("w_hi_done"), sem("w_free")
        rope_step, angles_done, sincos_done = sem("rope_step"), sem("angles_done"), sem("sincos_done")
        block = ctx.enter_context(nc.Block())

        @block.sync
        def _(sp):
            sp.dma_start(const[:, :], dram["consts"]).then_inc(const_in, 16)
            sp.dma_start(seq_i[:, :], dram["seqlens_by_token"]).then_inc(const_in, 16)
            sp.dma_start(w_tab[:, :, :], dram["norm_w"]).then_inc(const_in, 16)
            w_src = dram["w_all"].rearrange("(i p) e -> p i e", p=P)
            with sp.Fori(0, CHUNKS // 3) as c3:
                for k in range(3):
                    sp.wait_ge(w_free, c3 * 3 + k + 1)
                    sp.dma_start(w_in[:, k, :, :],
                                 w_src[:, :, bass.ds((c3 * 3 + k) * 512, 512)]).then_inc(w_loaded[k], 16)

        @block.scalar
        def _(act):
            with act.Fori(0, CHUNKS // 3) as c3:
                for k in range(3):
                    act.wait_ge(w_loaded[k], c3 * 16 + 16)
                    nc.scalar.activation(w_hi[:, :, bass.ds((c3 * 3 + k) * 512, 512)], w_in[:, k, :, :],
                                         ACT.Copy, scale=WSCALE).then_inc(w_hi_done, 1)
            act.wait_ge(angles_done, 2)
            nc.scalar.activation(cos_t[:, :, :], red_c[:, :, :], ACT.Sin).then_inc(sincos_done, 1)
            nc.scalar.activation(sin_t[:, :, :], red_s[:, :, :], ACT.Sin).then_inc(sincos_done, 1)

        @block.vector
        def _(dve):
            nc.vector.memset(pos[:, :], 0.0).then_inc(w_free, 3)
            dve.wait_ge(w_free, 3)
            dve.wait_ge(const_in, 16 * 3)
            steps = [0]

            def stepped(instruction):
                steps[0] += 1
                instruction.then_inc(rope_step, 1)
                dve.wait_ge(rope_step, steps[0])

            stepped(nc.vector.tensor_copy(pos[:, :], seq_i[:, :]))
            stepped(nc.vector.tensor_scalar(pos[:, :], pos[:, :], const[:, _cols["token_in_batch"]], None, ALU.add))
            freq = const[:, _cols["inv_freq"]]
            stepped(nc.vector.tensor_tensor(
                ang[:, :, :], pos[:, :].rearrange("p (t o) -> p t o", o=1).broadcast_to([P, TILES, D // 2]),
                freq.rearrange("p (o f) -> p o f", o=1).broadcast_to([P, TILES, D // 2]), ALU.mult))
            for quarter, red in ((0.25, red_c), (0.0, red_s)):
                stepped(nc.vector.tensor_scalar(turns[:, :, :], ang[:, :, :], 1.0 / TWO_PI, quarter, ALU.mult, ALU.add))
                stepped(nc.vector.tensor_scalar(turns[:, :, :], turns[:, :, :], MAGIC, MAGIC, ALU.add, ALU.subtract))
                src = ang
                for part in (PI2_HI, PI2_MID, PI2_LO):
                    stepped(nc.vector.scalar_tensor_tensor(out=red[:, :, :], in0=turns[:, :, :], scalar=-part,
                                                           in1=src[:, :, :], op0=ALU.mult, op1=ALU.add))
                    src = red
                stepped(nc.vector.tensor_scalar(red[:, :, :], red[:, :, :], quarter * TWO_PI, PI_SAFE, ALU.add, ALU.min))
                nc.vector.tensor_scalar(red[:, :, :], red[:, :, :], -PI_SAFE, None, ALU.max).then_inc(angles_done, 1)
            for j in range(2):
                stepped(nc.vector.tensor_scalar(w_tab[:, 2 * j + 1, 0:D // 2], w_tab[:, 2 * j + 1, 0:D // 2],
                                                -1.0, None, ALU.mult))
            with dve.Fori(0, CHUNKS // 3) as c3:
                for k in range(3):
                    dve.wait_ge(w_hi_done, c3 * 3 + k + 1)
                    nc.vector.scalar_tensor_tensor(
                        out=w_lo[:, :, bass.ds((c3 * 3 + k) * 512, 512)], in0=w_in[:, k, :, :], scalar=WSCALE,
                        in1=w_hi[:, :, bass.ds((c3 * 3 + k) * 512, 512)], op0=ALU.mult,
                        op1=ALU.subtract).then_inc(w_free, 1)
            dve.wait_ge(w_free, CHUNKS + 3)
            dve.wait_ge(sincos_done, 2)


def phase1(nc, dram, keep):
    const, w_hi, w_lo, cos_t, sin_t, w_tab, kt_all = (
        keep[k] for k in ("const", "w_hi", "w_lo", "cos_t", "sin_t", "w_tab", "kt_all"))
    ident = const[:, _cols["ident"]]
    with ExitStack() as ctx:
        def sb(name, shape, dt):
            return ctx.enter_context(nc.sbuf_tensor("p1_" + name, shape, dt))

        def ps(name, shape):
            return ctx.enter_context(nc.psum_tensor("p1_" + name, shape, F32))

        def sem(name):
            return ctx.enter_context(nc.semaphore("p1_" + name))

        x_in = sb("x_in", [P, KT, P], F32)
        x_hi = sb("x_hi", [P, 2, KT, P], F16)
        x_lo = sb("x_lo", [P, 2, KT, P], F16)
        piece_in = sb("piece_in", [P, 3, 512], F32)
        piece_out = sb("piece_out", [P, 2, 2, 512], F16)
        eps_t = sb("eps_t", [P, 2], F32)
        sumsq = sb("sumsq", [P, 2, REP], F32)
        rms = sb("rms", [P, 2, REP], F32)
        rrms = sb("rrms", [P, 2, REP], F32)
        normed = sb("normed", [P, 2, REP, D], F32)
        rot_a = sb("rot_a", [P, 3, REP, D], F32)
        rot_b = sb("rot_b", [P, 2, REP, D], F32)
        tables = sb("tables", [P, 4, D], F32)
        v_stage = sb("v_stage", [P, 2, 2, 512], F16)
        stage = sb("stage", [P, 2, 1024], F16)
        proj = [ps(f"proj{i}", [P, 512]) for i in range(3)]
        squares = ps("squares", [P, REP, D])
        turned = [ps(f"turned{i}", [P, 512]) for i in range(2)]

        x_loaded, x_hi_done, x_lo_done = sem("x_loaded"), sem("x_hi_done"), sem("x_lo_done")
        piece_loaded = [sem(f"piece_loaded{i}") for i in range(3)]
        piece_hi_done, piece_free = sem("piece_hi_done"), sem("piece_free")
        piece_stored = [sem("piece_stored0"), sem("piece_stored1")]
        proj_done, proj_free = sem("proj_done"), sem("proj_free")
        squares_done, rms_done, rrms_done = sem("squares_done"), sem("rms_done"), sem("rrms_done")
        normed_done, rotated_parts, rotated, turned_done = (
            sem("normed_done"), sem("rotated_parts"), sem("rotated"), sem("turned_done"))
        table_done = sem("table_done")
        stage_hi_done, stage_lo_done, v_hi_done = sem("stage_hi_done"), sem("stage_lo_done"), sem("v_hi_done")
        stored = [sem(f"stored{i}") for i in range(2)]
        v_stored = [sem(f"v_stored{i}") for i in range(2)]
        block = ctx.enter_context(nc.Block())

        def k_piece(tile, c, part):
            pages = kt_all[:, bass.ds((tile * NPIECE + c // 3) * 2, 2), :, part, :]
            return pages

        def split_q(slot, part):
            return stage[:, slot, :].rearrange("p (b l h s) -> p l h b s", b=BPT, l=2, h=REP)[:, part]

        def split_k(slot, part):
            return stage[:, slot, :].rearrange("p (b h l s) -> p l h b s", b=BPT, h=REP, l=2)[:, part]

        @block.sync
        def _(sp):
            x_src = dram["xt"].rearrange("(i p) t -> p i t", p=P)
            v_src = dram["v_cache"].rearrange("(t p) (h e) -> p t h e", p=P, e=512)
            o_src = dram["wo_t"].rearrange("(h p) n -> p h n", p=P)

            def load_piece(tile, c):
                sp.wait_ge(piece_free, tile * CHUNKS + c + 1)
                nth = tile * NPIECE + c // 3
                if c % 3 == 0:
                    src = dram["kt"][:, bass.ds(nth * 512, 512)]
                elif c % 3 == 1:
                    src = v_src[:, bass.ds(tile * 2 + c // 6, 1), (c // 3) % 2, :]
                else:
                    src = o_src[:, bass.ds(nth, 1), :]
                sp.dma_start(piece_in[:, c % 3, :], src).then_inc(piece_loaded[c % 3], 16)

            def store_chunk(tile, j):
                needed = sp.compute_val(tile * NORMED + j + 1)
                if j >= QCH:
                    sp.wait_ge(piece_free, 3)
                sp.wait_ge(stage_lo_done, needed)
                dst = dram["q_t"][bass.ds(tile * BPT, BPT), :, j, :] if j < QCH else \
                    dram["k_new"][bass.ds(tile * BPT, BPT), :, j - QCH, :]
                sp.dma_start(dst.rearrange("b p n -> p b n"),
                             stage[:, j % 2, :].rearrange("p (b n) -> p b n", b=BPT)).then_inc(stored[j % 2], 16)

            def store_v(tile, half):
                sp.wait_ge(proj_free, tile * CHUNKS + NORMED + half + 4)
                sp.dma_start(dram["v_new"][bass.ds(tile * P, P), :, half * 512:(half + 1) * 512],
                             v_stage[:, half, :, :]).then_inc(v_stored[half], 16)

            def store_piece(tile, c):
                sp.wait_ge(piece_free, tile * CHUNKS + c + 4)
                if c % 3 == 1:
                    half = (c // 3) % 2
                    dst = dram["v_split"][bass.ds((tile * 2 + c // 6) * P, P), :, half * 512:(half + 1) * 512]
                else:
                    dst = dram["wo_split"][:, bass.ds(tile * NPIECE + c // 3, 1), :, :].rearrange("p o l n -> p (o l) n")
                sp.dma_start(dst, piece_out[:, c % 3 - 1, :, :]).then_inc(piece_stored[c % 3 - 1], 16)

            sp.dma_start(x_in[:, :, :], x_src[:, :, 0:P]).then_inc(x_loaded, 16)
            for c in range(3):
                load_piece(0, c)
            with sp.Fori(0, TILES // 2) as i2:
                for tt in range(2):
                    tile = i2 * 2 + tt
                    for c in range(CHUNKS + 1):
                        if c >= TURN_LAG:
                            store_chunk(tile, c - TURN_LAG)
                        if c > NORMED:
                            store_v(tile, c - NORMED - 1)
                        if c == CHUNKS:
                            break
                        load_piece(tile + (c + 3) // CHUNKS, (c + 3) % CHUNKS)
                        if c % 3:
                            store_piece(tile, c)
                        if c == 1:
                            sp.wait_ge(x_lo_done, tile + 1)
                            sp.dma_start(x_in[:, :, :], x_src[:, :, bass.ds((tile + 1) * P, P)]).then_inc(x_loaded, 16)
            for slot in range(2):
                sp.wait_ge(stored[slot], TILES * (NORMED // 2) * 16)
                sp.wait_ge(piece_stored[slot], TILES * NPIECE * 16)
                sp.wait_ge(v_stored[slot], TILES * 16)
            for slot in range(3):
                sp.wait_ge(piece_loaded[slot], (TILES * NPIECE + 1) * 16)
            sp.wait_ge(x_loaded, (TILES + 1) * 16)

        @block.tensor
        def _(pe):
            with pe.Fori(0, TILES // 2) as i2:
                for tt in range(2):
                    tile = i2 * 2 + tt
                    pe.wait_ge(x_lo_done, tile + 1)
                    for c in range(CHUNKS + 1):
                        if c >= TURN_LAG:
                            j = c - TURN_LAG
                            pe.wait_ge(rotated, tile * NORMED + j + 1)
                            pe.wait_ge(stage_lo_done, tile * NORMED + max(j - 1, 0))
                            for h in range(REP):
                                last = nc.tensor.transpose(turned[j % 2][:, h * P:(h + 1) * P],
                                                           rot_a[:, j % 3, h, :], ident)
                            last.then_inc(turned_done, 1)
                        if c == CHUNKS:
                            break
                        pe.wait_ge(proj_free, tile * CHUNKS + c + 1)
                        n = 0
                        for k in range(KT):
                            for x_part, w_part in ((x_hi, w_hi), (x_hi, w_lo), (x_lo, w_hi)):
                                last = nc.tensor.matmul(proj[c % 3][:, :], x_part[:, tt, k, :],
                                                        w_part[:, k, c * 512:(c + 1) * 512],
                                                        start=(n == 0), stop=(n == 3 * KT - 1))
                                n += 1
                        last.then_inc(proj_done, 1)

        @block.scalar
        def _(act):
            act.wait_ge(proj_free, 3)
            act.wait_ge(x_loaded, 16)
            nc.scalar.activation(x_hi[:, 0, :, :], x_in[:, :, :], ACT.Copy).then_inc(x_hi_done, 1)
            with act.Fori(0, TILES // 2) as i2:
                for tt in range(2):
                    tile = i2 * 2 + tt

                    for c in range(CHUNKS + 1):
                        if c >= TURN_LAG:
                            j = c - TURN_LAG
                            act.wait_ge(turned_done, tile * NORMED + j + 1)
                            act.wait_ge(stored[j % 2], (tile * (NORMED // 2) + j // 2) * 16)
                            split = split_q if j < QCH else split_k
                            nc.scalar.activation(split(j % 2, 0),
                                                 turned[j % 2][:, :].rearrange("p (h b s) -> p h b s", h=REP, b=BPT),
                                                 ACT.Copy).then_inc(stage_hi_done, 1)
                        if c == CHUNKS:
                            break
                        slot, nth = c % 3, tile * NPIECE + c // 3
                        act.wait_ge(piece_loaded[slot], (nth + 1) * 16)
                        if slot == 0:
                            nc.scalar.activation(k_piece(tile, c, 0),
                                                 piece_in[:, slot, :].rearrange("p (g h s) -> p g h s", g=2, h=HK),
                                                 ACT.Copy).then_inc(piece_hi_done, 1)
                        else:
                            act.wait_ge(piece_stored[slot - 1], nth * 16)
                            nc.scalar.activation(piece_out[:, slot - 1, 0, :], piece_in[:, slot, :], ACT.Copy,
                                                 scale=WSCALE if slot == 2 else 1.0).then_inc(piece_hi_done, 1)
                        act.wait_ge(proj_done, tile * CHUNKS + c + 1)
                        if c < NORMED:
                            n = tile * NORMED + c
                            act.wait_ge(squares_done, n * REP)
                            for h in range(REP):
                                nc.scalar.activation(squares[:, h, :], proj[c % 3][:, h * D:(h + 1) * D], ACT.Square,
                                                     accum_out=sumsq[:, c % 2, h:h + 1]).then_inc(squares_done, 1)
                            act.wait_ge(squares_done, (n + 1) * REP)
                            act.wait_ge(rrms_done, tile * NORMED + max(c - 1, 0))
                            nc.scalar.activation(rms[:, c % 2, :], sumsq[:, c % 2, :], ACT.Sqrt,
                                                 bias=eps_t[:, 0:1], scale=1.0 / D).then_inc(rms_done, 1)
                        else:
                            act.wait_ge(v_stored[c - NORMED], tile * 16)
                            nc.scalar.activation(v_stage[:, c - NORMED, 0, :], proj[c % 3][:, :], ACT.Copy,
                                                 scale=1.0 / WSCALE).then_inc(v_hi_done, 1)
                        if c == 5:
                            act.wait_ge(x_loaded, (tile + 2) * 16)
                            act.wait_ge(proj_done, tile * CHUNKS)
                            nc.scalar.activation(x_hi[:, 1 - tt, :, :], x_in[:, :, :], ACT.Copy).then_inc(x_hi_done, 1)

        @block.vector
        def _(dve):
            nc.vector.memset(eps_t[:, 0:1], EPS * WSCALE * WSCALE).then_inc(proj_free, 3)
            nc.vector.memset(eps_t[:, 1:2], 0.0).then_inc(piece_free, 3)
            dve.wait_ge(x_hi_done, 1)
            nc.vector.tensor_tensor(x_lo[:, 0, :, :], x_in[:, :, :], x_hi[:, 0, :, :], ALU.subtract).then_inc(x_lo_done, 1)
            with dve.Fori(0, TILES // 2) as i2:
                for tt in range(2):
                    tile = i2 * 2 + tt
                    for c in range(CHUNKS + 1):
                        if c >= TURN_LAG:
                            j = c - TURN_LAG
                            split = split_q if j < QCH else split_k
                            dve.wait_ge(stage_hi_done, tile * NORMED + j + 1)
                            nc.vector.tensor_tensor(split(j % 2, 1),
                                                    turned[j % 2][:, :].rearrange("p (h b s) -> p h b s", h=REP, b=BPT),
                                                    split(j % 2, 0), ALU.subtract).then_inc(stage_lo_done, 1)
                        if c == CHUNKS:
                            break
                        if ROT_LAG <= c < NORMED + ROT_LAG:
                            j = c - ROT_LAG
                            dve.wait_ge(rotated_parts, (tile * NORMED + j + 1) * 2)
                            nc.vector.tensor_tensor(rot_a[:, j % 3, :, :], rot_a[:, j % 3, :, :],
                                                    rot_b[:, j % 2, :, :], ALU.add).then_inc(rotated, 1)
                        if c < NORMED:
                            n = tile * NORMED + c
                            dve.wait_ge(rms_done, n + 1)
                            nc.vector.reciprocal(rrms[:, c % 2, :], rms[:, c % 2, :]).then_inc(rrms_done, 1)
                            dve.wait_ge(rrms_done, n + 1)
                            nc.vector.tensor_tensor(
                                normed[:, c % 2, :, :], proj[c % 3][:, :].rearrange("p (h d) -> p h d", h=REP),
                                rrms[:, c % 2, :].rearrange("p (h o) -> p h o", o=1).broadcast_to([P, REP, D]),
                                ALU.mult).then_inc(proj_free, 1)
                        else:
                            dve.wait_ge(v_hi_done, tile * (CHUNKS - NORMED) + c - NORMED + 1)
                            nc.vector.scalar_tensor_tensor(out=v_stage[:, c - NORMED, 1, :], in0=proj[c % 3][:, :],
                                                           scalar=1.0 / WSCALE, in1=v_stage[:, c - NORMED, 0, :],
                                                           op0=ALU.mult, op1=ALU.subtract).then_inc(proj_free, 1)
                        if c % 3 != 1:
                            dve.wait_ge(piece_hi_done, tile * CHUNKS + c + 1)
                            dve.wait_ge(piece_free, tile * CHUNKS + c + 3)
                            if c % 3 == 0:
                                nc.vector.tensor_tensor(k_piece(tile, c, 1),
                                                        piece_in[:, 0, :].rearrange("p (g h s) -> p g h s", g=2, h=HK),
                                                        k_piece(tile, c, 0), ALU.subtract).then_inc(piece_free, 1)
                            else:
                                nc.vector.scalar_tensor_tensor(out=piece_out[:, 1, 1, :], in0=piece_in[:, 2, :],
                                                               scalar=WSCALE, in1=piece_out[:, 1, 0, :],
                                                               op0=ALU.mult, op1=ALU.subtract).then_inc(piece_free, 1)
                        if c == 5:
                            dve.wait_ge(x_hi_done, tile + 2)
                            nc.vector.tensor_tensor(x_lo[:, 1 - tt, :, :], x_in[:, :, :], x_hi[:, 1 - tt, :, :],
                                                    ALU.subtract).then_inc(x_lo_done, 1)

        @block.gpsimd
        def _(pool):
            with pool.Fori(0, TILES // 2) as i2:
                for tt in range(2):
                    tile = i2 * 2 + tt
                    pool.wait_ge(rotated_parts, tile * NORMED * 2)
                    for j, trig in enumerate((cos_t, sin_t, cos_t, sin_t)):
                        nc.gpsimd.tensor_tensor(
                            tables[:, j, :].rearrange("p (a f) -> p a f", a=2),
                            trig[:, bass.ds(tile, 1), :].broadcast_to([P, 2, D // 2]),
                            w_tab[:, j, :].rearrange("p (a f) -> p a f", a=2), ALU.mult).then_inc(table_done, 1)
                    pool.wait_ge(table_done, (tile + 1) * 4)
                    for c in range(CHUNKS):
                        if c % 3 == 1:
                            pool.wait_ge(piece_hi_done, tile * CHUNKS + c + 1)
                            pool.wait_ge(piece_free, tile * CHUNKS + c + 3)
                            nc.gpsimd.tensor_tensor(piece_out[:, 0, 1, :], piece_in[:, 1, :],
                                                    piece_out[:, 0, 0, :], ALU.subtract).then_inc(piece_free, 1)
                        if c < NORMED:
                            pool.wait_ge(proj_free, tile * CHUNKS + c + 4)
                            pool.wait_ge(turned_done, tile * NORMED + max(c - 2, 0))
                            kind, half = 0 if c < QCH else 2, D // 2
                            cos_b, sin_b = (tables[:, kind + k, :].rearrange("p (o d) -> p o d", o=1)
                                            .broadcast_to([P, REP, D]) for k in range(2))
                            nc.gpsimd.tensor_tensor(rot_a[:, c % 3, :, :], normed[:, c % 2, :, :], cos_b,
                                                    ALU.mult).then_inc(rotated_parts, 1)
                            for k in range(2):
                                ins = nc.gpsimd.tensor_tensor(rot_b[:, c % 2, :, k * half:(k + 1) * half],
                                                              normed[:, c % 2, :, (1 - k) * half:(2 - k) * half],
                                                              sin_b[:, :, k * half:(k + 1) * half], ALU.mult)
                            ins.then_inc(rotated_parts, 1)


def phase2(nc, dram, keep):
    const, kt_all = keep["const"], keep["kt_all"]
    ident = const[:, _cols["ident"]]
    pool_pages = 12
    last_iter = B // 2 - 1
    with ExitStack() as ctx:
        def sb(name, shape, dt):
            return ctx.enter_context(nc.sbuf_tensor("p2_" + name, shape, dt))

        def ps(name, shape):
            return ctx.enter_context(nc.psum_tensor("p2_" + name, shape, F32))

        def sem(name):
            return ctx.enter_context(nc.semaphore("p2_" + name))

        key_index = sb("key_index", [P, KEYS], F32)
        lens_i = sb("lens_i", [P, B], I32)
        lens = sb("lens", [P, B], F32)
        batch_len = sb("batch_len", [P, 2], F32)
        pages_i = sb("pages_i", [1, B * NPP // 4, 4], I32)
        pages_f = sb("pages_f", [1, B * NPP // 4, 4], F32)
        packed_f = sb("packed_f", [1, B * NPP // 4], F32)
        packed = sb("packed", [1, B * NPP // 4], I32)
        q_in = sb("q_in", [P, 2, HK, 2, P], F16)
        kn_in = sb("kn_in", [P, 2, HK, 2, S], F16)
        keys = sb("keys", [P, 2, HK, 2, KEYS], F16)
        v_in = sb("v_in", [P, 2, KT, 2, HK, D], F16)
        vn_in = sb("vn_in", [3 * S, 2, HK, D], F16)
        mask = sb("mask", [P, 2, KEYS], F32)
        masked = sb("masked", [P, 2, KEYS], F32)
        rowmax = sb("rowmax", [P, 4], F32)
        bias = sb("bias", [P, 4], F32)
        denom = sb("denom", [P, 4], F32)
        rdenom = sb("rdenom", [P, 4], F32)
        probs = sb("probs", [P, 2, KEYS], F32)
        pt_hi = sb("pt_hi", [P, 2, 4, P], F16)
        pt_lo = sb("pt_lo", [P, 2, 4, P], F16)
        three = sb("three", [P, 2, 3, S], F16)
        ident16 = sb("ident16", [P, P], F16)
        pt_three = sb("pt_three", [3 * S, 2, P], F16)
        o_stage = sb("o_stage", [P, 2, 4, D], F32)
        scores = [ps(f"scores{i}", [P, 2, 512]) for i in range(2)]
        pt_old = [ps(f"pt_old{i}", [P, 4, P]) for i in range(2)]
        pt_new = ctx.enter_context(nc.psum_tensor("p2_pt_new", [P, 1024], F16))
        o_acc = ps("o_acc", [P, 512])
        kt32 = kt_all[:, :, :, :, :].bitcast(F32)
        keys32 = keys[:, :, :, :, :].bitcast(F32)
        kn32 = kn_in[:, :, :, :, :].bitcast(F32)
        W = PSIZE // 2

        tables_in, packed_done = sem("tables_in"), sem("packed_done")
        q_loaded = [sem("q_loaded0"), sem("q_loaded1")]
        kn_loaded = [sem("kn_loaded0"), sem("kn_loaded1")]
        vn_loaded = [sem("vn_loaded0"), sem("vn_loaded1")]
        v_loaded = [sem("v_loaded0"), sem("v_loaded1")]
        keys_pool, keys_dve = sem("keys_pool"), sem("keys_dve")
        scores_done, masked_done, bias_done = sem("scores_done"), sem("masked_done"), sem("bias_done")
        len_done = sem("len_done")
        mask_done, rdenom_done, exp_done = sem("mask_done"), sem("rdenom_done"), sem("exp_done")
        turned_new, turned_old = sem("turned_new"), sem("turned_old")
        three_high, three_done, new_copied, hi_old, lo_old = (
            sem("three_high"), sem("three_done"), sem("new_copied"), sem("hi_old"), sem("lo_old"))
        pv_done, o_done = sem("pv_done"), sem("o_done")
        o_stored = [sem("o_stored0"), sem("o_stored1")]
        block = ctx.enter_context(nc.Block())

        def computed(eng, value):
            return value if isinstance(value, int) else eng.compute_val(value)

        def page_of(eng, batch, j, words):
            if j % 4 == 0:
                words[0] = eng.value_load(packed[0:1, bass.ds(batch * (NPP // 4) + j // 4, 1)],
                                          min_val=0, max_val=PAGES ** 4 - 1)
            return (words[0] >> (6 * (j % 4))) & (PAGES - 1)

        def gather(eng, ops, batch, buf, j, words):
            page = page_of(eng, batch, j, words)
            src = kt32[:, bass.ds(page, 1), :, :, :].rearrange("p o h l w -> p (o h) l w")
            return ops.tensor_copy(keys32[:, buf, :, :, j * W:(j + 1) * W], src)

        @block.sync
        def _(sp):
            sp.dma_start(pages_i[:, :, :], dram["pages"].rearrange("a (b c) -> a b c", c=4)).then_inc(tables_in, 16)
            sp.dma_start(lens_i[:, :], dram["seqlens_wide"]).then_inc(tables_in, 16)
            sp.dma_start(key_index[:, :], dram["key_index"]).then_inc(tables_in, 16)
            sp.wait_ge(packed_done, 5)

            def load_new_keys(batch, buf):
                sp.dma_start(kn_in[:, buf, :, :, :].rearrange("p h l s -> p (h l s)"),
                             dram["k_new"][bass.ds(batch, 1), :, :, :].rearrange("o p c n -> (o p) (c n)")
                             ).then_inc(kn_loaded[buf], 16)

            def load_values(batch, buf):
                words = [None]
                for j in range(NPP):
                    page = page_of(sp, batch, j, words)
                    r = (j % 4) * PSIZE
                    sp.dma_start(v_in[r:r + PSIZE, buf, j // 4, :, :, :].rearrange("p l h d -> p (l h d)"),
                                 dram["v_split"][bass.ds(page * PSIZE, PSIZE), :, :].rearrange("p l n -> p (l n)")
                                 ).then_inc(v_loaded[buf], 16)

            def batch_io(batch, buf, more):
                if more:
                    if not (isinstance(batch, int) and batch == 0):
                        copies_needed, units_needed = computed(sp, batch), computed(sp, batch * HK)
                        sp.wait_ge(packed_done, 5)
                        sp.wait_ge(keys_dve, copies_needed)
                        sp.wait_ge(pv_done, units_needed)
                    load_new_keys(batch + 1, 1 - buf)
                    load_values(batch + 1, 1 - buf)
                for half in range(2):
                    sp.wait_ge(o_done, batch * HK + half * 4 + 4)
                    sp.dma_start(dram["attn"][bass.ds(batch * P, P), half * 4 * D:(half + 1) * 4 * D],
                                 o_stage[:, half, :, :].rearrange("p u d -> p (u d)")).then_inc(o_stored[half], 16)

            load_new_keys(0, 0)
            load_values(0, 0)
            for k in range(2):
                batch_io(k, k, True)
            with sp.Fori(1, last_iter) as i:
                for k in range(2):
                    batch_io(i * 2 + k, k, True)
            for k in range(2):
                batch_io(last_iter * 2 + k, k, k == 0)
            for half in range(2):
                sp.wait_ge(o_stored[half], B * 16)

        @block.gpsimd
        def _(pool):
            pool.wait_ge(packed_done, 5)

            def gather_pool(batch, buf):
                words = [None]
                for j in range(pool_pages):
                    ins = gather(pool, nc.gpsimd, batch, buf, j, words)
                ins.then_inc(keys_pool, 1)

            def mask_of(batch, buf):
                nc.gpsimd.tensor_copy(batch_len[:, buf:buf + 1], lens[:, bass.ds(batch, 1)]).then_inc(len_done, 1)
                lens_needed = computed(pool, batch + 1)
                pool.wait_ge(packed_done, 5)
                pool.wait_ge(len_done, lens_needed)
                nc.gpsimd.tensor_scalar(mask[:, buf, :], key_index[:, :], batch_len[:, buf:buf + 1], NEG,
                                        ALU.is_ge, ALU.mult).then_inc(mask_done, 1)

            mask_of(0, 0)
            gather_pool(1, 1)
            mask_of(1, 1)
            with pool.Fori(1, B // 2) as i:
                for k in range(2):
                    pool.wait_ge(scores_done, (i * 2 + k - 1) * HK)
                    pool.wait_ge(keys_pool, i * 2 + k - 1)
                    gather_pool(i * 2 + k, k)
                    pool.wait_ge(masked_done, (i * 2 + k - 1) * HK)
                    pool.wait_ge(mask_done, i * 2 + k)
                    mask_of(i * 2 + k, k)

        @block.tensor
        def _(pe):
            def scores_of(i, s, u):
                buf, h = s // HK, s % HK
                if h == 0:
                    pe.wait_ge(q_loaded[buf], (i + 1) * 16)
                    if not (isinstance(i, int) and i * 2 + buf == 0):
                        pe.wait_ge(keys_pool, i * 2 + buf)
                    pe.wait_ge(keys_dve, i * 2 + buf + 1)
                if not (isinstance(u, int) and u < 2):
                    pe.wait_ge(masked_done, u - 1)
                q_hi, q_lo = q_in[:, buf, h, 0, :], q_in[:, buf, h, 1, :]
                k_hi, k_lo = keys[:, buf, h, 0, :], keys[:, buf, h, 1, :]
                for n, (q, k) in enumerate(((q_hi, k_hi), (q_hi, k_lo), (q_lo, k_hi))):
                    for half in range(2):
                        last = nc.tensor.matmul(scores[s % 2][:, half, 0:HALF], q, k[:, half * HALF:(half + 1) * HALF],
                                                start=(n == 0), stop=(n == 2))
                last.then_inc(scores_done, 1)

            def turn(i, s, first):
                g = i * UNITS + s
                pe.wait_ge(three_done, g + 1)
                if not (first and s < 1):
                    pe.wait_ge(new_copied, g)
                nc.tensor.transpose(pt_new[0:3 * S, 0:P], three[:, s % 2, :, :].rearrange("p a k -> p (a k)"), ident16[:, :]).then_inc(turned_new, 1)
                pe.wait_ge(exp_done, g + 1)
                if not (first and s < 2):
                    pe.wait_ge(lo_old, g - 1)
                for t in range(4):
                    last = nc.tensor.transpose(pt_old[s % 2][:, t, :], probs[:, s % 2, t * P:(t + 1) * P], ident)
                last.then_inc(turned_old, 1)

            def pv(i, s, first):
                g, buf, h = i * UNITS + s, s // HK, s % HK
                if h == 0:
                    pe.wait_ge(v_loaded[buf], (i + 1) * NPP * 16)
                    pe.wait_ge(vn_loaded[buf], (i + 1) * 48)
                pe.wait_ge(new_copied, g + 1)
                pe.wait_ge(lo_old, g + 1)
                if not (first and s < 1):
                    pe.wait_ge(o_done, g)
                for t in range(4):
                    for p_part, l in ((pt_hi, 0), (pt_hi, 1), (pt_lo, 0)):
                        nc.tensor.matmul(o_acc[:, 0:D], p_part[:, s % 2, t, :], v_in[:, buf, t, l, h, :],
                                         start=(t == 0 and p_part is pt_hi and l == 0), stop=False)
                last = nc.tensor.matmul(o_acc[:, 0:D], pt_three[:, s % 2, :], vn_in[:, buf, h, :], start=False, stop=True)
                last.then_inc(pv_done, 1)

            def iteration(i, first=False, last=False):
                for s in range(UNITS):
                    if s + 2 < UNITS:
                        scores_of(i, s + 2, i * UNITS + s + 2)
                    elif not last:
                        scores_of(i + 1, s + 2 - UNITS, i * UNITS + s + 2)
                    turn(i, s, first)
                    if s >= 1:
                        pv(i, s - 1, first)
                    elif not first:
                        pv(i - 1, UNITS - 1, False)

            scores_of(0, 0, 0)
            scores_of(0, 1, 1)
            iteration(0, first=True)
            with pe.Fori(1, last_iter) as i:
                iteration(i)
            iteration(last_iter, last=True)
            pv(last_iter, UNITS - 1, False)

        @block.scalar
        def _(act):
            def load_queries(batch, buf):
                act.dma_start(q_in[:, buf, :, :, :].rearrange("p h l n -> p (h l n)"),
                              dram["q_t"][bass.ds(batch, 1), :, :, :].rearrange("o p h n -> (o p) (h n)")
                              ).then_inc(q_loaded[buf], 16)

            def load_new_values(batch, buf, part):
                act.dma_start(vn_in[part * S:(part + 1) * S, buf, :, :].rearrange("p h d -> p (h d)"),
                              dram["v_new"][bass.ds(batch * S, S), part // 2, :]).then_inc(vn_loaded[buf], 16)

            def exp(i, s, u):
                act.wait_ge(bias_done, u + 1)
                nc.scalar.activation(probs[:, s % 2, :], masked[:, s % 2, :], ACT.Exp, bias=bias[:, s % 4:s % 4 + 1],
                                     scale=SCALE, accum_out=denom[:, s % 4:s % 4 + 1]).then_inc(exp_done, 1)

            def three_highs(s, u):
                act.wait_ge(exp_done, u + 1)
                nc.scalar.activation(three[:, s % 2, 0::2, :], probs[:, s % 2, L:KEYS].rearrange("p (o k) -> p o k", o=1)
                                     .broadcast_to([P, 2, S]), ACT.Copy).then_inc(three_high, 1)

            def output(i, s, first):
                g, half = i * UNITS + s, s // 4 % 2
                act.wait_ge(pv_done, g + 1)
                act.wait_ge(rdenom_done, g + 1)
                if s % 4 == 0 and not (first and s < HK):
                    act.wait_ge(o_stored[half], (i * 2 + s // HK) * 16)
                nc.scalar.activation(o_stage[:, half, s % 4, :], o_acc[:, 0:D], ACT.Copy,
                                     scale=rdenom[:, s % 4:s % 4 + 1]).then_inc(o_done, 1)

            def iteration(i, first=False, last=False):
                for s in range(UNITS):
                    g = i * UNITS + s
                    act.wait_ge(turned_new, g + 1)
                    if not (first and s < 2):
                        act.wait_ge(pv_done, g - 1)
                    nc.scalar.activation(pt_three[:, s % 2, :], pt_new[0:3 * S, 0:P], ACT.Copy).then_inc(new_copied, 1)
                    act.wait_ge(turned_old, g + 1)
                    nc.scalar.activation(pt_hi[:, s % 2, 0:4, :], pt_old[s % 2][:, :, :], ACT.Copy).then_inc(hi_old, 1)
                    if s + 2 < UNITS or not last:
                        exp(i, s + 2, g + 2)
                    if s >= 1:
                        output(i, s - 1, first)
                    elif not first:
                        output(i - 1, UNITS - 1, False)
                    if s + 2 < UNITS or not last:
                        three_highs(s, g + 2)
                    buf, h = s // HK, s % HK
                    if 2 <= h <= 5 and not (last and buf == 1):
                        batch, early = i * 2 + buf, first and buf == 0
                        if h == 2:
                            if not early:
                                act.wait_ge(scores_done, batch * HK)
                            load_queries(batch + 1, 1 - buf)
                        else:
                            if not early:
                                act.wait_ge(pv_done, batch * HK)
                            load_new_values(batch + 1, 1 - buf, h - 3)

            load_queries(0, 0)
            for part in range(3):
                load_new_values(0, 0, part)
            exp(0, 0, 0)
            exp(0, 1, 1)
            three_highs(0, 0)
            three_highs(1, 1)
            iteration(0, first=True)
            with act.Fori(1, last_iter) as i:
                iteration(i)
            iteration(last_iter, last=True)
            output(last_iter, UNITS - 1, False)

        @block.vector
        def _(dve):
            def masked_max(i, s, u):
                buf = s // HK
                if s % HK == 0:
                    dve.wait_ge(mask_done, i * 2 + buf + 1)
                early = isinstance(u, int) and u < 2
                scores_needed, exps_needed = computed(dve, u + 1), computed(dve, u - 1)
                dve.wait_ge(packed_done, 5)
                dve.wait_ge(scores_done, scores_needed)
                if not early:
                    dve.wait_ge(exp_done, exps_needed)
                nc.vector.tensor_tensor_reduce(
                    masked[:, s % 2, :].rearrange("p (a k) -> p a k", a=2), scores[s % 2][:, :, 0:HALF],
                    mask[:, buf, :].rearrange("p (a k) -> p a k", a=2), 1.0, 3.0 * NEG, ALU.add, ALU.max,
                    rowmax[:, s % 4:s % 4 + 1]).then_inc(masked_done, 1)
                dve.wait_ge(masked_done, u + 1)
                nc.vector.tensor_scalar(bias[:, s % 4:s % 4 + 1], rowmax[:, s % 4:s % 4 + 1], -SCALE, None,
                                        ALU.mult).then_inc(bias_done, 1)

            def three_low(s, u):
                dve.wait_ge(three_high, u + 1)
                nc.vector.tensor_tensor(three[:, s % 2, 1, :], probs[:, s % 2, L:KEYS], three[:, s % 2, 0, :],
                                        ALU.subtract).then_inc(three_done, 1)

            def copy_new_keys(batch, buf):
                nc.vector.tensor_copy(keys32[:, buf, :, :, NPP * W:], kn32[:, buf, :, :, :]).then_inc(keys_dve, 1)

            def iteration(i, first=False, last=False):
                words = [None]
                for s in range(UNITS):
                    g = i * UNITS + s
                    if s + 2 < UNITS:
                        masked_max(i, s + 2, g + 2)
                    elif not last:
                        masked_max(i + 1, s + 2 - UNITS, g + 2)
                    if s + 1 < UNITS or not last:
                        three_low(s + 1, g + 1)
                    dve.wait_ge(exp_done, g + 1)
                    nc.vector.reciprocal(rdenom[:, s % 4:s % 4 + 1], denom[:, s % 4:s % 4 + 1]).then_inc(rdenom_done, 1)
                    dve.wait_ge(hi_old, g + 1)
                    nc.vector.tensor_tensor(pt_lo[:, s % 2, 0:4, :], pt_old[s % 2][:, :, :], pt_hi[:, s % 2, 0:4, :],
                                            ALU.subtract).then_inc(lo_old, 1)
                    buf, h = s // HK, s % HK
                    if h <= NPP - pool_pages and not (last and buf == 1):
                        batch = i * 2 + buf
                        if h < NPP - pool_pages:
                            if h == 0 and not (first and buf == 0):
                                dve.wait_ge(scores_done, batch * HK)
                            gather(dve, nc.vector, batch + 1, 1 - buf, pool_pages + h, words)
                        else:
                            dve.wait_ge(kn_loaded[1 - buf], (i + buf + 1) * 16)
                            copy_new_keys(batch + 1, 1 - buf)

            dve.wait_ge(tables_in, 48)
            nc.vector.tensor_copy(ident16[:, :], ident)
            nc.vector.tensor_copy(lens[:, :], lens_i[:, :]).then_inc(packed_done, 1)
            nc.vector.tensor_copy(pages_f[:, :, :], pages_i[:, :, :]).then_inc(packed_done, 1)
            dve.wait_ge(packed_done, 2)
            previous = pages_f[:, :, 3]
            for n in (2, 1, 0):
                out = packed if n == 0 else packed_f
                nc.vector.scalar_tensor_tensor(out=out[:, :], in0=previous, scalar=float(PAGES), in1=pages_f[:, :, n],
                                               op0=ALU.mult, op1=ALU.add).then_inc(packed_done, 1)
                previous = packed_f[:, :]
                dve.wait_ge(packed_done, 5 - n)
            words = [None]
            for j in range(NPP):
                gather(dve, nc.vector, 0, 0, j, words)
            dve.wait_ge(kn_loaded[0], 16)
            copy_new_keys(0, 0)
            masked_max(0, 0, 0)
            masked_max(0, 1, 1)
            three_low(0, 0)
            iteration(0, first=True)
            with dve.Fori(1, last_iter) as i:
                iteration(i)
            iteration(last_iter, last=True)


def phase3(nc, dram, keep):
    const = keep["const"]
    ident = const[:, _cols["ident"]]
    groups = HQ // REP
    room = keep["kt_all"][:, :, :, :, :].bitcast(F32).rearrange("p a b c d -> p (a b c d)")
    toep = room.rearrange("p (s n) -> p s n", s=S)
    n_angle = 3 * S + 2 * S * KA + S * KB
    with ExitStack() as ctx:
        def sb(name, shape, dt):
            return ctx.enter_context(nc.sbuf_tensor("p3_" + name, shape, dt))

        def ps(name, shape):
            return ctx.enter_context(nc.psum_tensor("p3_" + name, shape, F32))

        def sem(name):
            return ctx.enter_context(nc.semaphore("p3_" + name))

        wo = sb("wo", [P, HQ, 2, HID], F16)
        x1_t = sb("x1_t", [P, KT, S, B], F32)
        keep_mask = sb("keep_mask", [P, KT, B], F32)
        a_in = sb("a_in", [P, 2, REP, HK * D], F32)
        x_in = sb("x_rows", [P, 2, HID], F32)
        at = sb("at", [P, 2, 2, REP, P], F16)
        x1_t_back = sb("x1_t_back", [P, KT, S, B], F32)
        x1 = sb("x1", [P, HID], F32)
        x1_back = sb("x1_back", [P, KT, P], F32)
        z = a_in[:, :, 0, 0:KT * 4 * B].rearrange("p t (i s b) -> p t i s b", i=KT, s=4)
        len_i = sb("len_i", [P, B], I32)
        len_f = sb("len_f", [P, B], F32)
        taken = [0]

        def borrow(n):
            taken[0] += n
            return room[:, taken[0] - n:taken[0]]

        s4 = borrow(5 * S).rearrange("p (k h) -> p k h", k=5)
        par = borrow(15 * S).rearrange("p (k h) -> p k h", k=15)
        ang3, turns3, growth = borrow(n_angle), borrow(n_angle), borrow(S * (KA + KB))
        conv_k = borrow(S * KB)[0:KA].rearrange("p (h b) -> p h b", h=S)
        d_row = borrow(S)[0:1]
        zeros = borrow(P)[0:S]
        turned = [ps(f"turned_a{i}", [P, REP, P]) for i in range(2)]
        y_acc = [ps(f"y_acc{i}", [P, HID]) for i in range(2)]
        x1_turned = [ps(f"x1_turned{i}", [P, KT, P]) for i in range(2)]
        k_acc = ps("k_acc", [P, 2, 512])

        lengths_in, mask_steps, wo_loaded = sem("lengths_in"), sem("mask_steps"), [sem(f"wo_loaded{i}") for i in range(4)]
        a_loaded = [sem("a_loaded0"), sem("a_loaded1")]
        params_in = sem("params_in")
        step = sem("step")
        rates_done, angles_ready, growth_done, trig_done = (
            sem("rates_done"), sem("angles_ready"), sem("growth_done"), sem("trig_done"))
        factors_done, k_done, k_ready, k_stored = sem("factors_done"), sem("k_done"), sem("k_ready"), sem("k_stored")
        zeros_ready = sem("zeros_ready")
        turned_done, at_hi_done, at_lo_done, group_done = (
            sem("turned_done"), sem("at_hi_done"), sem("at_lo_done"), sem("group_done"))
        x1_done, x1_turned_done, x1_t_done = sem("x1_done"), sem("x1_turned_done"), sem("x1_t_done")
        x1_back_done = sem("x1_back_done")
        toep_loaded = sem("toep_loaded")
        conv_done, z_part, z_done = sem("conv_done"), sem("z_part"), sem("z_done")
        z_stored = [sem("z_stored0"), sem("z_stored1")]
        block = ctx.enter_context(nc.Block())

        n_cos, n_sin, n_b = S + S * KA, 2 * S + S * KA, S * KB
        cos_part, sin_part, b_part = slice(0, n_cos), slice(n_cos, n_cos + n_sin), slice(n_cos + n_sin, n_angle)

        def grid(tile, at, steps):
            return tile[:, at:at + S * steps].rearrange("p (h k) -> p h k", h=S)

        @block.sync
        def _(sp):
            sp.dma_start(s4, dram["s4d"]).then_inc(params_in, 16)
            sp.dma_start(d_row, dram["s4d_d"]).then_inc(params_in, 16)
            sp.dma_start(len_i[:, :], dram["lengths_wide"]).then_inc(lengths_in, 16)

            def load_tile(tile, buf):
                rows = dram["attn"][bass.ds(tile * BPT * P, BPT * P), :].rearrange("(b h s) n -> b s h n", b=BPT, h=REP)
                for b in range(BPT):
                    sp.dma_start(a_in[b * S:(b + 1) * S, buf, :, :], rows[b]).then_inc(a_loaded[buf], 16)
                sp.dma_start(x_in[:, buf, :], dram["x"][bass.ds(tile * P, P), :]).then_inc(a_loaded[buf], 16)

            load_tile(0, 0)
            for n in range(4):
                sp.dma_start(wo[:, n * 8:(n + 1) * 8, :, :], dram["wo_split"][:, n * 8:(n + 1) * 8, :, :]
                             ).then_inc(wo_loaded[n], 16)
            load_tile(1, 1)
            with sp.Fori(1, TILES // 2) as i:
                for buf in range(2):
                    sp.wait_ge(group_done, (i * 2 + buf - 1) * groups)
                    sp.wait_ge(x1_done, i * 2 + buf - 1)
                    load_tile(i * 2 + buf, buf)
            with sp.Fori(0, S // 8) as i:
                for par in range(2):
                    sp.wait_ge(z_done, i * 2 + par + 1)
                    sp.dma_start(dram["out"][:, :, bass.ds((i * 2 + par) * 4, 4), :].rearrange("i p s b -> p i s b"),
                                 z[:, par, :, :, :]).then_inc(z_stored[par], 16)
            for par in range(2):
                sp.wait_ge(z_stored[par], S // 8 * 16)

        @block.gpsimd
        def _(pool):
            shifted = bass.AP(tensor=dram["conv_k"].tensor, offset=LCONV - (P - 1), ap=[[2 * LCONV, S], [1, P], [1, LCONV]])

            backwards = bass.AP(tensor=x1[:, :].tensor, offset=P - 1, ap=[[HID, P], [P, KT], [-1, P]])
            def turn_back(done):
                pool.wait_ge(x1_done, done)
                nc.gpsimd.tensor_copy(x1_back[:, :, :], backwards).then_inc(x1_back_done, 1)

            def load_toeplitz(done):
                for j in range(S // TILES):
                    s = (done - 1) * (S // TILES) + j
                    pool.dma_start(toep[:, bass.ds(s, 1), :].rearrange("p o n -> p (o n)"),
                                   shifted[bass.ds(s, 1)].rearrange("o p n -> (o p) n")).then_inc(toep_loaded, 16)

            nc.gpsimd.memset(zeros, 0.0).then_inc(zeros_ready, 1)
            pool.wait_ge(zeros_ready, 1)
            pool.dma_start(dram["conv_k"][:, LCONV - P:LCONV], zeros).then_inc(k_stored, 16)
            turn_back(1)
            pool.wait_ge(k_ready, 2)
            pool.dma_start(dram["conv_k"][:, LCONV:].rearrange("h (a b) -> a h b", b=KB), conv_k).then_inc(k_stored, 16)
            pool.wait_ge(k_stored, 32)
            load_toeplitz(1)
            with pool.Fori(2, TILES + 1) as done:
                pool.wait_ge(a_loaded[0], 16)
                turn_back(done)
                load_toeplitz(done)
            pool.wait_ge(toep_loaded, S * 16)

        @block.scalar
        def _(act):
            def high(n, hg, early):
                act.wait_ge(turned_done, n + 1)
                if not early:
                    act.wait_ge(group_done, n - 1)
                nc.scalar.activation(at[:, hg % 2, 0, :, :], turned[hg % 2][:, :, :], ACT.Copy).then_inc(at_hi_done, 1)

            def spread(tile):
                act.wait_ge(x1_turned_done, tile + 1)
                for src, dst in zip(x1_turned, (x1_t, x1_t_back)):
                    nc.scalar.activation(dst[:, :, :, bass.ds(tile * BPT, BPT)].rearrange("p i s b -> p i b s"),
                                         src[:, :, :].rearrange("p i (b s) -> p i b s", b=BPT),
                                         ACT.Copy).then_inc(x1_t_done, 1)

            def iteration(i, first=False):
                for tt in range(2):
                    for hg in range(groups):
                        high((i * 2 + tt) * groups + hg, hg, first and tt == 0 and hg < 2)
                        if first and tt == 0 and hg == 1:
                            act.wait_ge(angles_ready, 1)
                            nc.scalar.activation(par[:, 4, :], par[:, 2, :], ACT.Tanh, scale=0.5).then_inc(growth_done, 1)
                            nc.scalar.activation(growth, growth, ACT.Exp).then_inc(growth_done, 1)
                        if first and tt == 0 and hg == 6:
                            act.wait_ge(angles_ready, 4)
                            nc.scalar.activation(turns3, ang3, ACT.Sin).then_inc(trig_done, 1)
                        if hg == 4 and not (first and tt == 0):
                            spread(i * 2 + tt - 1)

            act.wait_ge(params_in, 32)
            nc.scalar.activation(par[:, 0:2, :], s4[:, 0:2, :], ACT.Exp).then_inc(rates_done, 1)
            iteration(0, first=True)
            with act.Fori(1, TILES // 2) as i:
                iteration(i)
            spread(TILES - 1)

        @block.vector
        def _(dve):
            v = nc.vector
            dve.wait_ge(lengths_in, 16)
            v.tensor_copy(len_f[:, :], len_i[:, :]).then_inc(mask_steps, 1)
            dve.wait_ge(mask_steps, 1)
            v.tensor_tensor(keep_mask[:, :, :],
                                  const[:, _cols["hid_index"]].rearrange("p (i o) -> p i o", o=1).broadcast_to([P, KT, B]),
                                  len_f[:, :].rearrange("p (o b) -> p o b", o=1).broadcast_to([P, KT, B]), ALU.is_lt).then_inc(mask_steps, 1)
            def low(n, hg):
                dve.wait_ge(at_hi_done, n + 1)
                v.tensor_tensor(at[:, hg % 2, 1, :, :], turned[hg % 2][:, :, :], at[:, hg % 2, 0, :, :],
                                ALU.subtract).then_inc(at_lo_done, 1)

            def iteration(i):
                for tt in range(2):
                    for hg in range(groups):
                        low((i * 2 + tt) * groups + hg, hg)
                        if hg == 0:
                            add_input(i - 1 + tt, i * 2 + tt - 1, 1 - tt)

            done = [0]

            def next_low():
                n = done[0]
                done[0] += 1
                low(n, n % groups)
                if n == groups:
                    add_input(0, 0, 0)

            def add_input(pair, tile, buf):
                dve.wait_ge(group_done, (tile + 1) * groups)
                dve.wait_ge(a_loaded[buf], (pair + 1) * (BPT + 1) * 16)
                dve.wait_ge(x1_turned_done, tile)
                v.scalar_tensor_tensor(out=x1[:, :], in0=y_acc[buf][:, :], scalar=1.0 / WSCALE, in1=x_in[:, buf, :],
                                       op0=ALU.mult, op1=ALU.add).then_inc(x1_done, 1)

            count = [0]

            def chain(instruction):
                count[0] += 1
                instruction.then_inc(step, 1)
                dve.wait_ge(step, count[0])

            wide3 = lambda t, k: t.rearrange("p (h o) -> p h o", o=1).broadcast_to([P, S, k])
            dt, ar, wr, wi, th, g_re, g_im, n_re, n_im, ct_re, ct_im, tmp, inv, fx, fy = (par[:, k, :] for k in range(15))
            ai, cr, ci = s4[:, 2, :], s4[:, 3, :], s4[:, 4, :]
            dve.wait_ge(params_in, 32)
            dve.wait_ge(rates_done, 1)
            chain(v.tensor_scalar(ar, ar, -1.0, None, ALU.mult))
            chain(v.tensor_tensor(wr, ar, dt, ALU.mult))
            chain(v.tensor_tensor(wi, ai, dt, ALU.mult))
            steps_of = {k: const[:, _cols[k]].rearrange("p (o k) -> p o k", o=1).broadcast_to([P, S, n])
                        for k, n in (("a_step", KA), ("b_step", KB))}
            chain(v.tensor_tensor(grid(growth, 0, KA), wide3(wr, KA), steps_of["a_step"], ALU.mult))
            v.tensor_tensor(grid(growth, S * KA, KB), wide3(wr, KB), steps_of["b_step"], ALU.mult).then_inc(angles_ready, 1)
            next_low()
            chain(v.tensor_copy(ang3[:, 0:S], wi))
            chain(v.tensor_copy(ang3[:, n_cos:n_cos + S], wi))
            chain(v.tensor_scalar(ang3[:, n_cos + S:n_cos + 2 * S], wi, 0.5, None, ALU.mult))
            chain(v.tensor_tensor(grid(ang3, S, KA), wide3(wi, KA), steps_of["a_step"], ALU.mult))
            chain(v.tensor_copy(ang3[:, n_cos + 2 * S:n_cos + n_sin], ang3[:, S:n_cos]))
            chain(v.tensor_tensor(grid(ang3, n_cos + n_sin, KB), wide3(wi, KB), steps_of["b_step"], ALU.mult))
            next_low()
            regions = ((cos_part, 0.25, 0.25 * TWO_PI), (sin_part, 0.0, 0.0),
                       (b_part, const[:, _cols["v_turn"]], const[:, _cols["v_angle"]]))
            for cols, quarter, _ in regions:
                chain(v.tensor_scalar(turns3[:, cols], ang3[:, cols], 1.0 / TWO_PI, quarter, ALU.mult, ALU.add))
            next_low()
            chain(v.tensor_scalar(turns3[:, :], turns3[:, :], MAGIC, MAGIC, ALU.add, ALU.subtract))
            for part in (PI2_HI, PI2_MID, PI2_LO):
                chain(v.scalar_tensor_tensor(out=ang3[:, :], in0=turns3[:, :], scalar=-part, in1=ang3[:, :],
                                             op0=ALU.mult, op1=ALU.add))
                next_low()
            for cols, _, angle in regions:
                chain(v.tensor_scalar(ang3[:, cols], ang3[:, cols], angle, PI_SAFE, ALU.add, ALU.min))
                v.tensor_scalar(ang3[:, cols], ang3[:, cols], -PI_SAFE, None, ALU.max).then_inc(angles_ready, 1)
            next_low()
            dve.wait_ge(growth_done, 1)
            chain(v.tensor_scalar(tmp, th, -1.0, 1.0, ALU.mult, ALU.add))
            chain(v.reciprocal(inv, tmp))
            chain(v.scalar_tensor_tensor(out=th, in0=th, scalar=2.0, in1=inv, op0=ALU.mult, op1=ALU.mult))
            dve.wait_ge(trig_done, 1)
            cos_w, sin_w, sin_h = turns3[:, 0:S], turns3[:, n_cos:n_cos + S], turns3[:, n_cos + S:n_cos + 2 * S]
            chain(v.tensor_tensor(tmp, sin_h, sin_h, ALU.mult))
            chain(v.tensor_tensor(g_re, th, cos_w, ALU.mult))
            chain(v.scalar_tensor_tensor(out=g_re, in0=tmp, scalar=-2.0, in1=g_re, op0=ALU.mult, op1=ALU.add))
            chain(v.scalar_tensor_tensor(out=g_im, in0=th, scalar=1.0, in1=sin_w, op0=ALU.add, op1=ALU.mult))
            chain(v.tensor_tensor(n_re, cr, g_re, ALU.mult))
            chain(v.tensor_tensor(tmp, ci, g_im, ALU.mult))
            chain(v.tensor_tensor(n_re, n_re, tmp, ALU.subtract))
            chain(v.tensor_tensor(n_im, cr, g_im, ALU.mult))
            chain(v.tensor_tensor(tmp, ci, g_re, ALU.mult))
            chain(v.tensor_tensor(n_im, n_im, tmp, ALU.add))
            next_low()
            chain(v.tensor_tensor(tmp, ar, ar, ALU.mult))
            chain(v.tensor_tensor(inv, ai, ai, ALU.mult))
            chain(v.tensor_tensor(tmp, tmp, inv, ALU.add))
            chain(v.reciprocal(inv, tmp))
            chain(v.tensor_tensor(ct_re, n_re, ar, ALU.mult))
            chain(v.tensor_tensor(tmp, n_im, ai, ALU.mult))
            chain(v.tensor_tensor(ct_re, ct_re, tmp, ALU.add))
            chain(v.tensor_tensor(ct_re, ct_re, inv, ALU.mult))
            chain(v.tensor_tensor(ct_im, n_im, ar, ALU.mult))
            chain(v.tensor_tensor(tmp, n_re, ai, ALU.mult))
            chain(v.tensor_tensor(ct_im, ct_im, tmp, ALU.subtract))
            chain(v.tensor_tensor(ct_im, ct_im, inv, ALU.mult))
            next_low()
            mix = _cols["mix"].start
            for out, one, two, m in ((fx, ct_re, ct_im, 0), (fy, ct_im, ct_re, 2)):
                chain(v.tensor_scalar(tmp, one, const[:, mix + m:mix + m + 1], None, ALU.mult))
                chain(v.scalar_tensor_tensor(out=out, in0=two, scalar=const[:, mix + m + 1:mix + m + 2], in1=tmp,
                                             op0=ALU.mult, op1=ALU.add))
            cos_a, sin_a = grid(turns3, S, KA), grid(turns3, n_cos + 2 * S, KA)
            chain(v.tensor_tensor(cos_a, cos_a, wide3(fx, KA), ALU.mult))
            chain(v.tensor_tensor(sin_a, sin_a, wide3(fy, KA), ALU.mult))
            next_low()
            chain(v.tensor_tensor(cos_a, cos_a, sin_a, ALU.add))
            next_low()
            dve.wait_ge(growth_done, 2)
            chain(v.tensor_tensor(grid(ang3, 0, KA), cos_a, grid(growth, 0, KA), ALU.mult))
            v.tensor_tensor(grid(ang3, S * KA, KB), grid(turns3, n_cos + n_sin, KB), grid(growth, S * KA, KB),
                            ALU.mult).then_inc(factors_done, 1)
            next_low()
            dve.wait_ge(k_done, 1)
            v.tensor_copy(conv_k.rearrange("p h b -> p (h b)"),
                          k_acc[0:KA, :, :].rearrange("p a n -> p (a n)")).then_inc(k_ready, 1)
            dve.wait_ge(k_ready, 1)
            v.tensor_tensor(conv_k[0:1, :, 0], conv_k[0:1, :, 0], d_row, ALU.add).then_inc(k_ready, 1)

            while done[0] < 2 * groups:
                next_low()
            with dve.Fori(1, TILES // 2) as i:
                iteration(i)
            add_input(TILES // 2 - 1, TILES - 1, 1)
            dve.wait_ge(x1_t_done, TILES * 2)
            dve.wait_ge(mask_steps, 2)
            with dve.Fori(0, S // 8) as i:
                for par_z in range(2):
                    q = i * 2 + par_z
                    dve.wait_ge(conv_done, q + 1)
                    dve.wait_ge(z_stored[par_z], i * 16)
                    zq = z[:, par_z, :, :, :].rearrange("p i s b -> p s i b")
                    v.tensor_tensor(zq, k_acc[:, par_z, :].rearrange("p (s i b) -> p s i b", s=4, i=KT),
                                    keep_mask[:, :, :].rearrange("p (o i) b -> p o i b", o=1).broadcast_to([P, 4, KT, B]),
                                    ALU.mult).then_inc(z_part, 1)
                    dve.wait_ge(z_part, q + 1)
                    v.tensor_tensor(z[:, par_z, :, :, :], z[:, par_z, :, :, :], x1_t[:, :, bass.ds(q * 4, 4), :],
                                    ALU.add).then_inc(z_done, 1)

        @block.tensor
        def _(pe):
            def turn(i, n, tt, hg):
                if hg == 0:
                    pe.wait_ge(a_loaded[tt], (i + 1) * (BPT + 1) * 16)
                if not (isinstance(n, int) and n == 0):
                    pe.wait_ge(at_lo_done, n - 1)
                for h in range(REP):
                    last = nc.tensor.transpose(turned[hg % 2][:, h, :], a_in[:, tt, h, hg * D:(hg + 1) * D], ident)
                last.then_inc(turned_done, 1)

            def project(n, tt, hg):
                pe.wait_ge(at_lo_done, n + 1)
                for h in range(REP):
                    head = hg * REP + h
                    for k, (a, w) in enumerate(((0, 0), (0, 1), (1, 0))):
                        last = nc.tensor.matmul(y_acc[tt][:, :], at[:, hg % 2, a, h, :], wo[:, head, w, :],
                                                start=(head == 0 and k == 0), stop=(head == HQ - 1 and k == 2))
                last.then_inc(group_done, 1)

            def make_kernels():
                pe.wait_ge(factors_done, 1)
                for h in range(S):
                    last = nc.tensor.matmul(k_acc[0:KA, h // 16, h % 16 * KB:(h % 16 + 1) * KB],
                                            ang3[:, h * KA:(h + 1) * KA], ang3[:, S * KA + h * KB:S * KA + (h + 1) * KB],
                                            start=True, stop=True)
                last.then_inc(k_done, 1)

            def turn_x1(tile):
                pe.wait_ge(x1_done, tile + 1)
                pe.wait_ge(x1_t_done, tile * 2)
                for k in range(KT):
                    nc.tensor.transpose(x1_turned[0][:, k, :], x1[:, k * P:(k + 1) * P], ident)
                pe.wait_ge(x1_back_done, tile + 1)
                for k in range(KT):
                    last = nc.tensor.transpose(x1_turned[1][:, k, :], x1_back[:, k, :], ident)
                last.then_inc(x1_turned_done, 1)

            def iteration(i, first=False, final=False):
                for tt in range(2):
                    for hg in range(groups):
                        n = (i * 2 + tt) * groups + hg
                        if hg + 1 < groups:
                            turn(i, n + 1, tt, hg + 1)
                        elif not (final and tt == 1):
                            turn(i + tt, n + 1, 1 - tt, 0)
                        if hg == 2 and not (first and tt == 0):
                            turn_x1(i * 2 + tt - 1)
                        if first and tt == 0 and hg % 2 == 0:
                            pe.wait_ge(wo_loaded[hg // 2], 16)
                        if hg == 0 and not first:
                            pe.wait_ge(x1_done, i * 2 + tt - 1)
                        project(n, tt, hg)
                        if first and n == 11:
                            make_kernels()

            turn(0, 0, 0, 0)
            iteration(0, first=True)
            with pe.Fori(1, TILES // 2 - 1) as i:
                iteration(i)
            iteration(TILES // 2 - 1, final=True)
            turn_x1(TILES - 1)
            pe.wait_ge(x1_t_done, TILES * 2)
            pe.wait_ge(toep_loaded, S * 16)
            for i in range(S // 8):
                for j in range(8):
                    if j % 4 == 0 and i > 0:
                        pe.wait_ge(z_part, i * 2 - 1 + j // 4)
                    s = i * 8 + j
                    for d in range(KT):
                        base = j % 4 * KT * B
                        last = nc.tensor.matmul(
                            k_acc[:, j // 4, base + d * B:base + KT * B], toep[:, s, d * P:(d + 1) * P],
                            x1_t_back[:, 0:KT - d, s, :],
                            start=(d == 0), stop=(d == KT - 1))
                    if j % 4 == 3:
                        last.then_inc(conv_done, 1)


def build_program(nc, dram):
    keep = {}
    with ExitStack() as outer:
        def sb(stack, name, shape, dt):
            keep[name] = stack.enter_context(nc.sbuf_tensor(name, shape, dt))

        sb(outer, "const", [P, NCONST], F32)
        with ExitStack() as keys:
            sb(keys, "kt_all", [P, PAGES, HK, 2, PSIZE], F16)
            with ExitStack() as weights:
                sb(weights, "w_hi", [P, KT, E_ALL], F16)
                sb(weights, "w_lo", [P, KT, E_ALL], F16)
                sb(weights, "cos_t", [P, TILES, D // 2], F32)
                sb(weights, "sin_t", [P, TILES, D // 2], F32)
                sb(weights, "w_tab", [P, 4, D], F32)
                phase0(nc, dram, keep)
                phase1(nc, dram, keep)
            phase2(nc, dram, keep)
            phase3(nc, dram, keep)


def constants():
    c = np.zeros((P, NCONST), np.float32)
    p = np.arange(P)
    c[:, _cols["ident"]] = np.eye(P)
    c[:, _cols["token_in_batch"]] = (p % S)[:, None]
    c[:, _cols["inv_freq"]] = np.float32(1.0) / np.float32(10000.0) ** (np.arange(0, D, 2, dtype=np.float32) / np.float32(D))
    c[:, _cols["hid_index"]] = p[:, None] + P * np.arange(KT)
    c[:, _cols["a_step"]] = KB * np.arange(KA)
    c[:, _cols["b_step"]] = np.arange(KB)
    c[:, _cols["v_turn"]] = np.where(p < NSTATE, 0.25, 0.0)[:, None]
    c[:, _cols["v_angle"]] = c[:, _cols["v_turn"]] * np.float32(TWO_PI)
    top, low = (p < NSTATE)[:, None], (p >= NSTATE)[:, None]
    c[:, _cols["mix"]] = np.concatenate([2.0 * top, -2.0 * low, -2.0 * top, -2.0 * low], 1)
    return c


SCRATCH = {
    "q_t": ([B, P, HK, 2 * REP * S], F16),
    "k_new": ([B, P, HK * D // 512, 2 * REP * S], F16),
    "v_new": ([TOK, 2, HK * D], F16),
    "v_split": ([PAGES * PSIZE, 2, HK * D], F16),
    "wo_split": ([P, HQ, 2, HID], F16),
    "attn": ([B * REP * S, HK * D], F32),
    "conv_k": ([S, 2 * LCONV], F32),
}


def layout(x, itok_Bx16_0_63, itok_B_207_1644, itok_B_78_3631, L0_cond_Wq, L0_cond_Wk, L0_cond_Wv, L0_cond_Wo,
           L0_cond_q_norm_w, L0_cond_k_norm_w, L0_cond_k_cache, L0_cond_v_cache, L1_cond_log_dt, L1_cond_C,
           L1_cond_log_A_real, L1_cond_A_imag, L1_cond_D):
    a = np.asarray
    h = D // 2
    rows = a(x).reshape(TOK, HID)
    qw, kw = a(L0_cond_q_norm_w), a(L0_cond_k_norm_w)
    tab = np.stack([qw, np.concatenate([qw[h:], qw[:h]]), kw, np.concatenate([kw[h:], kw[:h]])])
    twice = lambda m: np.concatenate([a(m).T, a(m).T])
    wide = lambda v: np.broadcast_to(a(v), (P,) + a(v).shape)
    c = a(L1_cond_C)

    def padded(m, n, axis):
        return np.pad(m, [(0, n if k == axis else 0) for k in range(2)])

    arrays = {
        "x": rows,
        "xt": padded(rows.T, P, 1),
        "w_all": np.concatenate([a(L0_cond_Wq), a(L0_cond_Wk), a(L0_cond_Wv)]).T,
        "wo_t": padded(a(L0_cond_Wo).T, P, 0),
        "kt": padded(a(L0_cond_k_cache).transpose(3, 0, 2, 1).reshape(D, PAGES * HK * PSIZE), 512, 1),
        "v_cache": padded(a(L0_cond_v_cache).reshape(PAGES * PSIZE, HK * D), P, 0),
        "norm_w": wide(tab),
        "pages": a(itok_Bx16_0_63).reshape(1, B * NPP),
        "seqlens_by_token": np.repeat(a(itok_B_207_1644), S).reshape(TILES, P).T,
        "seqlens_wide": wide(itok_B_207_1644),
        "lengths_wide": wide(itok_B_78_3631),
        "s4d": np.stack([wide(L1_cond_log_dt), twice(L1_cond_log_A_real), twice(L1_cond_A_imag),
                         twice(c[:, :, 0]), twice(c[:, :, 1])], 1),
        "s4d_d": a(L1_cond_D).reshape(1, S),
        "consts": constants(),
        "key_index": wide(np.concatenate([np.arange(L), np.full(S, -1)]).astype(np.float32)),
    }
    return {k: np.ascontiguousarray(v) for k, v in arrays.items()}


def kernel(**inputs):
    from concourse import bacc
    from concourse.bass_utils import run_bass_kernel_spmd

    nc = bacc.Bacc("TRN2", target_bir_lowering=False, num_devices=1)
    arrays = layout(**inputs)
    dram = {n: nc.dram_tensor(n, list(v.shape), mybir.dt.from_np(v.dtype), kind="ExternalInput").ap()
            for n, v in arrays.items()}
    for n, (shape, dt) in SCRATCH.items():
        dram[n] = nc.dram_tensor(n, shape, dt, kind="Internal").ap()
    dram["out"] = nc.dram_tensor("out", [KT, P, S, B], F32, kind="ExternalOutput").ap()
    build_program(nc, dram)
    r = run_bass_kernel_spmd(nc, [arrays], core_ids=[0])
    out = r.results[0]["out"]
    return np.ascontiguousarray(out.transpose(3, 2, 0, 1).reshape(B, S, HID))
```

```python
from contextlib import ExitStack

import numpy as np

import concourse.bass as bass
from concourse import mybir

F32 = mybir.dt.float32
F16 = mybir.dt.float16
I32 = mybir.dt.int32
ALU = mybir.AluOpType
ACT = mybir.ActivationFunctionType
AX_X = mybir.AxisListType.X

P = 128
B, S, HID = 32, 32, 512
D, HQ, HK = 128, 32, 8
REP = HQ // HK
PAGES, PSIZE, NPP = 64, 32, 16
L = NPP * PSIZE
KEYS = L + S
HALF = KEYS // 2
TOK = B * S
TILES = TOK // P
BPT = P // S
KT = HID // P
E_ALL = (HQ + 2 * HK) * D
CHUNKS = E_ALL // 512
NORMED = (HQ + HK) * D // 512
QCH = HQ * D // 512
NPIECE = 4
UNITS = 2 * HK
NSTATE, LCONV = 64, HID
KA, KB = 16, 32
EPS = 1e-6
SCALE = 1.0 / float(np.sqrt(D))
WSCALE = 64.0
NEG = -1e30
MAGIC = 1.5 * 2.0 ** 23
TWO_PI = 6.283185307179586
PI2_HI = 6.28125
PI2_MID = float(np.float32(np.float16(TWO_PI - PI2_HI)))
PI2_LO = TWO_PI - PI2_HI - PI2_MID
PI_SAFE = 3.1415925
W_SLOTS = 6
ROT_LAG, TURN_LAG = 2, 3
TURN_AT = 3

_cols, _at = {}, 0
for _name, _n in (("ident", P), ("token_in_batch", 1), ("inv_freq", D // 2),
                  ("hid_index", KT), ("a_step", KA), ("b_step", KB), ("v_turn", 1), ("v_angle", 1),
                  ("mix", 4)):
    _cols[_name] = slice(_at, _at + _n)
    _at += _n
NCONST = _at


def phase0(nc, dram, keep):
    const, w_hi, w_lo, cos_t, sin_t, w_tab, kt_all, lens, packed = (
        keep[k] for k in ("const", "w_hi", "w_lo", "cos_t", "sin_t", "w_tab", "kt_all", "lens", "packed"))
    with ExitStack() as ctx:
        def sb(name, shape, dt):
            return ctx.enter_context(nc.sbuf_tensor("p0_" + name, shape, dt))

        def sem(name):
            return ctx.enter_context(nc.semaphore("p0_" + name))

        w_in = kt_all[:, :, :, :, :].bitcast(F32).rearrange("p a b c d -> p (a b c d)")[:, 0:W_SLOTS * KT * 512].rearrange(
            "p (c i e) -> p c i e", c=W_SLOTS, i=KT)
        seq_i = sb("seq_i", [P, TILES], I32)
        lens_i = sb("lens_i", [P, B], I32)
        pages_i = sb("pages_i", [1, B * NPP // 4, 4], I32)
        pages_f = sb("pages_f", [1, B * NPP // 4, 4], F32)
        packed_f = sb("packed_f", [1, B * NPP // 4], F32)
        tables_in, packed_done = sem("tables_in"), sem("packed_done")
        slots = sb("slots", [P, 1], F32)
        pos = sb("pos", [P, TILES], F32)
        ang = sb("ang", [P, TILES, D // 2], F32)
        turns = sb("turns", [P, TILES, D // 2], F32)
        off = sb("off", [P, TILES, D // 2], F32)
        red_c = sb("red_c", [P, TILES, D // 2], F32)
        red_s = sb("red_s", [P, TILES, D // 2], F32)
        const_in, w_loaded = sem("const_in"), [sem(f"w_loaded{i}") for i in range(W_SLOTS)]
        w_hi_done, w_free = sem("w_hi_done"), sem("w_free")
        rope_step, angles_done, sincos_done = sem("rope_step"), sem("angles_done"), sem("sincos_done")
        block = ctx.enter_context(nc.Block())

        @block.sync
        def _(sp):
            sp.dma_start(const[:, :], dram["consts"]).then_inc(const_in, 16)
            sp.dma_start(seq_i[:, :], dram["seqlens_by_token"]).then_inc(const_in, 16)
            sp.dma_start(w_tab[:, :, :], dram["norm_w"]).then_inc(const_in, 16)
            sp.dma_start(pages_i[:, :, :], dram["pages"].rearrange("a (b c) -> a b c", c=4)).then_inc(tables_in, 16)
            sp.dma_start(lens_i[:, :], dram["seqlens_wide"]).then_inc(tables_in, 16)
            w_src = dram["w_all"].rearrange("(i p) e -> p i e", p=P)
            with sp.Fori(0, CHUNKS // W_SLOTS) as rnd:
                for k in range(W_SLOTS):
                    sp.wait_ge(w_free, rnd * W_SLOTS + k + 1)
                    sp.dma_start(w_in[:, k, :, :],
                                 w_src[:, :, bass.ds((rnd * W_SLOTS + k) * 512, 512)]).then_inc(w_loaded[k], 16)

        @block.scalar
        def _(act):
            with act.Fori(0, CHUNKS // W_SLOTS) as rnd:
                for k in range(W_SLOTS):
                    act.wait_ge(w_loaded[k], rnd * 16 + 16)
                    nc.scalar.activation(w_hi[:, :, bass.ds((rnd * W_SLOTS + k) * 512, 512)], w_in[:, k, :, :],
                                         ACT.Copy, scale=WSCALE).then_inc(w_hi_done, 1)
            act.wait_ge(angles_done, 2)
            nc.scalar.activation(cos_t[:, :, :], red_c[:, :, :], ACT.Sin).then_inc(sincos_done, 1)
            nc.scalar.activation(sin_t[:, :, :], red_s[:, :, :], ACT.Sin).then_inc(sincos_done, 1)

        @block.gpsimd
        def _(pool):
            pool.wait_ge(const_in, 16 * 3)
            steps = [0]

            def stepped(instruction):
                steps[0] += 1
                instruction.then_inc(rope_step, 1)
                pool.wait_ge(rope_step, steps[0])

            stepped(nc.gpsimd.tensor_copy(pos[:, :], seq_i[:, :]))
            stepped(nc.gpsimd.tensor_scalar(pos[:, :], pos[:, :], const[:, _cols["token_in_batch"]], None, ALU.add))
            freq = const[:, _cols["inv_freq"]]
            stepped(nc.gpsimd.tensor_tensor(
                ang[:, :, :], pos[:, :].rearrange("p (t o) -> p t o", o=1).broadcast_to([P, TILES, D // 2]),
                freq.rearrange("p (o f) -> p o f", o=1).broadcast_to([P, TILES, D // 2]), ALU.mult))
            for quarter, red in ((0.25, red_c), (0.0, red_s)):
                stepped(nc.gpsimd.tensor_scalar(turns[:, :, :], ang[:, :, :], 1.0 / TWO_PI, quarter, ALU.mult, ALU.add))
                stepped(nc.gpsimd.tensor_scalar(turns[:, :, :], turns[:, :, :], MAGIC, MAGIC, ALU.add, ALU.subtract))
                src = ang
                for part in (PI2_HI, PI2_MID, PI2_LO):
                    stepped(nc.gpsimd.tensor_scalar(off[:, :, :], turns[:, :, :], -part, None, ALU.mult))
                    stepped(nc.gpsimd.tensor_tensor(red[:, :, :], off[:, :, :], src[:, :, :], ALU.add))
                    src = red
                stepped(nc.gpsimd.tensor_scalar(red[:, :, :], red[:, :, :], quarter * TWO_PI, PI_SAFE, ALU.add, ALU.min))
                nc.gpsimd.tensor_scalar(red[:, :, :], red[:, :, :], -PI_SAFE, None, ALU.max).then_inc(angles_done, 1)
            for j in range(2):
                stepped(nc.gpsimd.tensor_scalar(w_tab[:, 2 * j + 1, 0:D // 2], w_tab[:, 2 * j + 1, 0:D // 2],
                                                -1.0, None, ALU.mult))

        @block.vector
        def _(dve):
            nc.vector.memset(slots[:, :], 0.0).then_inc(w_free, W_SLOTS)
            dve.wait_ge(w_free, W_SLOTS)
            dve.wait_ge(tables_in, 32)
            nc.vector.tensor_copy(lens[:, :], lens_i[:, :]).then_inc(packed_done, 1)
            nc.vector.tensor_copy(pages_f[:, :, :], pages_i[:, :, :]).then_inc(packed_done, 1)
            dve.wait_ge(packed_done, 2)
            previous = pages_f[:, :, 3]
            for n in (2, 1, 0):
                out = packed if n == 0 else packed_f
                nc.vector.scalar_tensor_tensor(out=out[:, :], in0=previous, scalar=float(PAGES), in1=pages_f[:, :, n],
                                               op0=ALU.mult, op1=ALU.add).then_inc(packed_done, 1)
                previous = packed_f[:, :]
                dve.wait_ge(packed_done, 5 - n)
            with dve.Fori(0, CHUNKS // W_SLOTS) as rnd:
                for k in range(W_SLOTS):
                    dve.wait_ge(w_hi_done, rnd * W_SLOTS + k + 1)
                    nc.vector.scalar_tensor_tensor(
                        out=w_lo[:, :, bass.ds((rnd * W_SLOTS + k) * 512, 512)], in0=w_in[:, k, :, :], scalar=WSCALE,
                        in1=w_hi[:, :, bass.ds((rnd * W_SLOTS + k) * 512, 512)], op0=ALU.mult,
                        op1=ALU.subtract).then_inc(w_free, 1)
            dve.wait_ge(w_free, CHUNKS + W_SLOTS)
            dve.wait_ge(sincos_done, 2)


def phase1(nc, dram, keep):
    const, w_hi, w_lo, cos_t, sin_t, w_tab, kt_all = (
        keep[k] for k in ("const", "w_hi", "w_lo", "cos_t", "sin_t", "w_tab", "kt_all"))
    ident = const[:, _cols["ident"]]
    with ExitStack() as ctx:
        def sb(name, shape, dt):
            return ctx.enter_context(nc.sbuf_tensor("p1_" + name, shape, dt))

        def ps(name, shape):
            return ctx.enter_context(nc.psum_tensor("p1_" + name, shape, F32))

        def sem(name):
            return ctx.enter_context(nc.semaphore("p1_" + name))

        x_in = sb("x_in", [P, KT, P], F32)
        x_hi = sb("x_hi", [P, 2, KT, P], F16)
        x_lo = sb("x_lo", [P, 2, KT, P], F16)
        piece_in = sb("piece_in", [P, 3, 512], F32)
        piece_out = sb("piece_out", [P, 2, 2, 512], F16)
        eps_t = sb("eps_t", [P, 2], F32)
        sumsq = sb("sumsq", [P, 2, REP], F32)
        rms = sb("rms", [P, 2, REP], F32)
        rrms = sb("rrms", [P, 2, REP], F32)
        normed = sb("normed", [P, 2, REP, D], F32)
        rot_a = sb("rot_a", [P, 3, REP, D], F32)
        rot_b = sb("rot_b", [P, 2, REP, D], F32)
        tables = sb("tables", [P, 4, D], F32)
        v_stage = sb("v_stage", [P, 2, 2, 512], F16)
        stage = sb("stage", [P, 2, 1024], F16)
        proj = [ps(f"proj{i}", [P, 512]) for i in range(3)]
        squares = ps("squares", [P, REP, D])
        turned = [ps(f"turned{i}", [P, 512]) for i in range(2)]

        x_loaded, x_hi_done, x_lo_done = sem("x_loaded"), sem("x_hi_done"), sem("x_lo_done")
        piece_loaded = [sem(f"piece_loaded{i}") for i in range(3)]
        piece_hi_done, piece_free = sem("piece_hi_done"), sem("piece_free")
        piece_stored = [sem("piece_stored0"), sem("piece_stored1")]
        proj_done, proj_free = sem("proj_done"), sem("proj_free")
        squares_done, rms_done, rrms_done = sem("squares_done"), sem("rms_done"), sem("rrms_done")
        normed_done, rotated_parts, rotated, turned_done = (
            sem("normed_done"), sem("rotated_parts"), sem("rotated"), sem("turned_done"))
        table_done = sem("table_done")
        stage_hi_done, stage_lo_done, v_hi_done = sem("stage_hi_done"), sem("stage_lo_done"), sem("v_hi_done")
        stored = [sem(f"stored{i}") for i in range(2)]
        v_stored = [sem(f"v_stored{i}") for i in range(2)]
        block = ctx.enter_context(nc.Block())

        def k_piece(tile, c, part):
            pages = kt_all[:, bass.ds((tile * NPIECE + c // 3) * 2, 2), :, part, :]
            return pages

        def split_q(slot, part):
            return stage[:, slot, :].rearrange("p (b l h s) -> p l h b s", b=BPT, l=2, h=REP)[:, part]

        def split_k(slot, part):
            return stage[:, slot, :].rearrange("p (b h l s) -> p l h b s", b=BPT, h=REP, l=2)[:, part]

        @block.sync
        def _(sp):
            x_src = dram["xt"].rearrange("(i p) t -> p i t", p=P)
            v_src = dram["v_cache"].rearrange("(t p) (h e) -> p t h e", p=P, e=512)
            o_src = dram["wo_t"].rearrange("(h p) n -> p h n", p=P)

            def load_piece(tile, c):
                sp.wait_ge(piece_free, tile * CHUNKS + c + 1)
                nth = tile * NPIECE + c // 3
                if c % 3 == 0:
                    src = dram["kt"][:, bass.ds(nth * 512, 512)]
                elif c % 3 == 1:
                    src = v_src[:, bass.ds(tile * 2 + c // 6, 1), (c // 3) % 2, :]
                else:
                    src = o_src[:, bass.ds(nth, 1), :]
                sp.dma_start(piece_in[:, c % 3, :], src).then_inc(piece_loaded[c % 3], 16)

            def store_chunk(tile, j):
                needed = sp.compute_val(tile * NORMED + j + 1)
                if j >= QCH:
                    sp.wait_ge(piece_free, 3)
                sp.wait_ge(stage_lo_done, needed)
                dst = dram["q_t"][bass.ds(tile * BPT, BPT), :, j, :] if j < QCH else \
                    dram["k_new"][bass.ds(tile * BPT, BPT), :, j - QCH, :]
                sp.dma_start(dst.rearrange("b p n -> p b n"),
                             stage[:, j % 2, :].rearrange("p (b n) -> p b n", b=BPT)).then_inc(stored[j % 2], 16)

            def store_v(tile, half):
                sp.wait_ge(proj_free, tile * CHUNKS + NORMED + half + 4)
                sp.dma_start(dram["v_new"][bass.ds(tile * P, P), :, half * 512:(half + 1) * 512],
                             v_stage[:, half, :, :]).then_inc(v_stored[half], 16)

            def store_piece(tile, c):
                sp.wait_ge(piece_free, tile * CHUNKS + c + 4)
                if c % 3 == 1:
                    half = (c // 3) % 2
                    dst = dram["v_split"][bass.ds((tile * 2 + c // 6) * P, P), :, half * 512:(half + 1) * 512]
                else:
                    dst = dram["wo_split"][:, bass.ds(tile * NPIECE + c // 3, 1), :, :].rearrange("p o l n -> p (o l) n")
                sp.dma_start(dst, piece_out[:, c % 3 - 1, :, :]).then_inc(piece_stored[c % 3 - 1], 16)

            sp.dma_start(x_in[:, :, :], x_src[:, :, 0:P]).then_inc(x_loaded, 16)
            for c in range(3):
                load_piece(0, c)
            with sp.Fori(0, TILES // 2) as i2:
                for tt in range(2):
                    tile = i2 * 2 + tt
                    for c in range(CHUNKS + 1):
                        if c >= TURN_LAG:
                            store_chunk(tile, c - TURN_LAG)
                        if c > NORMED:
                            store_v(tile, c - NORMED - 1)
                        if c >= 1:
                            load_piece(tile + (c + 2) // CHUNKS, (c + 2) % CHUNKS)
                            if (c - 1) % 3:
                                store_piece(tile, c - 1)
                        if c == 1:
                            sp.wait_ge(x_lo_done, tile + 1)
                            sp.dma_start(x_in[:, :, :], x_src[:, :, bass.ds((tile + 1) * P, P)]).then_inc(x_loaded, 16)
            for slot in range(2):
                sp.wait_ge(stored[slot], TILES * (NORMED // 2) * 16)
                sp.wait_ge(piece_stored[slot], TILES * NPIECE * 16)
                sp.wait_ge(v_stored[slot], TILES * 16)
            for slot in range(3):
                sp.wait_ge(piece_loaded[slot], (TILES * NPIECE + 1) * 16)
            sp.wait_ge(x_loaded, (TILES + 1) * 16)

        @block.tensor
        def _(pe):
            with pe.Fori(0, TILES // 2) as i2:
                for tt in range(2):
                    tile = i2 * 2 + tt
                    pe.wait_ge(x_lo_done, tile + 1)

                    def turn(j):
                        pe.wait_ge(rotated, tile * NORMED + j + 1)
                        pe.wait_ge(stage_lo_done, tile * NORMED + max(j - 1, 0))
                        for h in range(REP):
                            last = nc.tensor.transpose(turned[j % 2][:, h * P:(h + 1) * P], rot_a[:, j % 3, h, :], ident)
                        last.then_inc(turned_done, 1)

                    for c in range(CHUNKS):
                        pe.wait_ge(proj_free, tile * CHUNKS + c + 1)
                        n = 0
                        for k in range(KT):
                            for x_part, w_part in ((x_hi, w_hi), (x_hi, w_lo), (x_lo, w_hi)):
                                if n == TURN_AT and c >= TURN_LAG:
                                    turn(c - TURN_LAG)
                                last = nc.tensor.matmul(proj[c % 3][:, :], x_part[:, tt, k, :],
                                                        w_part[:, k, c * 512:(c + 1) * 512],
                                                        start=(n == 0), stop=(n == 3 * KT - 1))
                                n += 1
                        last.then_inc(proj_done, 1)
                    turn(CHUNKS - TURN_LAG)

        @block.scalar
        def _(act):
            act.wait_ge(proj_free, 3)
            act.wait_ge(x_loaded, 16)
            nc.scalar.activation(x_hi[:, 0, :, :], x_in[:, :, :], ACT.Copy).then_inc(x_hi_done, 1)
            with act.Fori(0, TILES // 2) as i2:
                for tt in range(2):
                    tile = i2 * 2 + tt

                    for c in range(CHUNKS + 1):
                        if c >= TURN_LAG:
                            j = c - TURN_LAG
                            act.wait_ge(turned_done, tile * NORMED + j + 1)
                            act.wait_ge(stored[j % 2], (tile * (NORMED // 2) + j // 2) * 16)
                            split = split_q if j < QCH else split_k
                            nc.scalar.activation(split(j % 2, 0),
                                                 turned[j % 2][:, :].rearrange("p (h b s) -> p h b s", h=REP, b=BPT),
                                                 ACT.Copy).then_inc(stage_hi_done, 1)
                        if c == CHUNKS:
                            break
                        slot, nth = c % 3, tile * NPIECE + c // 3
                        act.wait_ge(piece_loaded[slot], (nth + 1) * 16)
                        if slot == 0:
                            nc.scalar.activation(k_piece(tile, c, 0),
                                                 piece_in[:, slot, :].rearrange("p (g h s) -> p g h s", g=2, h=HK),
                                                 ACT.Copy).then_inc(piece_hi_done, 1)
                        else:
                            act.wait_ge(piece_stored[slot - 1], nth * 16)
                            nc.scalar.activation(piece_out[:, slot - 1, 0, :], piece_in[:, slot, :], ACT.Copy,
                                                 scale=WSCALE if slot == 2 else 1.0).then_inc(piece_hi_done, 1)
                        act.wait_ge(proj_done, tile * CHUNKS + c + 1)
                        if c < NORMED:
                            n = tile * NORMED + c
                            act.wait_ge(squares_done, n * REP)
                            for h in range(REP):
                                nc.scalar.activation(squares[:, h, :], proj[c % 3][:, h * D:(h + 1) * D], ACT.Square,
                                                     accum_out=sumsq[:, c % 2, h:h + 1]).then_inc(squares_done, 1)
                            act.wait_ge(squares_done, (n + 1) * REP)
                            act.wait_ge(rrms_done, tile * NORMED + max(c - 1, 0))
                            nc.scalar.activation(rms[:, c % 2, :], sumsq[:, c % 2, :], ACT.Sqrt,
                                                 bias=eps_t[:, 0:1], scale=1.0 / D).then_inc(rms_done, 1)
                        else:
                            act.wait_ge(v_stored[c - NORMED], tile * 16)
                            nc.scalar.activation(v_stage[:, c - NORMED, 0, :], proj[c % 3][:, :], ACT.Copy,
                                                 scale=1.0 / WSCALE).then_inc(v_hi_done, 1)
                        if c == 5:
                            act.wait_ge(x_loaded, (tile + 2) * 16)
                            act.wait_ge(proj_done, tile * CHUNKS)
                            nc.scalar.activation(x_hi[:, 1 - tt, :, :], x_in[:, :, :], ACT.Copy).then_inc(x_hi_done, 1)

        @block.vector
        def _(dve):
            nc.vector.memset(eps_t[:, 0:1], EPS * WSCALE * WSCALE).then_inc(proj_free, 3)
            nc.vector.memset(eps_t[:, 1:2], 0.0).then_inc(piece_free, 3)
            dve.wait_ge(x_hi_done, 1)
            nc.vector.tensor_tensor(x_lo[:, 0, :, :], x_in[:, :, :], x_hi[:, 0, :, :], ALU.subtract).then_inc(x_lo_done, 1)
            with dve.Fori(0, TILES // 2) as i2:
                for tt in range(2):
                    tile = i2 * 2 + tt
                    for c in range(CHUNKS + 1):
                        if ROT_LAG <= c < NORMED + ROT_LAG:
                            j = c - ROT_LAG
                            dve.wait_ge(rotated_parts, (tile * NORMED + j + 1) * 2)
                            nc.vector.tensor_tensor(rot_a[:, j % 3, :, :], rot_a[:, j % 3, :, :],
                                                    rot_b[:, j % 2, :, :], ALU.add).then_inc(rotated, 1)
                        if c >= TURN_LAG:
                            j = c - TURN_LAG
                            split = split_q if j < QCH else split_k
                            dve.wait_ge(stage_hi_done, tile * NORMED + j + 1)
                            nc.vector.tensor_tensor(split(j % 2, 1),
                                                    turned[j % 2][:, :].rearrange("p (h b s) -> p h b s", h=REP, b=BPT),
                                                    split(j % 2, 0), ALU.subtract).then_inc(stage_lo_done, 1)
                        if c >= 1 and (c - 1) % 3 != 1:
                            pc = c - 1
                            dve.wait_ge(piece_hi_done, tile * CHUNKS + pc + 1)
                            dve.wait_ge(piece_free, tile * CHUNKS + pc + 3)
                            if pc % 3 == 0:
                                nc.vector.tensor_tensor(k_piece(tile, pc, 1),
                                                        piece_in[:, 0, :].rearrange("p (g h s) -> p g h s", g=2, h=HK),
                                                        k_piece(tile, pc, 0), ALU.subtract).then_inc(piece_free, 1)
                            else:
                                nc.vector.scalar_tensor_tensor(out=piece_out[:, 1, 1, :], in0=piece_in[:, 2, :],
                                                               scalar=WSCALE, in1=piece_out[:, 1, 0, :],
                                                               op0=ALU.mult, op1=ALU.subtract).then_inc(piece_free, 1)
                        if c == CHUNKS:
                            break
                        if c < NORMED:
                            n = tile * NORMED + c
                            dve.wait_ge(rms_done, n + 1)
                            nc.vector.reciprocal(rrms[:, c % 2, :], rms[:, c % 2, :]).then_inc(rrms_done, 1)
                            dve.wait_ge(rrms_done, n + 1)
                            nc.vector.tensor_tensor(
                                normed[:, c % 2, :, :], proj[c % 3][:, :].rearrange("p (h d) -> p h d", h=REP),
                                rrms[:, c % 2, :].rearrange("p (h o) -> p h o", o=1).broadcast_to([P, REP, D]),
                                ALU.mult).then_inc(proj_free, 1)
                        else:
                            dve.wait_ge(v_hi_done, tile * (CHUNKS - NORMED) + c - NORMED + 1)
                            nc.vector.scalar_tensor_tensor(out=v_stage[:, c - NORMED, 1, :], in0=proj[c % 3][:, :],
                                                           scalar=1.0 / WSCALE, in1=v_stage[:, c - NORMED, 0, :],
                                                           op0=ALU.mult, op1=ALU.subtract).then_inc(proj_free, 1)
                        if c == 5:
                            dve.wait_ge(x_hi_done, tile + 2)
                            nc.vector.tensor_tensor(x_lo[:, 1 - tt, :, :], x_in[:, :, :], x_hi[:, 1 - tt, :, :],
                                                    ALU.subtract).then_inc(x_lo_done, 1)

        @block.gpsimd
        def _(pool):
            with pool.Fori(0, TILES // 2) as i2:
                for tt in range(2):
                    tile = i2 * 2 + tt
                    pool.wait_ge(rotated_parts, tile * NORMED * 2)
                    for j, trig in enumerate((cos_t, sin_t, cos_t, sin_t)):
                        nc.gpsimd.tensor_tensor(
                            tables[:, j, :].rearrange("p (a f) -> p a f", a=2),
                            trig[:, bass.ds(tile, 1), :].broadcast_to([P, 2, D // 2]),
                            w_tab[:, j, :].rearrange("p (a f) -> p a f", a=2), ALU.mult).then_inc(table_done, 1)
                    pool.wait_ge(table_done, (tile + 1) * 4)
                    for c in range(CHUNKS):
                        if c % 3 == 1:
                            pool.wait_ge(piece_hi_done, tile * CHUNKS + c + 1)
                            pool.wait_ge(piece_free, tile * CHUNKS + c + 3)
                            nc.gpsimd.tensor_tensor(piece_out[:, 0, 1, :], piece_in[:, 1, :],
                                                    piece_out[:, 0, 0, :], ALU.subtract).then_inc(piece_free, 1)
                        if c < NORMED:
                            pool.wait_ge(proj_free, tile * CHUNKS + c + 4)
                            pool.wait_ge(turned_done, tile * NORMED + max(c - 2, 0))
                            kind, half = 0 if c < QCH else 2, D // 2
                            cos_b, sin_b = (tables[:, kind + k, :].rearrange("p (o d) -> p o d", o=1)
                                            .broadcast_to([P, REP, D]) for k in range(2))
                            nc.gpsimd.tensor_tensor(rot_a[:, c % 3, :, :], normed[:, c % 2, :, :], cos_b,
                                                    ALU.mult).then_inc(rotated_parts, 1)
                            for k in range(2):
                                ins = nc.gpsimd.tensor_tensor(rot_b[:, c % 2, :, k * half:(k + 1) * half],
                                                              normed[:, c % 2, :, (1 - k) * half:(2 - k) * half],
                                                              sin_b[:, :, k * half:(k + 1) * half], ALU.mult)
                            ins.then_inc(rotated_parts, 1)


def phase2(nc, dram, keep):
    const, kt_all, lens, packed = (keep[k] for k in ("const", "kt_all", "lens", "packed"))
    ident = const[:, _cols["ident"]]
    pool_pages = 12
    last_iter = B // 2 - 1
    with ExitStack() as ctx:
        def sb(name, shape, dt):
            return ctx.enter_context(nc.sbuf_tensor("p2_" + name, shape, dt))

        def ps(name, shape):
            return ctx.enter_context(nc.psum_tensor("p2_" + name, shape, F32))

        def sem(name):
            return ctx.enter_context(nc.semaphore("p2_" + name))

        key_index = sb("key_index", [P, KEYS], F32)
        batch_len = sb("batch_len", [P, 2], F32)
        q_in = sb("q_in", [P, 2, HK, 2, P], F16)
        kn_in = sb("kn_in", [P, 2, HK, 2, S], F16)
        keys = sb("keys", [P, 2, HK, 2, KEYS], F16)
        v_in = sb("v_in", [P, 2, KT, 2, HK, D], F16)
        vn_in = sb("vn_in", [3 * S, 2, HK, D], F16)
        mask = sb("mask", [P, 2, KEYS], F32)
        masked = sb("masked", [P, 2, KEYS], F32)
        rowmax = sb("rowmax", [P, 4], F32)
        bias = sb("bias", [P, 4], F32)
        denom = sb("denom", [P, 4], F32)
        rdenom = sb("rdenom", [P, 4], F32)
        probs = sb("probs", [P, 2, KEYS], F32)
        pt_hi = sb("pt_hi", [P, 2, 4, P], F16)
        pt_lo = sb("pt_lo", [P, 2, 4, P], F16)
        three = sb("three", [P, 2, 3, S], F16)
        ident16 = sb("ident16", [P, P], F16)
        pt_three = sb("pt_three", [3 * S, 2, P], F16)
        o_stage = sb("o_stage", [P, 2, 4, D], F32)
        scores = [ps(f"scores{i}", [P, 2, 512]) for i in range(2)]
        pt_old = [ps(f"pt_old{i}", [P, 4, P]) for i in range(2)]
        pt_new = ctx.enter_context(nc.psum_tensor("p2_pt_new", [P, 1024], F16))
        o_acc = ps("o_acc", [P, 512])
        kt32 = kt_all[:, :, :, :, :].bitcast(F32)
        keys32 = keys[:, :, :, :, :].bitcast(F32)
        kn32 = kn_in[:, :, :, :, :].bitcast(F32)
        W = PSIZE // 2

        tables_in, packed_done, ahead_loaded = sem("tables_in"), sem("packed_done"), sem("ahead_loaded")
        q_loaded = [sem("q_loaded0"), sem("q_loaded1")]
        kn_loaded = [sem("kn_loaded0"), sem("kn_loaded1")]
        vn_loaded = [sem("vn_loaded0"), sem("vn_loaded1")]
        v_loaded = [sem("v_loaded0"), sem("v_loaded1")]
        keys_pool, keys_dve = sem("keys_pool"), sem("keys_dve")
        scores_done, masked_done, bias_done = sem("scores_done"), sem("masked_done"), sem("bias_done")
        len_done = sem("len_done")
        mask_done, rdenom_done, exp_done = sem("mask_done"), sem("rdenom_done"), sem("exp_done")
        turned_new, turned_old = sem("turned_new"), sem("turned_old")
        three_high, three_done, new_copied, hi_old, lo_old = (
            sem("three_high"), sem("three_done"), sem("new_copied"), sem("hi_old"), sem("lo_old"))
        pv_done, o_done = sem("pv_done"), sem("o_done")
        o_stored = [sem("o_stored0"), sem("o_stored1")]
        block = ctx.enter_context(nc.Block())

        def computed(eng, value):
            return value if isinstance(value, int) else eng.compute_val(value)

        def page_of(eng, batch, j, words):
            if j % 4 == 0:
                words[0] = eng.value_load(packed[0:1, bass.ds(batch * (NPP // 4) + j // 4, 1)],
                                          min_val=0, max_val=PAGES ** 4 - 1)
            return (words[0] >> (6 * (j % 4))) & (PAGES - 1)

        def gather(eng, ops, batch, buf, j, words):
            page = page_of(eng, batch, j, words)
            src = kt32[:, bass.ds(page, 1), :, :, :].rearrange("p o h l w -> p (o h) l w")
            return ops.tensor_copy(keys32[:, buf, :, :, j * W:(j + 1) * W], src)

        @block.sync
        def _(sp):
            sp.dma_start(key_index[:, :], dram["key_index"]).then_inc(tables_in, 16)

            def load_new_keys(batch, buf):
                sp.dma_start(kn_in[:, buf, :, :, :].rearrange("p h l s -> p (h l s)"),
                             dram["k_new"][bass.ds(batch, 1), :, :, :].rearrange("o p c n -> (o p) (c n)")
                             ).then_inc(kn_loaded[buf], 16)

            def load_values(batch, buf):
                words = [None]
                for j in range(NPP):
                    page = page_of(sp, batch, j, words)
                    r = (j % 4) * PSIZE
                    sp.dma_start(v_in[r:r + PSIZE, buf, j // 4, :, :, :].rearrange("p l h d -> p (l h d)"),
                                 dram["v_split"][bass.ds(page * PSIZE, PSIZE), :, :].rearrange("p l n -> p (l n)")
                                 ).then_inc(v_loaded[buf], 16)

            def batch_io(batch, buf, more):
                if more:
                    if not (isinstance(batch, int) and batch == 0):
                        copies_needed, units_needed = computed(sp, batch), computed(sp, batch * HK)
                        sp.wait_ge(packed_done, 1)
                        sp.wait_ge(keys_dve, copies_needed)
                        sp.wait_ge(pv_done, units_needed)
                    load_new_keys(batch + 1, 1 - buf)
                    load_values(batch + 1, 1 - buf)
                for half in range(2):
                    sp.wait_ge(o_done, batch * HK + half * 4 + 4)
                    sp.dma_start(dram["attn"][bass.ds(batch * P, P), half * 4 * D:(half + 1) * 4 * D],
                                 o_stage[:, half, :, :].rearrange("p u d -> p (u d)")).then_inc(o_stored[half], 16)

            load_new_keys(0, 0)
            load_values(0, 0)
            for k in range(2):
                batch_io(k, k, True)
            with sp.Fori(1, last_iter) as i:
                for k in range(2):
                    batch_io(i * 2 + k, k, True)
            for k in range(2):
                batch_io(last_iter * 2 + k, k, k == 0)
                if k == 0:
                    sp.dma_start(keep["wo_first"][:, :, :, :], dram["wo_split"][:, 0:HQ // 4, :, :]).then_inc(ahead_loaded, 16)
                    sp.wait_ge(keys_pool, B - 1)
                    sp.wait_ge(keys_dve, B)
                    for half in range(2):
                        sp.wait_ge(o_stored[half], BPT * 16)
                    first = first_tile(keep)
                    rows = dram["attn"][0:BPT * P, :].rearrange("(b h s) n -> b s h n", b=BPT, h=REP)
                    for b in range(BPT):
                        sp.dma_start(first[b * S:(b + 1) * S, :, :], rows[b]).then_inc(ahead_loaded, 16)
            sp.wait_ge(ahead_loaded, (BPT + 1) * 16)
            for half in range(2):
                sp.wait_ge(o_stored[half], B * 16)

        @block.gpsimd
        def _(pool):
            pool.wait_ge(tables_in, 16)

            def gather_pool(batch, buf):
                words = [None]
                for j in range(pool_pages):
                    ins = gather(pool, nc.gpsimd, batch, buf, j, words)
                ins.then_inc(keys_pool, 1)

            def mask_of(batch, buf):
                nc.gpsimd.tensor_copy(batch_len[:, buf:buf + 1], lens[:, bass.ds(batch, 1)]).then_inc(len_done, 1)
                lens_needed = computed(pool, batch + 1)
                pool.wait_ge(packed_done, 1)
                pool.wait_ge(len_done, lens_needed)
                nc.gpsimd.tensor_scalar(mask[:, buf, :], key_index[:, :], batch_len[:, buf:buf + 1], NEG,
                                        ALU.is_ge, ALU.mult).then_inc(mask_done, 1)

            mask_of(0, 0)
            gather_pool(1, 1)
            mask_of(1, 1)
            with pool.Fori(1, B // 2) as i:
                for k in range(2):
                    pool.wait_ge(scores_done, (i * 2 + k - 1) * HK)
                    pool.wait_ge(keys_pool, i * 2 + k - 1)
                    gather_pool(i * 2 + k, k)
                    pool.wait_ge(masked_done, (i * 2 + k - 1) * HK)
                    pool.wait_ge(mask_done, i * 2 + k)
                    mask_of(i * 2 + k, k)

        @block.tensor
        def _(pe):
            def scores_of(i, s, u):
                buf, h = s // HK, s % HK
                if h == 0:
                    pe.wait_ge(q_loaded[buf], (i + 1) * 16)
                    if not (isinstance(i, int) and i * 2 + buf == 0):
                        pe.wait_ge(keys_pool, i * 2 + buf)
                    pe.wait_ge(keys_dve, i * 2 + buf + 1)
                if not (isinstance(u, int) and u < 2):
                    pe.wait_ge(masked_done, u - 1)
                q_hi, q_lo = q_in[:, buf, h, 0, :], q_in[:, buf, h, 1, :]
                k_hi, k_lo = keys[:, buf, h, 0, :], keys[:, buf, h, 1, :]
                for n, (q, k) in enumerate(((q_hi, k_hi), (q_hi, k_lo), (q_lo, k_hi))):
                    for half in range(2):
                        last = nc.tensor.matmul(scores[s % 2][:, half, 0:HALF], q, k[:, half * HALF:(half + 1) * HALF],
                                                start=(n == 0), stop=(n == 2))
                last.then_inc(scores_done, 1)

            def turn(i, s, first):
                g = i * UNITS + s
                pe.wait_ge(three_done, g + 1)
                if not (first and s < 1):
                    pe.wait_ge(new_copied, g)
                nc.tensor.transpose(pt_new[0:3 * S, 0:P], three[:, s % 2, :, :].rearrange("p a k -> p (a k)"), ident16[:, :]).then_inc(turned_new, 1)
                pe.wait_ge(exp_done, g + 1)
                if not (first and s < 2):
                    pe.wait_ge(lo_old, g - 1)
                for t in range(4):
                    last = nc.tensor.transpose(pt_old[s % 2][:, t, :], probs[:, s % 2, t * P:(t + 1) * P], ident)
                last.then_inc(turned_old, 1)

            def pv(i, s, first):
                g, buf, h = i * UNITS + s, s // HK, s % HK
                if h == 0:
                    pe.wait_ge(v_loaded[buf], (i + 1) * NPP * 16)
                    pe.wait_ge(vn_loaded[buf], (i + 1) * 48)
                pe.wait_ge(new_copied, g + 1)
                pe.wait_ge(lo_old, g + 1)
                if not (first and s < 1):
                    pe.wait_ge(o_done, g)
                for t in range(4):
                    for p_part, l in ((pt_hi, 0), (pt_hi, 1), (pt_lo, 0)):
                        nc.tensor.matmul(o_acc[:, 0:D], p_part[:, s % 2, t, :], v_in[:, buf, t, l, h, :],
                                         start=(t == 0 and p_part is pt_hi and l == 0), stop=False)
                last = nc.tensor.matmul(o_acc[:, 0:D], pt_three[:, s % 2, :], vn_in[:, buf, h, :], start=False, stop=True)
                last.then_inc(pv_done, 1)

            def iteration(i, first=False, last=False):
                for s in range(UNITS):
                    if s + 2 < UNITS:
                        scores_of(i, s + 2, i * UNITS + s + 2)
                    elif not last:
                        scores_of(i + 1, s + 2 - UNITS, i * UNITS + s + 2)
                    turn(i, s, first)
                    if s >= 1:
                        pv(i, s - 1, first)
                    elif not first:
                        pv(i - 1, UNITS - 1, False)

            scores_of(0, 0, 0)
            scores_of(0, 1, 1)
            iteration(0, first=True)
            with pe.Fori(1, last_iter) as i:
                iteration(i)
            iteration(last_iter, last=True)
            pv(last_iter, UNITS - 1, False)

        @block.scalar
        def _(act):
            def load_queries(batch, buf):
                act.dma_start(q_in[:, buf, :, :, :].rearrange("p h l n -> p (h l n)"),
                              dram["q_t"][bass.ds(batch, 1), :, :, :].rearrange("o p h n -> (o p) (h n)")
                              ).then_inc(q_loaded[buf], 16)

            def load_new_values(batch, buf, part):
                act.dma_start(vn_in[part * S:(part + 1) * S, buf, :, :].rearrange("p h d -> p (h d)"),
                              dram["v_new"][bass.ds(batch * S, S), part // 2, :]).then_inc(vn_loaded[buf], 16)

            def exp(i, s, u):
                act.wait_ge(bias_done, u + 1)
                nc.scalar.activation(probs[:, s % 2, :], masked[:, s % 2, :], ACT.Exp, bias=bias[:, s % 4:s % 4 + 1],
                                     scale=SCALE, accum_out=denom[:, s % 4:s % 4 + 1]).then_inc(exp_done, 1)

            def three_highs(s, u):
                act.wait_ge(exp_done, u + 1)
                nc.scalar.activation(three[:, s % 2, 0::2, :], probs[:, s % 2, L:KEYS].rearrange("p (o k) -> p o k", o=1)
                                     .broadcast_to([P, 2, S]), ACT.Copy).then_inc(three_high, 1)

            def output(i, s, first):
                g, half = i * UNITS + s, s // 4 % 2
                act.wait_ge(pv_done, g + 1)
                act.wait_ge(rdenom_done, g + 1)
                if s % 4 == 0 and not (first and s < HK):
                    act.wait_ge(o_stored[half], (i * 2 + s // HK) * 16)
                nc.scalar.activation(o_stage[:, half, s % 4, :], o_acc[:, 0:D], ACT.Copy,
                                     scale=rdenom[:, s % 4:s % 4 + 1]).then_inc(o_done, 1)

            def iteration(i, first=False, last=False):
                for s in range(UNITS):
                    g = i * UNITS + s
                    act.wait_ge(turned_new, g + 1)
                    if not (first and s < 2):
                        act.wait_ge(pv_done, g - 1)
                    nc.scalar.activation(pt_three[:, s % 2, :], pt_new[0:3 * S, 0:P], ACT.Copy).then_inc(new_copied, 1)
                    act.wait_ge(turned_old, g + 1)
                    nc.scalar.activation(pt_hi[:, s % 2, 0:4, :], pt_old[s % 2][:, :, :], ACT.Copy).then_inc(hi_old, 1)
                    if s + 2 < UNITS or not last:
                        exp(i, s + 2, g + 2)
                    if s >= 1:
                        output(i, s - 1, first)
                    elif not first:
                        output(i - 1, UNITS - 1, False)
                    if s + 2 < UNITS or not last:
                        three_highs(s, g + 2)
                    buf, h = s // HK, s % HK
                    if 2 <= h <= 5 and not (last and buf == 1):
                        batch, early = i * 2 + buf, first and buf == 0
                        if h == 2:
                            if not early:
                                act.wait_ge(scores_done, batch * HK)
                            load_queries(batch + 1, 1 - buf)
                        else:
                            if not early:
                                act.wait_ge(pv_done, batch * HK)
                            load_new_values(batch + 1, 1 - buf, h - 3)

            load_queries(0, 0)
            for part in range(3):
                load_new_values(0, 0, part)
            exp(0, 0, 0)
            exp(0, 1, 1)
            three_highs(0, 0)
            three_highs(1, 1)
            iteration(0, first=True)
            with act.Fori(1, last_iter) as i:
                iteration(i)
            iteration(last_iter, last=True)
            output(last_iter, UNITS - 1, False)

        @block.vector
        def _(dve):
            def masked_max(i, s, u):
                buf = s // HK
                if s % HK == 0:
                    dve.wait_ge(mask_done, i * 2 + buf + 1)
                early = isinstance(u, int) and u < 2
                scores_needed, exps_needed = computed(dve, u + 1), computed(dve, u - 1)
                dve.wait_ge(packed_done, 1)
                dve.wait_ge(scores_done, scores_needed)
                if not early:
                    dve.wait_ge(exp_done, exps_needed)
                nc.vector.tensor_tensor_reduce(
                    masked[:, s % 2, :].rearrange("p (a k) -> p a k", a=2), scores[s % 2][:, :, 0:HALF],
                    mask[:, buf, :].rearrange("p (a k) -> p a k", a=2), 1.0, 3.0 * NEG, ALU.add, ALU.max,
                    rowmax[:, s % 4:s % 4 + 1]).then_inc(masked_done, 1)
                dve.wait_ge(masked_done, u + 1)
                nc.vector.tensor_scalar(bias[:, s % 4:s % 4 + 1], rowmax[:, s % 4:s % 4 + 1], -SCALE, None,
                                        ALU.mult).then_inc(bias_done, 1)

            def three_low(s, u):
                dve.wait_ge(three_high, u + 1)
                nc.vector.tensor_tensor(three[:, s % 2, 1, :], probs[:, s % 2, L:KEYS], three[:, s % 2, 0, :],
                                        ALU.subtract).then_inc(three_done, 1)

            def copy_new_keys(batch, buf):
                nc.vector.tensor_copy(keys32[:, buf, :, :, NPP * W:], kn32[:, buf, :, :, :]).then_inc(keys_dve, 1)

            def iteration(i, first=False, last=False):
                words = [None]
                for s in range(UNITS):
                    g = i * UNITS + s
                    if s + 2 < UNITS:
                        masked_max(i, s + 2, g + 2)
                    elif not last:
                        masked_max(i + 1, s + 2 - UNITS, g + 2)
                    if s + 1 < UNITS or not last:
                        three_low(s + 1, g + 1)
                    dve.wait_ge(exp_done, g + 1)
                    nc.vector.reciprocal(rdenom[:, s % 4:s % 4 + 1], denom[:, s % 4:s % 4 + 1]).then_inc(rdenom_done, 1)
                    dve.wait_ge(hi_old, g + 1)
                    nc.vector.tensor_tensor(pt_lo[:, s % 2, 0:4, :], pt_old[s % 2][:, :, :], pt_hi[:, s % 2, 0:4, :],
                                            ALU.subtract).then_inc(lo_old, 1)
                    buf, h = s // HK, s % HK
                    if h <= NPP - pool_pages and not (last and buf == 1):
                        batch = i * 2 + buf
                        if h < NPP - pool_pages:
                            if h == 0 and not (first and buf == 0):
                                dve.wait_ge(scores_done, batch * HK)
                            gather(dve, nc.vector, batch + 1, 1 - buf, pool_pages + h, words)
                        else:
                            dve.wait_ge(kn_loaded[1 - buf], (i + buf + 1) * 16)
                            copy_new_keys(batch + 1, 1 - buf)

            nc.vector.tensor_copy(ident16[:, :], ident).then_inc(packed_done, 1)
            words = [None]
            for j in range(NPP):
                gather(dve, nc.vector, 0, 0, j, words)
            dve.wait_ge(kn_loaded[0], 16)
            copy_new_keys(0, 0)
            masked_max(0, 0, 0)
            masked_max(0, 1, 1)
            three_low(0, 0)
            iteration(0, first=True)
            with dve.Fori(1, last_iter) as i:
                iteration(i)
            iteration(last_iter, last=True)


def first_tile(keep):
    room = keep["kt_all"][:, :, :, :, :].bitcast(F32).rearrange("p a b c d -> p (a b c d)")
    return room[:, PAGES * HK * PSIZE - REP * HK * D:].rearrange("p (h n) -> p h n", h=REP)


def phase3(nc, dram, keep):
    const = keep["const"]
    ident = const[:, _cols["ident"]]
    groups = HQ // REP
    room = keep["kt_all"][:, :, :, :, :].bitcast(F32).rearrange("p a b c d -> p (a b c d)")
    toep = keep["kt_all"][:, :, :, :, :].rearrange("p a b c d -> p (a b c d)").rearrange("p (s l n) -> p s l n", s=S, l=2)
    n_angle = 3 * S + 2 * S * KA + S * KB
    with ExitStack() as ctx:
        def sb(name, shape, dt):
            return ctx.enter_context(nc.sbuf_tensor("p3_" + name, shape, dt))

        def ps(name, shape):
            return ctx.enter_context(nc.psum_tensor("p3_" + name, shape, F32))

        def sem(name):
            return ctx.enter_context(nc.semaphore("p3_" + name))

        wo = sb("wo", [P, HQ - HQ // 4, 2, HID], F16)
        x1_t = sb("x1_t", [P, KT, S, B], F32)
        keep_mask = sb("keep_mask", [P, KT, B], F32)
        a_in = sb("a_in", [P, 2, REP, HK * D], F32)
        x_in = sb("x_rows", [P, 2, HID], F32)
        at = sb("at", [P, 2, 2, REP, P], F16)
        x1_t_back = sb("x1_t_back", [P, 2, KT, S, B], F16)
        x1 = sb("x1", [P, HID], F32)
        x1_back = sb("x1_back", [P, KT, P], F32)
        z = a_in[:, :, 0, 0:KT * 4 * B].rearrange("p t (i s b) -> p t i s b", i=KT, s=4)
        len_i = sb("len_i", [P, B], I32)
        len_f = sb("len_f", [P, B], F32)
        taken = [0]

        def borrow(n):
            taken[0] += n
            return room[:, taken[0] - n:taken[0]]

        s4 = borrow(5 * S).rearrange("p (k h) -> p k h", k=5)
        par = borrow(15 * S).rearrange("p (k h) -> p k h", k=15)
        ang3, turns3, growth = borrow(n_angle), borrow(n_angle), borrow(S * (KA + KB))
        conv_k = borrow(S * KB)[0:KA].rearrange("p (h b) -> p h b", h=S)
        d_row = borrow(S)[0:1]
        kernel_parts = borrow(S * KB)[0:KA].bitcast(F16).rearrange("p (l h b) -> p l h b", l=2, h=S)
        zeros = borrow(P)[0:S].bitcast(F16)
        turned = [ps(f"turned_a{i}", [P, REP, P]) for i in range(2)]
        y_acc = [ps(f"y_acc{i}", [P, HID]) for i in range(2)]
        x1_turned = [ps(f"x1_turned{i}", [P, KT, P]) for i in range(2)]
        k_acc = ps("k_acc", [P, 2, 512])

        lengths_in, mask_steps, wo_loaded = sem("lengths_in"), sem("mask_steps"), [sem(f"wo_loaded{i}") for i in range(3)]
        a_loaded = [sem("a_loaded0"), sem("a_loaded1")]
        params_in = sem("params_in")
        step = sem("step")
        rates_done, angles_ready, growth_done, trig_done = (
            sem("rates_done"), sem("angles_ready"), sem("growth_done"), sem("trig_done"))
        k_hi_done, k_lo_done, back_lo_done = sem("k_hi_done"), sem("k_lo_done"), sem("back_lo_done")
        factors_done, k_done, k_ready, k_stored = sem("factors_done"), sem("k_done"), sem("k_ready"), sem("k_stored")
        zeros_ready = sem("zeros_ready")
        turned_done, at_hi_done, at_lo_done, group_done = (
            sem("turned_done"), sem("at_hi_done"), sem("at_lo_done"), sem("group_done"))
        x1_done, x1_turned_done, x1_t_done = sem("x1_done"), sem("x1_turned_done"), sem("x1_t_done")
        x1_back_done = sem("x1_back_done")
        toep_loaded = sem("toep_loaded")
        conv_done, z_part, z_done = sem("conv_done"), sem("z_part"), sem("z_done")
        z_stored = [sem("z_stored0"), sem("z_stored1")]
        block = ctx.enter_context(nc.Block())

        first_a = first_tile(keep)

        def wo_head(head, part):
            return keep["wo_first"][:, head, part, :] if head < HQ // 4 else wo[:, head - HQ // 4, part, :]

        def loads(pair, buf):
            return pair * (BPT + 1) * 16 + (16 if buf == 0 else (BPT + 1) * 16)

        n_cos, n_sin = S + S * KA, 2 * S + S * KA
        cos_part, sin_part, b_part = slice(0, n_cos), slice(n_cos, n_cos + n_sin), slice(n_cos + n_sin, n_angle)

        def grid(tile, at, steps):
            return tile[:, at:at + S * steps].rearrange("p (h k) -> p h k", h=S)

        @block.sync
        def _(sp):
            sp.dma_start(s4, dram["s4d"]).then_inc(params_in, 16)
            sp.dma_start(d_row, dram["s4d_d"]).then_inc(params_in, 16)
            sp.dma_start(len_i[:, :], dram["lengths_wide"]).then_inc(lengths_in, 16)

            def load_tile(tile, buf):
                sp.dma_start(x_in[:, buf, :], dram["x"][bass.ds(tile * P, P), :]).then_inc(a_loaded[buf], 16)
                if isinstance(tile, int) and tile == 0:
                    return
                rows = dram["attn"][bass.ds(tile * BPT * P, BPT * P), :].rearrange("(b h s) n -> b s h n", b=BPT, h=REP)
                for b in range(BPT):
                    sp.dma_start(a_in[b * S:(b + 1) * S, buf, :, :], rows[b]).then_inc(a_loaded[buf], 16)

            load_tile(0, 0)
            quarter = HQ // 4
            for n in range(3):
                sp.dma_start(wo[:, n * quarter:(n + 1) * quarter, :, :],
                             dram["wo_split"][:, (n + 1) * quarter:(n + 2) * quarter, :, :]).then_inc(wo_loaded[n], 16)
            load_tile(1, 1)
            with sp.Fori(1, TILES // 2) as i:
                for buf in range(2):
                    sp.wait_ge(group_done, (i * 2 + buf - 1) * groups)
                    sp.wait_ge(x1_done, i * 2 + buf - 1)
                    load_tile(i * 2 + buf, buf)
            with sp.Fori(0, S // 8) as i:
                for par in range(2):
                    sp.wait_ge(z_done, i * 2 + par + 1)
                    sp.dma_start(dram["out"][:, :, bass.ds((i * 2 + par) * 4, 4), :].rearrange("i p s b -> p i s b"),
                                 z[:, par, :, :, :]).then_inc(z_stored[par], 16)
            for par in range(2):
                sp.wait_ge(z_stored[par], S // 8 * 16)

        @block.gpsimd
        def _(pool):
            shifted = bass.AP(tensor=dram["conv_k"].tensor, offset=LCONV - (P - 1),
                              ap=[[4 * LCONV, S], [1, P], [2 * LCONV, 2], [1, LCONV]])

            backwards = bass.AP(tensor=x1[:, :].tensor, offset=P - 1, ap=[[HID, P], [P, KT], [-1, P]])
            def turn_back(done):
                if not isinstance(done, int):
                    pool.wait_ge(zeros_ready, 1)
                pool.wait_ge(x1_done, done)
                nc.gpsimd.tensor_copy(x1_back[:, :, :], backwards).then_inc(x1_back_done, 1)

            def load_toeplitz(done):
                for j in range(S // TILES):
                    s = (done - 1) * (S // TILES) + j
                    pool.dma_start(toep[:, bass.ds(s, 1), :, :].rearrange("p o l n -> p (o l) n"),
                                   shifted[bass.ds(s, 1)].rearrange("o p l n -> (o p) l n")).then_inc(toep_loaded, 16)

            nc.gpsimd.memset(zeros, 0.0).then_inc(zeros_ready, 1)
            pool.wait_ge(zeros_ready, 1)
            for part in range(2):
                pool.dma_start(dram["conv_k"][:, part, LCONV - P:LCONV], zeros[:, 0:P]).then_inc(k_stored, 16)
            turn_back(1)
            turn_back(2)
            pool.wait_ge(k_lo_done, 1)
            for part in range(2):
                pool.dma_start(dram["conv_k"][:, part, LCONV:].rearrange("h (a b) -> a h b", b=KB),
                               kernel_parts[:, part, :, :]).then_inc(k_stored, 16)
            pool.wait_ge(k_stored, 64)
            load_toeplitz(1)
            load_toeplitz(2)
            with pool.Fori(3, TILES + 1) as done:
                load_toeplitz(done)
                turn_back(done)
            pool.wait_ge(toep_loaded, S * 16)

        @block.scalar
        def _(act):
            def high(n, hg, early):
                act.wait_ge(turned_done, n + 1)
                if not early:
                    act.wait_ge(group_done, n - 1)
                nc.scalar.activation(at[:, hg % 2, 0, :, :], turned[hg % 2][:, :, :], ACT.Copy).then_inc(at_hi_done, 1)

            def spread(tile):
                act.wait_ge(x1_turned_done, tile + 1)
                for n, dst in enumerate((x1_t, x1_t_back[:, 0])):
                    nc.scalar.activation(dst[:, :, :, bass.ds(tile * BPT, BPT)].rearrange("p i s b -> p i b s"),
                                         x1_turned[n][:, :, :].rearrange("p i (b s) -> p i b s", b=BPT),
                                         ACT.Copy).then_inc(x1_t_done, 1)

            def iteration(i, first=False):
                for tt in range(2):
                    for hg in range(groups):
                        high((i * 2 + tt) * groups + hg, hg, first and tt == 0 and hg < 2)
                        if first and tt == 0 and hg == 1:
                            act.wait_ge(params_in, 32)
                            nc.scalar.activation(par[:, 0:2, :], s4[:, 0:2, :], ACT.Exp).then_inc(rates_done, 1)
                        if first and tt == 0 and hg == 2:
                            act.wait_ge(angles_ready, 1)
                            nc.scalar.activation(par[:, 4, :], par[:, 2, :], ACT.Tanh, scale=0.5).then_inc(growth_done, 1)
                            nc.scalar.activation(growth, growth, ACT.Exp).then_inc(growth_done, 1)
                        if first and tt == 1 and hg == 0:
                            act.wait_ge(angles_ready, 4)
                            nc.scalar.activation(turns3, ang3, ACT.Sin).then_inc(trig_done, 1)
                        if first and tt == 1 and hg == 6:
                            act.wait_ge(k_ready, 2)
                            nc.scalar.activation(kernel_parts[:, 0, :, :], conv_k, ACT.Copy, scale=WSCALE).then_inc(k_hi_done, 1)
                        if hg == 4 and not (first and tt == 0):
                            spread(i * 2 + tt - 1)

            iteration(0, first=True)
            with act.Fori(1, TILES // 2) as i:
                iteration(i)
            spread(TILES - 1)

        @block.vector
        def _(dve):
            v = nc.vector

            def spread_low(tile):
                dve.wait_ge(x1_t_done, (tile + 1) * 2)
                hi, lo = (x1_t_back[:, part, :, :, bass.ds(tile * BPT, BPT)].rearrange("p i s b -> p i b s")
                          for part in range(2))
                v.tensor_tensor(lo, x1_turned[1][:, :, :].rearrange("p i (b s) -> p i b s", b=BPT), hi,
                                ALU.subtract).then_inc(back_lo_done, 1)

            dve.wait_ge(lengths_in, 16)
            v.tensor_copy(len_f[:, :], len_i[:, :]).then_inc(mask_steps, 1)
            dve.wait_ge(mask_steps, 1)
            v.tensor_tensor(keep_mask[:, :, :],
                                  const[:, _cols["hid_index"]].rearrange("p (i o) -> p i o", o=1).broadcast_to([P, KT, B]),
                                  len_f[:, :].rearrange("p (o b) -> p o b", o=1).broadcast_to([P, KT, B]), ALU.is_lt).then_inc(mask_steps, 1)
            dve.wait_ge(mask_steps, 2)
            v.tensor_scalar(keep_mask[:, :, :], keep_mask[:, :, :], 1.0 / WSCALE, None, ALU.mult).then_inc(mask_steps, 1)
            def low(n, hg):
                dve.wait_ge(at_hi_done, n + 1)
                v.tensor_tensor(at[:, hg % 2, 1, :, :], turned[hg % 2][:, :, :], at[:, hg % 2, 0, :, :],
                                ALU.subtract).then_inc(at_lo_done, 1)

            def iteration(i):
                for tt in range(2):
                    for hg in range(groups):
                        low((i * 2 + tt) * groups + hg, hg)
                        if hg == 0:
                            add_input(i - 1 + tt, i * 2 + tt - 1, 1 - tt)
                        if hg == 5:
                            spread_low(i * 2 + tt - 1)

            done = [0]

            def next_low():
                n = done[0]
                done[0] += 1
                low(n, n % groups)
                if n == groups:
                    add_input(0, 0, 0)
                if n == groups + 5:
                    spread_low(0)

            def add_input(pair, tile, buf):
                dve.wait_ge(group_done, (tile + 1) * groups)
                dve.wait_ge(a_loaded[buf], loads(pair, buf))
                dve.wait_ge(x1_turned_done, tile)
                v.scalar_tensor_tensor(out=x1[:, :], in0=y_acc[buf][:, :], scalar=1.0 / WSCALE, in1=x_in[:, buf, :],
                                       op0=ALU.mult, op1=ALU.add).then_inc(x1_done, 1)

            count = [0]

            def chain(instruction):
                count[0] += 1
                instruction.then_inc(step, 1)
                dve.wait_ge(step, count[0])

            wide3 = lambda t, k: t.rearrange("p (h o) -> p h o", o=1).broadcast_to([P, S, k])
            dt, ar, wr, wi, th, g_re, g_im, n_re, n_im, ct_re, ct_im, tmp, inv, fx, fy = (par[:, k, :] for k in range(15))
            ai, cr, ci = s4[:, 2, :], s4[:, 3, :], s4[:, 4, :]
            dve.wait_ge(params_in, 32)
            next_low()
            next_low()
            dve.wait_ge(rates_done, 1)
            chain(v.tensor_scalar(ar, ar, -1.0, None, ALU.mult))
            chain(v.tensor_tensor(wr, ar, dt, ALU.mult))
            chain(v.tensor_tensor(wi, ai, dt, ALU.mult))
            steps_of = {k: const[:, _cols[k]].rearrange("p (o k) -> p o k", o=1).broadcast_to([P, S, n])
                        for k, n in (("a_step", KA), ("b_step", KB))}
            chain(v.tensor_tensor(grid(growth, 0, KA), wide3(wr, KA), steps_of["a_step"], ALU.mult))
            v.tensor_tensor(grid(growth, S * KA, KB), wide3(wr, KB), steps_of["b_step"], ALU.mult).then_inc(angles_ready, 1)
            next_low()
            chain(v.tensor_copy(ang3[:, 0:S], wi))
            chain(v.tensor_copy(ang3[:, n_cos:n_cos + S], wi))
            chain(v.tensor_scalar(ang3[:, n_cos + S:n_cos + 2 * S], wi, 0.5, None, ALU.mult))
            chain(v.tensor_tensor(grid(ang3, S, KA), wide3(wi, KA), steps_of["a_step"], ALU.mult))
            chain(v.tensor_copy(ang3[:, n_cos + 2 * S:n_cos + n_sin], ang3[:, S:n_cos]))
            chain(v.tensor_tensor(grid(ang3, n_cos + n_sin, KB), wide3(wi, KB), steps_of["b_step"], ALU.mult))
            next_low()
            regions = ((cos_part, 0.25, 0.25 * TWO_PI), (sin_part, 0.0, 0.0),
                       (b_part, const[:, _cols["v_turn"]], const[:, _cols["v_angle"]]))
            for cols, quarter, _ in regions:
                chain(v.tensor_scalar(turns3[:, cols], ang3[:, cols], 1.0 / TWO_PI, quarter, ALU.mult, ALU.add))
            next_low()
            chain(v.tensor_scalar(turns3[:, :], turns3[:, :], MAGIC, MAGIC, ALU.add, ALU.subtract))
            for part in (PI2_HI, PI2_MID, PI2_LO):
                chain(v.scalar_tensor_tensor(out=ang3[:, :], in0=turns3[:, :], scalar=-part, in1=ang3[:, :],
                                             op0=ALU.mult, op1=ALU.add))
                next_low()
            for cols, _, angle in regions:
                chain(v.tensor_scalar(ang3[:, cols], ang3[:, cols], angle, PI_SAFE, ALU.add, ALU.min))
                v.tensor_scalar(ang3[:, cols], ang3[:, cols], -PI_SAFE, None, ALU.max).then_inc(angles_ready, 1)
            next_low()
            dve.wait_ge(growth_done, 1)
            chain(v.tensor_scalar(tmp, th, -1.0, 1.0, ALU.mult, ALU.add))
            chain(v.reciprocal(inv, tmp))
            chain(v.scalar_tensor_tensor(out=th, in0=th, scalar=2.0, in1=inv, op0=ALU.mult, op1=ALU.mult))
            dve.wait_ge(trig_done, 1)
            cos_w, sin_w, sin_h = turns3[:, 0:S], turns3[:, n_cos:n_cos + S], turns3[:, n_cos + S:n_cos + 2 * S]
            chain(v.tensor_tensor(tmp, sin_h, sin_h, ALU.mult))
            chain(v.tensor_tensor(g_re, th, cos_w, ALU.mult))
            chain(v.scalar_tensor_tensor(out=g_re, in0=tmp, scalar=-2.0, in1=g_re, op0=ALU.mult, op1=ALU.add))
            chain(v.scalar_tensor_tensor(out=g_im, in0=th, scalar=1.0, in1=sin_w, op0=ALU.add, op1=ALU.mult))
            chain(v.tensor_tensor(n_re, cr, g_re, ALU.mult))
            chain(v.tensor_tensor(tmp, ci, g_im, ALU.mult))
            chain(v.tensor_tensor(n_re, n_re, tmp, ALU.subtract))
            chain(v.tensor_tensor(n_im, cr, g_im, ALU.mult))
            chain(v.tensor_tensor(tmp, ci, g_re, ALU.mult))
            chain(v.tensor_tensor(n_im, n_im, tmp, ALU.add))
            next_low()
            chain(v.tensor_tensor(tmp, ar, ar, ALU.mult))
            chain(v.tensor_tensor(inv, ai, ai, ALU.mult))
            chain(v.tensor_tensor(tmp, tmp, inv, ALU.add))
            chain(v.reciprocal(inv, tmp))
            chain(v.tensor_tensor(ct_re, n_re, ar, ALU.mult))
            chain(v.tensor_tensor(tmp, n_im, ai, ALU.mult))
            chain(v.tensor_tensor(ct_re, ct_re, tmp, ALU.add))
            chain(v.tensor_tensor(ct_re, ct_re, inv, ALU.mult))
            chain(v.tensor_tensor(ct_im, n_im, ar, ALU.mult))
            chain(v.tensor_tensor(tmp, n_re, ai, ALU.mult))
            chain(v.tensor_tensor(ct_im, ct_im, tmp, ALU.subtract))
            chain(v.tensor_tensor(ct_im, ct_im, inv, ALU.mult))
            next_low()
            mix = _cols["mix"].start
            for out, one, two, m in ((fx, ct_re, ct_im, 0), (fy, ct_im, ct_re, 2)):
                chain(v.tensor_scalar(tmp, one, const[:, mix + m:mix + m + 1], None, ALU.mult))
                chain(v.scalar_tensor_tensor(out=out, in0=two, scalar=const[:, mix + m + 1:mix + m + 2], in1=tmp,
                                             op0=ALU.mult, op1=ALU.add))
            cos_a, sin_a = grid(turns3, S, KA), grid(turns3, n_cos + 2 * S, KA)
            chain(v.tensor_tensor(cos_a, cos_a, wide3(fx, KA), ALU.mult))
            chain(v.tensor_tensor(sin_a, sin_a, wide3(fy, KA), ALU.mult))
            next_low()
            chain(v.tensor_tensor(cos_a, cos_a, sin_a, ALU.add))
            next_low()
            dve.wait_ge(growth_done, 2)
            chain(v.tensor_tensor(grid(ang3, 0, KA), cos_a, grid(growth, 0, KA), ALU.mult))
            v.tensor_tensor(grid(ang3, S * KA, KB), grid(turns3, n_cos + n_sin, KB), grid(growth, S * KA, KB),
                            ALU.mult).then_inc(factors_done, 1)
            next_low()
            dve.wait_ge(k_done, 1)
            v.tensor_copy(conv_k.rearrange("p h b -> p (h b)"),
                          k_acc[0:KA, :, :].rearrange("p a n -> p (a n)")).then_inc(k_ready, 1)
            dve.wait_ge(k_ready, 1)
            v.tensor_tensor(conv_k[0:1, :, 0], conv_k[0:1, :, 0], d_row, ALU.add).then_inc(k_ready, 1)

            next_low()
            next_low()
            dve.wait_ge(k_hi_done, 1)
            v.scalar_tensor_tensor(out=kernel_parts[:, 1, :, :], in0=conv_k, scalar=WSCALE, in1=kernel_parts[:, 0, :, :],
                                   op0=ALU.mult, op1=ALU.subtract).then_inc(k_lo_done, 1)
            while done[0] < 2 * groups:
                next_low()
            with dve.Fori(1, TILES // 2) as i:
                iteration(i)
            add_input(TILES // 2 - 1, TILES - 1, 1)
            spread_low(TILES - 1)
            dve.wait_ge(mask_steps, 3)
            with dve.Fori(0, S // 8) as i:
                for par_z in range(2):
                    q = i * 2 + par_z
                    dve.wait_ge(conv_done, q + 1)
                    dve.wait_ge(z_stored[par_z], i * 16)
                    zq = z[:, par_z, :, :, :].rearrange("p i s b -> p s i b")
                    v.tensor_tensor(zq, k_acc[:, par_z, :].rearrange("p (s i b) -> p s i b", s=4, i=KT),
                                    keep_mask[:, :, :].rearrange("p (o i) b -> p o i b", o=1).broadcast_to([P, 4, KT, B]),
                                    ALU.mult).then_inc(z_part, 1)
                    dve.wait_ge(z_part, q + 1)
                    v.tensor_tensor(z[:, par_z, :, :, :], z[:, par_z, :, :, :], x1_t[:, :, bass.ds(q * 4, 4), :],
                                    ALU.add).then_inc(z_done, 1)

        @block.tensor
        def _(pe):
            def turn(i, n, tt, hg):
                if hg == 0 and not (isinstance(n, int) and n == 0):
                    pe.wait_ge(a_loaded[tt], loads(i, tt))
                if not (isinstance(n, int) and n == 0):
                    pe.wait_ge(at_lo_done, n - 1)
                for h in range(REP):
                    rows = first_a if isinstance(n, int) and n < groups else a_in[:, tt]
                    last = nc.tensor.transpose(turned[hg % 2][:, h, :], rows[:, h, hg * D:(hg + 1) * D], ident)
                last.then_inc(turned_done, 1)

            def project(n, tt, hg):
                pe.wait_ge(at_lo_done, n + 1)
                for h in range(REP):
                    head = hg * REP + h
                    for k, (a, w) in enumerate(((0, 0), (0, 1), (1, 0))):
                        last = nc.tensor.matmul(y_acc[tt][:, :], at[:, hg % 2, a, h, :], wo_head(head, w),
                                                start=(head == 0 and k == 0), stop=(head == HQ - 1 and k == 2))
                last.then_inc(group_done, 1)

            def make_kernels():
                pe.wait_ge(factors_done, 1)
                for h in range(S):
                    last = nc.tensor.matmul(k_acc[0:KA, h // 16, h % 16 * KB:(h % 16 + 1) * KB],
                                            ang3[:, h * KA:(h + 1) * KA], ang3[:, S * KA + h * KB:S * KA + (h + 1) * KB],
                                            start=True, stop=True)
                last.then_inc(k_done, 1)

            def turn_x1(tile):
                pe.wait_ge(x1_done, tile + 1)
                pe.wait_ge(x1_t_done, tile * 2)
                pe.wait_ge(back_lo_done, tile)
                for k in range(KT):
                    nc.tensor.transpose(x1_turned[0][:, k, :], x1[:, k * P:(k + 1) * P], ident)
                pe.wait_ge(x1_back_done, tile + 1)
                for k in range(KT):
                    last = nc.tensor.transpose(x1_turned[1][:, k, :], x1_back[:, k, :], ident)
                last.then_inc(x1_turned_done, 1)

            def iteration(i, first=False, final=False):
                for tt in range(2):
                    for hg in range(groups):
                        n = (i * 2 + tt) * groups + hg
                        if hg + 1 < groups:
                            turn(i, n + 1, tt, hg + 1)
                        elif not (final and tt == 1):
                            turn(i + tt, n + 1, 1 - tt, 0)
                        if hg == 2 and not (first and tt == 0):
                            turn_x1(i * 2 + tt - 1)
                        if first and tt == 0 and hg >= 2 and hg % 2 == 0:
                            pe.wait_ge(wo_loaded[hg // 2 - 1], 16)
                        if hg == 0 and not first:
                            pe.wait_ge(x1_done, i * 2 + tt - 1)
                        project(n, tt, hg)
                        if first and n == 13:
                            make_kernels()

            turn(0, 0, 0, 0)
            iteration(0, first=True)
            with pe.Fori(1, TILES // 2 - 1) as i:
                iteration(i)
            iteration(TILES // 2 - 1, final=True)
            turn_x1(TILES - 1)
            pe.wait_ge(back_lo_done, TILES)
            pe.wait_ge(toep_loaded, S * 16)

            def convolve(i, first=False):
                for j in range(8):
                    if j % 4 == 0 and not first:
                        pe.wait_ge(z_part, i * 2 - 1 + j // 4)
                    base = j % 4 * KT * B
                    for d in range(KT):
                        for k, x in ((0, 0), (0, 1), (1, 0)):
                            last = nc.tensor.matmul(
                                k_acc[:, j // 4, base + d * B:base + KT * B],
                                toep[:, bass.ds(i * 8 + j, 1), k, d * P:(d + 1) * P].rearrange("p o n -> p (o n)"),
                                x1_t_back[:, x, 0:KT - d, bass.ds(i * 8 + j, 1), :].rearrange("p i o b -> p i (o b)"),
                                start=(d == 0 and k == 0 and x == 0), stop=(d == KT - 1 and k == 1))
                    if j % 4 == 3:
                        last.then_inc(conv_done, 1)

            convolve(0, first=True)
            with pe.Fori(1, S // 8) as i:
                convolve(i)




def build_program(nc, dram):
    keep = {}
    with ExitStack() as outer:
        def sb(stack, name, shape, dt):
            keep[name] = stack.enter_context(nc.sbuf_tensor(name, shape, dt))

        sb(outer, "const", [P, NCONST], F32)
        sb(outer, "lens", [P, B], F32)
        sb(outer, "packed", [1, B * NPP // 4], I32)
        with ExitStack() as keys:
            sb(keys, "kt_all", [P, PAGES, HK, 2, PSIZE], F16)
            with ExitStack() as weights:
                sb(weights, "w_hi", [P, KT, E_ALL], F16)
                sb(weights, "w_lo", [P, KT, E_ALL], F16)
                sb(weights, "cos_t", [P, TILES, D // 2], F32)
                sb(weights, "sin_t", [P, TILES, D // 2], F32)
                sb(weights, "w_tab", [P, 4, D], F32)
                phase0(nc, dram, keep)
                phase1(nc, dram, keep)
            sb(keys, "wo_first", [P, HQ // 4, 2, HID], F16)
            phase2(nc, dram, keep)
            phase3(nc, dram, keep)


def constants():
    c = np.zeros((P, NCONST), np.float32)
    p = np.arange(P)
    c[:, _cols["ident"]] = np.eye(P)
    c[:, _cols["token_in_batch"]] = (p % S)[:, None]
    c[:, _cols["inv_freq"]] = np.float32(1.0) / np.float32(10000.0) ** (np.arange(0, D, 2, dtype=np.float32) / np.float32(D))
    c[:, _cols["hid_index"]] = p[:, None] + P * np.arange(KT)
    c[:, _cols["a_step"]] = KB * np.arange(KA)
    c[:, _cols["b_step"]] = np.arange(KB)
    c[:, _cols["v_turn"]] = np.where(p < NSTATE, 0.25, 0.0)[:, None]
    c[:, _cols["v_angle"]] = c[:, _cols["v_turn"]] * np.float32(TWO_PI)
    top, low = (p < NSTATE)[:, None], (p >= NSTATE)[:, None]
    c[:, _cols["mix"]] = np.concatenate([2.0 * top, -2.0 * low, -2.0 * top, -2.0 * low], 1)
    return c


SCRATCH = {
    "q_t": ([B, P, HK, 2 * REP * S], F16),
    "k_new": ([B, P, HK * D // 512, 2 * REP * S], F16),
    "v_new": ([TOK, 2, HK * D], F16),
    "v_split": ([PAGES * PSIZE, 2, HK * D], F16),
    "wo_split": ([P, HQ, 2, HID], F16),
    "attn": ([B * REP * S, HK * D], F32),
    "conv_k": ([S, 2, 2 * LCONV], F16),
}


def layout(x, itok_Bx16_0_63, itok_B_207_1644, itok_B_78_3631, L0_cond_Wq, L0_cond_Wk, L0_cond_Wv, L0_cond_Wo,
           L0_cond_q_norm_w, L0_cond_k_norm_w, L0_cond_k_cache, L0_cond_v_cache, L1_cond_log_dt, L1_cond_C,
           L1_cond_log_A_real, L1_cond_A_imag, L1_cond_D):
    a = np.asarray
    h = D // 2
    rows = a(x).reshape(TOK, HID)
    qw, kw = a(L0_cond_q_norm_w), a(L0_cond_k_norm_w)
    tab = np.stack([qw, np.concatenate([qw[h:], qw[:h]]), kw, np.concatenate([kw[h:], kw[:h]])])
    twice = lambda m: np.concatenate([a(m).T, a(m).T])
    wide = lambda v: np.broadcast_to(a(v), (P,) + a(v).shape)
    c = a(L1_cond_C)

    def padded(m, n, axis):
        return np.pad(m, [(0, n if k == axis else 0) for k in range(2)])

    arrays = {
        "x": rows,
        "xt": padded(rows.T, P, 1),
        "w_all": np.concatenate([a(L0_cond_Wq), a(L0_cond_Wk), a(L0_cond_Wv)]).T,
        "wo_t": padded(a(L0_cond_Wo).T, P, 0),
        "kt": padded(a(L0_cond_k_cache).transpose(3, 0, 2, 1).reshape(D, PAGES * HK * PSIZE), 512, 1),
        "v_cache": padded(a(L0_cond_v_cache).reshape(PAGES * PSIZE, HK * D), P, 0),
        "norm_w": wide(tab),
        "pages": a(itok_Bx16_0_63).reshape(1, B * NPP),
        "seqlens_by_token": np.repeat(a(itok_B_207_1644), S).reshape(TILES, P).T,
        "seqlens_wide": wide(itok_B_207_1644),
        "lengths_wide": wide(itok_B_78_3631),
        "s4d": np.stack([wide(L1_cond_log_dt), twice(L1_cond_log_A_real), twice(L1_cond_A_imag),
                         twice(c[:, :, 0]), twice(c[:, :, 1])], 1),
        "s4d_d": a(L1_cond_D).reshape(1, S),
        "consts": constants(),
        "key_index": wide(np.concatenate([np.arange(L), np.full(S, -1)]).astype(np.float32)),
    }
    return {k: np.ascontiguousarray(v) for k, v in arrays.items()}


def kernel(**inputs):
    from concourse import bacc
    from concourse.bass_utils import run_bass_kernel_spmd

    nc = bacc.Bacc("TRN2", target_bir_lowering=False, num_devices=1)
    arrays = layout(**inputs)
    dram = {n: nc.dram_tensor(n, list(v.shape), mybir.dt.from_np(v.dtype), kind="ExternalInput").ap()
            for n, v in arrays.items()}
    for n, (shape, dt) in SCRATCH.items():
        dram[n] = nc.dram_tensor(n, shape, dt, kind="Internal").ap()
    dram["out"] = nc.dram_tensor("out", [KT, P, S, B], F32, kind="ExternalOutput").ap()
    build_program(nc, dram)
    r = run_bass_kernel_spmd(nc, [arrays], core_ids=[0])
    out = r.results[0]["out"]
    return np.ascontiguousarray(out.transpose(3, 2, 0, 1).reshape(B, S, HID))
```
